# Optimizing a Trainium2 kernel written in Bass

```python
import numpy as np
import jax
import jax.numpy as jnp

def _softmax(x, axis=-1):
    return jax.nn.softmax(x, axis=axis)

def _gelu(x):
    return jax.nn.gelu(x, approximate=True)

def _silu(x):
    return jax.nn.silu(x)

def _sigmoid(x):
    return jax.nn.sigmoid(x)

def _layernorm(x, axis=-1, eps=1e-05):
    m = jnp.mean(x, axis=axis, keepdims=True)
    v = jnp.var(x, axis=axis, keepdims=True)
    return (x - m) / jnp.sqrt(v + eps)

def _scatter_add(tgt, idx, src, axis=0):
    return tgt.at[idx].add(src)

def _segment_sum(src, seg, n):
    return jax.ops.segment_sum(src, seg, n)
kernel_name = 'mk_decoder_postln_d2_seqx_r4_03a850'

def setup_inputs(seed: int=0):
    np.random.seed(seed)
    _w = jnp.asarray

    def _rec_inputs():
        import jax
        import jax.numpy as jnp
        _rk = jax.random.key(seed)
        x = -0.0002928 + 1 * jax.random.normal(jax.random.fold_in(_rk, 1), (4, 512, 256), jnp.float32)
        _lenS = 512 - jax.random.randint(jax.random.fold_in(_rk, 7), (4,), 0, max(1, 512 // 4) + 1, jnp.int32)
        _lenS2 = 512 - jax.random.randint(jax.random.fold_in(_rk, 8), (4,), 0, max(1, 512 // 4) + 1, jnp.int32)
        _ctx_1024P = jax.random.normal(jax.random.fold_in(_rk, 11), (4, 16, 256), jnp.float32)
        _ctx_1024c = jax.random.dirichlet(jax.random.fold_in(_rk, 511), 0.3 * jnp.ones((16,), jnp.float32), (4, 512))
        _ctx_1024t = jnp.einsum('bsk,bkd->bsd', _ctx_1024c, _ctx_1024P)
        _ctx_1024t = _ctx_1024t * jax.lax.rsqrt(jnp.mean(jnp.square(_ctx_1024t)) + 1e-12) * 0.953939
        ctx_1024 = -1.39393e-06 + 0.999914 * (_ctx_1024t + 0.3 * jax.random.normal(jax.random.fold_in(_rk, 611), (4, 512, 256), jnp.float32))
        _validS = jnp.arange(512)[None, :] < _lenS[:, None]
        _validS2 = jnp.arange(512)[None, :] < _lenS2[:, None]
        _causal = jnp.tril(jnp.ones((512, 512), dtype=bool))
        mask_SxS2_ik0 = jnp.where(jnp.broadcast_to(_validS2[0:1, :], (512, 512)), 0, 1).astype(jnp.int32)
        return (x, ctx_1024, mask_SxS2_ik0)
    x, ctx_1024, mask_SxS2_ik0 = _rec_inputs()

    def _L0_attn_setup():
        import jax, jax.numpy as jnp
        import numpy as np
        D_MODEL, N_QUERY, N_HEAD = (256, 2, 8)
        D_HEAD = D_MODEL // (N_QUERY * N_HEAD)
        KV = D_HEAD * N_HEAD

        def _reference_tuple_inner(x, Wq, Wk, Wv, memory, memory_norm, memory_weight):
            B, S, _ = x.shape
            QH = N_QUERY * N_HEAD
            scale = 1.0 / jnp.sqrt(jnp.float32(D_HEAD))
            q = x @ Wq
            k = x @ Wk
            v = x @ Wv
            q4 = q.reshape(B, S, QH, D_HEAD)
            k4 = jnp.repeat(k.reshape(B, S, N_HEAD, D_HEAD), N_QUERY, axis=2)
            v4 = jnp.repeat(v.reshape(B, S, N_HEAD, D_HEAD), N_QUERY, axis=2)
            scores = jnp.einsum('bsnd,btnd->bnst', q4, k4) * scale
            probs = jax.nn.softmax(scores, axis=-1)
            a_dot = jnp.einsum('bnst,btnd->bsnd', probs, v4)
            sigma_q = jax.nn.elu(q.reshape(B, S, N_QUERY, KV))
            num = sigma_q @ memory
            den = (sigma_q @ memory_norm)[..., None]
            a_mem = (num / den).reshape(B, S, QH, D_HEAD)
            sigma_k = jax.nn.elu(k)
            retrieved = sigma_k @ memory / (sigma_k @ memory_norm)[..., None]
            new_memory = memory + jnp.einsum('bsk,bsv->kv', sigma_k, v - retrieved)
            new_memory_norm = memory_norm + jnp.sum(sigma_k, axis=(0, 1))
            w = jax.nn.sigmoid(memory_weight)
            out = (a_dot * (1.0 - w) + a_mem * w).reshape(B, S, D_MODEL)
            return (out, new_memory, new_memory_norm)
        key = jax.random.key(seed)
        ks = jax.random.split(key, 6)
        B, S = (2, 512)
        x = jax.random.normal(ks[0], (B, S, D_MODEL), jnp.float32)
        Wq = jax.random.normal(ks[1], (D_MODEL, D_MODEL), jnp.float32) / np.sqrt(D_MODEL)
        Wk = jax.random.normal(ks[2], (D_MODEL, KV), jnp.float32) / np.sqrt(D_MODEL)
        Wv = jax.random.normal(ks[3], (D_MODEL, KV), jnp.float32) / np.sqrt(D_MODEL)
        memory = jax.random.normal(ks[4], (KV, KV), jnp.float32)
        memory_norm = jnp.ones((KV,), jnp.float32)
        memory_weight = jnp.ones((1,), jnp.float32)
        return {'x': x, 'Wq': Wq, 'Wk': Wk, 'Wv': Wv, 'memory': memory, 'memory_norm': memory_norm, 'memory_weight': memory_weight}
    _L0_attn_all = _L0_attn_setup()
    _L0_attn_in = {k: v for k, v in _L0_attn_all.items() if k in ('Wq', 'Wk', 'Wv', 'memory', 'memory_norm', 'memory_weight')}
    del _L0_attn_all

    def _L0_xattn_setup():
        import jax, jax.numpy as jnp
        import numpy as np
        B, S, D, H = (2, 512, 256, 16)
        HD = D // H

        def rotate_half(x):
            x1, x2 = (x[..., :HD // 2], x[..., HD // 2:])
            return jnp.concatenate((-x2, x1), axis=-1)

        def rope_cache(seq_len, dtype):
            inv_freq = 1.0 / 10000.0 ** (jnp.arange(0, HD, 2, dtype=jnp.float32) / HD)
            t = jnp.arange(seq_len, dtype=jnp.float32)
            freqs = t[:, None] * inv_freq[None, :]
            emb = jnp.concatenate((freqs, freqs), axis=-1)
            return (jnp.cos(emb).astype(dtype), jnp.sin(emb).astype(dtype))
        key = jax.random.key(seed)
        ks = jax.random.split(key, 8)
        xav = (6.0 / (D + D)) ** 0.5
        return {'query': jax.random.normal(ks[0], (B, S, D), jnp.float32), 'key': jax.random.normal(ks[1], (B, S, D), jnp.float32), 'value': jax.random.normal(ks[2], (B, S, D), jnp.float32), 'Wq': jax.random.uniform(ks[3], (D, D), jnp.float32, -xav, xav), 'bq': jnp.zeros((D,), jnp.float32), 'Wk': jax.random.uniform(ks[4], (D, D), jnp.float32, -xav, xav), 'bk': jnp.zeros((D,), jnp.float32), 'Wv': jax.random.uniform(ks[5], (D, D), jnp.float32, -xav, xav), 'bv': jnp.zeros((D,), jnp.float32), 'Wo': jax.random.uniform(ks[6], (D, D), jnp.float32, -xav, xav), 'bo': jnp.zeros((D,), jnp.float32)}
    _L0_xattn_all = _L0_xattn_setup()
    _L0_xattn_in = {k: v for k, v in _L0_xattn_all.items() if k in ('Wq', 'bq', 'Wk', 'bk', 'Wv', 'bv', 'Wo', 'bo')}
    del _L0_xattn_all

    def _L0_ffn_setup():
        import jax, jax.numpy as jnp
        import numpy as np
        import math
        B, S, D = (4, 512, 256)
        E, DFF = (16, 512)
        CAP_FACTOR = 2.0
        ROUTER_HIDDEN = 128
        CAPACITY = int(math.ceil(S * CAP_FACTOR / E))
        key = jax.random.key(seed)
        ks = jax.random.split(key, 6)

        def uinit(k, shape, fan_in):
            bound = math.sqrt(3.0) * math.sqrt(1.0 / 3.0) / math.sqrt(fan_in)
            return jax.random.uniform(k, shape, jnp.float32, -bound, bound)
        return {'hidden_states': jax.random.normal(ks[0], (B, S, D), jnp.float32), 'router_w1': jax.random.normal(ks[1], (D, ROUTER_HIDDEN), jnp.float32) / math.sqrt(D), 'router_w2': jax.random.normal(ks[2], (ROUTER_HIDDEN, E), jnp.float32) / math.sqrt(ROUTER_HIDDEN), 'w1': uinit(ks[3], (E, D, DFF), D), 'w2': uinit(ks[4], (E, D, DFF), D), 'w3': uinit(ks[5], (E, DFF, D), DFF)}
    _L0_ffn_all = _L0_ffn_setup()
    _L0_ffn_in = {k: v for k, v in _L0_ffn_all.items() if k in ('router_w1', 'router_w2', 'w1', 'w2', 'w3')}
    del _L0_ffn_all

    def _L1_attn_setup():
        import jax, jax.numpy as jnp
        import numpy as np
        import math
        CTX_LEN = 192
        N_EMBD = 256

        def _depthwise_causal_conv(z, w, T, C):
            return jax.lax.conv_general_dilated(z, w, window_strides=(1,), padding=[(T - 1, 0)], feature_group_count=C, dimension_numbers=('NCH', 'OIH', 'NCH'))
        key = jax.random.key(seed)
        ks = jax.random.split(key, 8)
        B, T, C = (8, CTX_LEN, N_EMBD)
        x = jax.random.normal(ks[0], (B, T, C), dtype=jnp.float32)
        time_decay = jax.random.normal(ks[1], (C, 1), dtype=jnp.float32) * 0.1
        time_first = jnp.full((C, 1), math.log(0.3), dtype=jnp.float32)
        time_mix = jax.random.uniform(ks[2], (1, 1, C), dtype=jnp.float32)
        s = 0.02
        Wk = jax.random.normal(ks[3], (C, C), dtype=jnp.float32) * s
        Wv = jax.random.normal(ks[4], (C, C), dtype=jnp.float32) * s
        Wr = jax.random.normal(ks[5], (C, C), dtype=jnp.float32) * s
        Wo = jax.random.normal(ks[6], (C, C), dtype=jnp.float32) * s
        return {'x': x, 'time_decay': time_decay, 'time_first': time_first, 'time_mix': time_mix, 'Wk': Wk, 'Wv': Wv, 'Wr': Wr, 'Wo': Wo}
    _L1_attn_all = _L1_attn_setup()
    _L1_attn_in = {k: v for k, v in _L1_attn_all.items() if k in ('time_decay', 'time_first', 'time_mix', 'Wk', 'Wv', 'Wr', 'Wo')}
    del _L1_attn_all

    def _L1_xattn_setup():
        import jax, jax.numpy as jnp
        import numpy as np
        D_MODEL = 256
        NUM_HEADS = 16
        D_K = D_MODEL // NUM_HEADS
        BATCH = 4
        SEQ = 512

        def _split_heads(x):
            b, s, _ = x.shape
            return x.reshape(b, s, NUM_HEADS, D_K).transpose(0, 2, 1, 3)
        key = jax.random.key(seed)
        ks = jax.random.split(key, 12)
        s = 0.02
        inp = {'Q': jax.random.normal(ks[0], (BATCH, SEQ, D_MODEL), jnp.float32), 'K': jax.random.normal(ks[1], (BATCH, SEQ, D_MODEL), jnp.float32), 'V': jax.random.normal(ks[2], (BATCH, SEQ, D_MODEL), jnp.float32), 'mask': jnp.tril(jnp.ones((SEQ, SEQ), jnp.int32)), 'Wq': jax.random.normal(ks[3], (D_MODEL, D_MODEL), jnp.float32) * s, 'bq': jax.random.normal(ks[4], (D_MODEL,), jnp.float32) * s, 'Wk': jax.random.normal(ks[5], (D_MODEL, D_MODEL), jnp.float32) * s, 'bk': jax.random.normal(ks[6], (D_MODEL,), jnp.float32) * s, 'Wv': jax.random.normal(ks[7], (D_MODEL, D_MODEL), jnp.float32) * s, 'bv': jax.random.normal(ks[8], (D_MODEL,), jnp.float32) * s, 'Wo': jax.random.normal(ks[9], (D_MODEL, D_MODEL), jnp.float32) * s, 'bo': jax.random.normal(ks[10], (D_MODEL,), jnp.float32) * s}
        return inp
    _L1_xattn_all = _L1_xattn_setup()
    _L1_xattn_in = {k: v for k, v in _L1_xattn_all.items() if k in ('Wq', 'bq', 'Wk', 'bk', 'Wv', 'bv', 'Wo', 'bo')}
    del _L1_xattn_all

    def _L1_ffn_setup():
        import jax, jax.numpy as jnp
        import numpy as np
        H = 256
        F = 1024
        E = 8
        TOP_K = 2
        B, S = (1, 512)
        key = jax.random.key(seed)
        k0, k1, k2, k3 = jax.random.split(key, 4)
        hidden_states = jax.random.normal(k0, (B, S, H), dtype=jnp.float32)
        gate_w = jax.random.normal(k1, (E, H), dtype=jnp.float32) * 0.02
        gate_up_w = jax.random.normal(k2, (E, 2 * F, H), dtype=jnp.float32) * 0.02
        down_w = jax.random.normal(k3, (E, H, F), dtype=jnp.float32) * 0.02
        return {'hidden_states': hidden_states, 'gate_w': gate_w, 'gate_up_w': gate_up_w, 'down_w': down_w}
    _L1_ffn_all = _L1_ffn_setup()
    _L1_ffn_in = {k: v for k, v in _L1_ffn_all.items() if k in ('gate_w', 'gate_up_w', 'down_w')}
    del _L1_ffn_all
    return {'x': x, 'ctx_1024': ctx_1024, 'mask_SxS2_ik0': mask_SxS2_ik0, 'L0_attn_Wq': _L0_attn_in['Wq'], 'L0_attn_Wk': _L0_attn_in['Wk'], 'L0_attn_Wv': _L0_attn_in['Wv'], 'L0_attn_memory': _L0_attn_in['memory'], 'L0_attn_memory_norm': _L0_attn_in['memory_norm'], 'L0_attn_memory_weight': _L0_attn_in['memory_weight'], 'L0_xattn_Wq': _L0_xattn_in['Wq'], 'L0_xattn_bq': _L0_xattn_in['bq'], 'L0_xattn_Wk': _L0_xattn_in['Wk'], 'L0_xattn_bk': _L0_xattn_in['bk'], 'L0_xattn_Wv': _L0_xattn_in['Wv'], 'L0_xattn_bv': _L0_xattn_in['bv'], 'L0_xattn_Wo': _L0_xattn_in['Wo'], 'L0_xattn_bo': _L0_xattn_in['bo'], 'L0_ffn_router_w1': _L0_ffn_in['router_w1'], 'L0_ffn_router_w2': _L0_ffn_in['router_w2'], 'L0_ffn_w1': _L0_ffn_in['w1'], 'L0_ffn_w2': _L0_ffn_in['w2'], 'L0_ffn_w3': _L0_ffn_in['w3'], 'L1_attn_time_decay': _L1_attn_in['time_decay'], 'L1_attn_time_first': _L1_attn_in['time_first'], 'L1_attn_time_mix': _L1_attn_in['time_mix'], 'L1_attn_Wk': _L1_attn_in['Wk'], 'L1_attn_Wv': _L1_attn_in['Wv'], 'L1_attn_Wr': _L1_attn_in['Wr'], 'L1_attn_Wo': _L1_attn_in['Wo'], 'L1_xattn_Wq': _L1_xattn_in['Wq'], 'L1_xattn_bq': _L1_xattn_in['bq'], 'L1_xattn_Wk': _L1_xattn_in['Wk'], 'L1_xattn_bk': _L1_xattn_in['bk'], 'L1_xattn_Wv': _L1_xattn_in['Wv'], 'L1_xattn_bv': _L1_xattn_in['bv'], 'L1_xattn_Wo': _L1_xattn_in['Wo'], 'L1_xattn_bo': _L1_xattn_in['bo'], 'L1_ffn_gate_w': _L1_ffn_in['gate_w'], 'L1_ffn_gate_up_w': _L1_ffn_in['gate_up_w'], 'L1_ffn_down_w': _L1_ffn_in['down_w']}

def reference(x, ctx_1024, mask_SxS2_ik0, L0_attn_Wq, L0_attn_Wk, L0_attn_Wv, L0_attn_memory, L0_attn_memory_norm, L0_attn_memory_weight, L0_xattn_Wq, L0_xattn_bq, L0_xattn_Wk, L0_xattn_bk, L0_xattn_Wv, L0_xattn_bv, L0_xattn_Wo, L0_xattn_bo, L0_ffn_router_w1, L0_ffn_router_w2, L0_ffn_w1, L0_ffn_w2, L0_ffn_w3, L1_attn_time_decay, L1_attn_time_first, L1_attn_time_mix, L1_attn_Wk, L1_attn_Wv, L1_attn_Wr, L1_attn_Wo, L1_xattn_Wq, L1_xattn_bq, L1_xattn_Wk, L1_xattn_bk, L1_xattn_Wv, L1_xattn_bv, L1_xattn_Wo, L1_xattn_bo, L1_ffn_gate_w, L1_ffn_gate_up_w, L1_ffn_down_w):
    import jax
    import jax.numpy as jnp

    def _L0_attn_ref(x, Wq, Wk, Wv, memory, memory_norm, memory_weight):
        import jax, jax.numpy as jnp
        import numpy as np
        D_MODEL, N_QUERY, N_HEAD = (256, 2, 8)
        D_HEAD = D_MODEL // (N_QUERY * N_HEAD)
        KV = D_HEAD * N_HEAD

        def _reference_tuple_inner(x, Wq, Wk, Wv, memory, memory_norm, memory_weight):
            B, S, _ = x.shape
            QH = N_QUERY * N_HEAD
            scale = 1.0 / jnp.sqrt(jnp.float32(D_HEAD))
            q = x @ Wq
            k = x @ Wk
            v = x @ Wv
            q4 = q.reshape(B, S, QH, D_HEAD)
            k4 = jnp.repeat(k.reshape(B, S, N_HEAD, D_HEAD), N_QUERY, axis=2)
            v4 = jnp.repeat(v.reshape(B, S, N_HEAD, D_HEAD), N_QUERY, axis=2)
            scores = jnp.einsum('bsnd,btnd->bnst', q4, k4) * scale
            probs = jax.nn.softmax(scores, axis=-1)
            a_dot = jnp.einsum('bnst,btnd->bsnd', probs, v4)
            sigma_q = jax.nn.elu(q.reshape(B, S, N_QUERY, KV))
            num = sigma_q @ memory
            den = (sigma_q @ memory_norm)[..., None]
            a_mem = (num / den).reshape(B, S, QH, D_HEAD)
            sigma_k = jax.nn.elu(k)
            retrieved = sigma_k @ memory / (sigma_k @ memory_norm)[..., None]
            new_memory = memory + jnp.einsum('bsk,bsv->kv', sigma_k, v - retrieved)
            new_memory_norm = memory_norm + jnp.sum(sigma_k, axis=(0, 1))
            w = jax.nn.sigmoid(memory_weight)
            out = (a_dot * (1.0 - w) + a_mem * w).reshape(B, S, D_MODEL)
            return (out, new_memory, new_memory_norm)
        return _reference_tuple_inner(x, Wq, Wk, Wv, memory, memory_norm, memory_weight)[0]

    def _L0_xattn_ref(query, key, value, Wq, bq, Wk, bk, Wv, bv, Wo, bo):
        import jax, jax.numpy as jnp
        import numpy as np
        B, S, D, H = (2, 512, 256, 16)
        HD = D // H

        def rotate_half(x):
            x1, x2 = (x[..., :HD // 2], x[..., HD // 2:])
            return jnp.concatenate((-x2, x1), axis=-1)

        def rope_cache(seq_len, dtype):
            inv_freq = 1.0 / 10000.0 ** (jnp.arange(0, HD, 2, dtype=jnp.float32) / HD)
            t = jnp.arange(seq_len, dtype=jnp.float32)
            freqs = t[:, None] * inv_freq[None, :]
            emb = jnp.concatenate((freqs, freqs), axis=-1)
            return (jnp.cos(emb).astype(dtype), jnp.sin(emb).astype(dtype))
        b, s, d = query.shape

        def split(x):
            return x.reshape(b, s, H, HD).transpose(0, 2, 1, 3)
        q = split(query @ Wq.T + bq)
        k = split(key @ Wk.T + bk)
        v = split(value @ Wv.T + bv)
        cos, sin = rope_cache(s, q.dtype)
        q = q * cos + rotate_half(q) * sin
        k = k * cos + rotate_half(k) * sin
        scores = jnp.einsum('bhqd,bhkd->bhqk', q, k) / HD ** 0.5
        attn = jax.nn.softmax(scores, axis=-1)
        ctx = jnp.einsum('bhqk,bhkd->bhqd', attn, v)
        ctx = ctx.transpose(0, 2, 1, 3).reshape(b, s, d)
        return ctx @ Wo.T + bo

    def _L0_ffn_ref(hidden_states, router_w1, router_w2, w1, w2, w3):
        import jax, jax.numpy as jnp
        import numpy as np
        import math
        B, S, D = (4, 512, 256)
        E, DFF = (16, 512)
        CAP_FACTOR = 2.0
        ROUTER_HIDDEN = 128
        CAPACITY = int(math.ceil(S * CAP_FACTOR / E))
        b, s, d = hidden_states.shape
        e = w1.shape[0]
        cap = CAPACITY
        router_logits = jax.nn.silu(hidden_states @ router_w1) @ router_w2
        expert_probs = jax.nn.softmax(router_logits.transpose(0, 2, 1), axis=-1)
        expert_weights, token_indices = jax.lax.top_k(expert_probs, cap)
        expert_weights = expert_weights / (expert_weights.sum(-1, keepdims=True) + 1e-09)
        expert_inputs = jax.vmap(lambda h, i: h[i])(hidden_states, token_indices)
        gate = jax.nn.silu(jnp.einsum('becd,edf->becf', expert_inputs, w1))
        value = jnp.einsum('becd,edf->becf', expert_inputs, w2)
        expert_out = jnp.einsum('becf,efd->becd', gate * value, w3)
        weighted = expert_out * expert_weights[..., None]

        def combine(idx, vals):
            return jnp.zeros((s, d), vals.dtype).at[idx.reshape(-1)].add(vals.reshape(-1, d))
        output = jax.vmap(combine)(token_indices, weighted)
        return output

    def _L1_attn_ref(x, time_decay, time_first, time_mix, Wk, Wv, Wr, Wo):
        import jax, jax.numpy as jnp
        import numpy as np
        import math
        CTX_LEN = 192
        N_EMBD = 256

        def _depthwise_causal_conv(z, w, T, C):
            return jax.lax.conv_general_dilated(z, w, window_strides=(1,), padding=[(T - 1, 0)], feature_group_count=C, dimension_numbers=('NCH', 'OIH', 'NCH'))
        B, T, C = x.shape
        xs = jnp.pad(x, ((0, 0), (1, 0), (0, 0)))[:, :-1]
        xm = x * time_mix + xs * (1.0 - time_mix)
        k = jnp.einsum('btc,dc->bdt', xm, Wk)
        v = jnp.einsum('btc,dc->bdt', xm, Wv)
        r = jnp.einsum('btc,dc->btd', xm, Wr)
        k = jnp.exp(jnp.minimum(k, 60.0))
        kv = k * v
        time_curve = (jnp.arange(T - 1, dtype=jnp.float32) - (T - 2))[None, :]
        time_w = jnp.concatenate([jnp.exp(time_decay) * time_curve, time_first], axis=-1)
        w = jnp.exp(time_w)[:, None, :]
        wkv = _depthwise_causal_conv(kv, w, T, C)
        wk = _depthwise_causal_conv(k, w, T, C) + 1e-09
        rwkv = jax.nn.sigmoid(r) * jnp.swapaxes(wkv / wk, 1, 2)
        return jnp.einsum('btc,dc->btd', rwkv, Wo)

    def _L1_xattn_ref(Q, K, V, mask, Wq, bq, Wk, bk, Wv, bv, Wo, bo):
        import jax, jax.numpy as jnp
        import numpy as np
        D_MODEL = 256
        NUM_HEADS = 16
        D_K = D_MODEL // NUM_HEADS
        BATCH = 4
        SEQ = 512

        def _split_heads(x):
            b, s, _ = x.shape
            return x.reshape(b, s, NUM_HEADS, D_K).transpose(0, 2, 1, 3)
        q = _split_heads(Q @ Wq.T + bq)
        k = _split_heads(K @ Wk.T + bk)
        v = _split_heads(V @ Wv.T + bv)
        scale = 1.0 / jnp.sqrt(jnp.asarray(D_K, q.dtype))
        scores = jnp.einsum('bhqd,bhkd->bhqk', q, k) * scale
        scores = jnp.where(mask == 0, jnp.asarray(-jnp.inf, scores.dtype), scores)
        attn = jax.nn.softmax(scores, axis=-1)
        out = jnp.einsum('bhqk,bhkd->bhqd', attn, v)
        b, h, s, dk = out.shape
        out = out.transpose(0, 2, 1, 3).reshape(b, s, h * dk)
        return out @ Wo.T + bo

    def _L1_ffn_ref(hidden_states, gate_w, gate_up_w, down_w):
        import jax, jax.numpy as jnp
        import numpy as np
        H = 256
        F = 1024
        E = 8
        TOP_K = 2
        B, S = (1, 512)
        b, s, h = hidden_states.shape
        x = hidden_states.reshape(-1, h)
        router_logits = x @ gate_w.T
        probs = jax.nn.softmax(router_logits.astype(jnp.float32), axis=-1)
        topw, sel = jax.lax.top_k(probs, TOP_K)
        topw = topw / jnp.sum(topw, axis=-1, keepdims=True)
        topw = topw.astype(x.dtype)
        combine = jnp.sum(jax.nn.one_hot(sel, E, dtype=x.dtype) * topw[..., None], axis=1)
        gu = jnp.einsum('th,efh->etf', x, gate_up_w)
        gate, up = (gu[..., :F], gu[..., F:])
        hact = up * jax.nn.gelu(gate, approximate=False)
        expert_out = jnp.einsum('etf,ehf->eth', hact, down_w)
        out = jnp.einsum('eth,te->th', expert_out, combine)
        return out.reshape(b, s, h)
    x = _layernorm(x + _L0_attn_ref(x, L0_attn_Wq, L0_attn_Wk, L0_attn_Wv, L0_attn_memory, L0_attn_memory_norm, L0_attn_memory_weight), axis=-1)
    x = _layernorm(x + _L0_xattn_ref(x, ctx_1024, ctx_1024, L0_xattn_Wq, L0_xattn_bq, L0_xattn_Wk, L0_xattn_bk, L0_xattn_Wv, L0_xattn_bv, L0_xattn_Wo, L0_xattn_bo), axis=-1)
    x = _layernorm(x + _L0_ffn_ref(x, L0_ffn_router_w1, L0_ffn_router_w2, L0_ffn_w1, L0_ffn_w2, L0_ffn_w3), axis=-1)
    x = _layernorm(x + _L1_attn_ref(x, L1_attn_time_decay, L1_attn_time_first, L1_attn_time_mix, L1_attn_Wk, L1_attn_Wv, L1_attn_Wr, L1_attn_Wo), axis=-1)
    x = _layernorm(x + _L1_xattn_ref(x, ctx_1024, ctx_1024, mask_SxS2_ik0, L1_xattn_Wq, L1_xattn_bq, L1_xattn_Wk, L1_xattn_bk, L1_xattn_Wv, L1_xattn_bv, L1_xattn_Wo, L1_xattn_bo), axis=-1)
    x = _layernorm(x + _L1_ffn_ref(x, L1_ffn_gate_w, L1_ffn_gate_up_w, L1_ffn_down_w), axis=-1)
    return x

_drawn_inputs = setup_inputs


def setup_inputs(seed=0):
    import zlib

    import numpy as np

    out = dict(_drawn_inputs(seed))
    spreads = {'L0_attn_memory_norm': (1.0, 0.2),
     'L0_xattn_bq': (0.0, 0.556),
     'L0_xattn_bk': (0.0, 0.8),
     'L0_xattn_bv': (0.0, 0.1),
     'L0_xattn_bo': (0.0, 0.1),
     'L1_attn_time_first': (-1.2039728164672852, 0.6)}
    factors = {'L0_attn_Wk': 3.033,
     'L0_attn_Wv': 2.681,
     'L0_ffn_router_w1': 8.0,
     'L0_ffn_router_w2': 8.0,
     'L0_ffn_w1': 8.0,
     'L0_ffn_w2': 8.0,
     'L0_ffn_w3': 8.0,
     'L1_attn_time_decay': 8.0,
     'L1_attn_time_mix': 7.012,
     'L1_attn_Wk': 8.0,
     'L1_attn_Wr': 8.0,
     'L1_xattn_Wq': 8.0,
     'L1_xattn_bq': 43.522,
     'L1_xattn_Wk': 8.0,
     'L1_xattn_bk': 64.0,
     'L1_xattn_bv': 8.0,
     'L1_xattn_bo': 2.729}
    for name, (base, spread) in spreads.items():
        noise = np.random.default_rng([zlib.crc32(name.encode()), seed]).standard_normal(out[name].shape)
        drawn = base * np.exp(spread * noise) if base else spread * noise
        out[name] = jnp.asarray(drawn.astype(out[name].dtype))
    for name, factor in factors.items():
        out[name] = (out[name] * factor).astype(out[name].dtype)
    return out
```

```python
import math
from contextlib import ExitStack

import numpy as np
import concourse.bass as bass
from concourse import mybir
from concourse.alu_op_type import AluOpType as ALU

FP32 = mybir.dt.float32
F32R = mybir.dt.float32r
BF16 = mybir.dt.bfloat16
I32 = mybir.dt.int32
U32 = mybir.dt.uint32
ACT = mybir.ActivationFunctionType
AX = mybir.AxisListType

P = 128
B, S, D = 4, 512, 256
T = B * S
TT = T // P
SC = S // P
KC = D // P
NH, HD = 16, 16
GH = 4
NG = NH // GH
UNITS = NG * SC
AUG = 96
LN_EPS = 1e-5
MASKED = -1e38


def r32(ap):
    return ap.bitcast(F32R)


def heads_stage(nc, name, src_t, dst, w, features, bias=None, rope=None, v=None):
    mcs = features // P
    with ExitStack() as ctx:
        sb = lambda n, shape, dt=FP32: ctx.enter_context(nc.sbuf_tensor(f"{name}_{n}", shape, dt))
        sem = lambda n: ctx.enter_context(nc.semaphore(f"{name}_{n}"))
        x_sb = sb("x", [P, 2, KC, S])
        w_sb = sb("w", [P, KC, features])
        hi = sb("hi", [P, 2, mcs, S], F32R)
        lo = sb("lo", [P, 2, mcs, S], F32R)
        full = sb("full", [P, mcs, S])
        bias_sb = sb("bias", [P, mcs]) if bias is not None else None
        if rope:
            w_swapped, bias_swapped, cos, sin = rope
            wsw_sb, bsw_sb = sb("wsw", [P, KC, features]), sb("bsw", [P, mcs])
            cos_sb, sin_sb = sb("cos", [P, S]), sb("sin", [P, S])
            rot_a, rot_b = sb("rot_a", [P, mcs, S]), sb("rot_b", [P, mcs, S])
        if v:
            wv, v_bias, v_sb = v
            vf = v_sb.shape[2]
            wv_sb, vb_sb = sb("wv", [P, KC, vf]), sb("vb", [P, vf])
        ps = ctx.enter_context(nc.psum_tensor(f"{name}_ps", [P, 8, 512], FP32))
        V_BANK = 4
        weights_loaded, x_loaded = sem("weights_loaded"), [sem("x_loaded0"), sem("x_loaded1")]
        projected = sem("projected")
        rotated, hi_done, lo_done = sem("rotated"), sem("hi_done"), sem("lo_done")
        stored = [sem("stored0"), sem("stored1")]
        v_projected, v_done, halves = sem("v_projected"), sem("v_done"), sem("halves")
        n_weights = 1 + (bias is not None) + 4 * bool(rope) + (1 + (v is not None and v[1] is not None)) * bool(v)
        block = ctx.enter_context(nc.Block())

        @block.sync
        def _(sp):
            def load_x(b):
                if b >= 2:
                    sp.wait_ge(projected, mcs * (b - 1))
                    if v:
                        sp.wait_ge(v_projected, SC * (b - 1))
                sp.dma_start(x_sb[:, b % 2], src_t[:, b * S:(b + 1) * S].rearrange("(k p) t -> p k t", p=P))\
                  .then_inc(x_loaded[b % 2], 16)

            load_x(0)
            sp.dma_start(w_sb[:], w.rearrange("(k p) f -> p k f", p=P)).then_inc(weights_loaded, 16)
            if bias is not None:
                sp.dma_start(bias_sb[:], bias).then_inc(weights_loaded, 16)
            if rope:
                sp.dma_start(wsw_sb[:], w_swapped.rearrange("(k p) f -> p k f", p=P)).then_inc(weights_loaded, 16)
                sp.dma_start(bsw_sb[:], bias_swapped).then_inc(weights_loaded, 16)
                sp.dma_start(cos_sb[:], cos).then_inc(weights_loaded, 16)
                sp.dma_start(sin_sb[:], sin).then_inc(weights_loaded, 16)
            if v:
                sp.dma_start(wv_sb[:], wv.rearrange("(k p) f -> p k f", p=P)).then_inc(weights_loaded, 16)
                if v_bias is not None:
                    sp.dma_start(vb_sb[:], v_bias.partition_broadcast(P)).then_inc(weights_loaded, 16)
            load_x(1)
            for b in range(B):
                for m in range(mcs):
                    sp.wait_ge(lo_done, b * mcs + m + 1)
                    for part, tile in enumerate((hi, lo)):
                        sp.dma_start(dst[part, m * P:(m + 1) * P, b * S:(b + 1) * S],
                                     tile[:, b % 2, m].bitcast(FP32)).then_inc(stored[b % 2], 16)
                if b + 2 < B:
                    load_x(b + 2)
            for slot in range(2):
                sp.wait_ge(stored[slot], 32 * mcs * (B // 2))

        @block.tensor
        def _(pe):
            pe.wait_ge(weights_loaded, 16 * n_weights)
            with pe.Fori(0, B // 2) as pairs:
                pair = pairs * 2
                for par in range(2):
                    b = pair + par
                    pe.wait_ge(x_loaded[par], pair * 8 + 16)
                    pe.wait_ge(lo_done, b * mcs)
                    for m in range(mcs):
                        for k in range(KC):
                            last = nc.tensor.matmul(ps[:, m], w_sb[:, k, m * P:(m + 1) * P], x_sb[:, par, k],
                                                    start=(k == 0), stop=(k == KC - 1))
                        if rope:
                            for k in range(KC):
                                last = nc.tensor.matmul(ps[:, mcs + m], wsw_sb[:, k, m * P:(m + 1) * P],
                                                        x_sb[:, par, k], start=(k == 0), stop=(k == KC - 1))
                        last.then_inc(projected, 1)
                    if v:
                        pe.wait_ge(v_done, b * SC)
                        for sc in range(SC):
                            for k in range(KC):
                                last = nc.tensor.matmul(ps[:, V_BANK + sc, 0:vf], x_sb[:, par, k, sc * P:(sc + 1) * P],
                                                        wv_sb[:, k], start=(k == 0), stop=(k == KC - 1))
                            last.then_inc(v_projected, 1)

        @block.scalar
        def _(act):
            act.wait_ge(weights_loaded, 16 * n_weights)
            with act.Fori(0, B // 2) as pairs:
                pair = pairs * 2
                for par in range(2):
                    b = pair + par
                    act.wait_ge(stored[par], pair * (16 * mcs))
                    for m in range(mcs):
                        if rope:
                            act.wait_ge(rotated, b * mcs + m + 1)
                            nc.scalar.activation(hi[:, par, m], full[:, m], ACT.Copy).then_inc(hi_done, 1)
                        else:
                            act.wait_ge(projected, b * mcs + m + 1)
                            nc.scalar.activation(hi[:, par, m], ps[:, m], ACT.Identity,
                                                 bias=bias_sb[:, m:m + 1] if bias is not None else 0.0).then_inc(hi_done, 1)

        @block.vector
        def _(dve):
            dve.wait_ge(weights_loaded, 16 * n_weights)
            with dve.Fori(0, B // 2) as pairs:
                pair = pairs * 2
                for par in range(2):
                    b = pair + par
                    dve.wait_ge(stored[par], pair * (16 * mcs))
                    for m in range(mcs):
                        i = b * mcs + m
                        dve.wait_ge(projected, i + 1)
                        if rope:
                            nc.vector.scalar_tensor_tensor(rot_a[:, m], ps[:, m], bias_sb[:, m:m + 1], cos_sb[:],
                                                           op0=ALU.add, op1=ALU.mult).then_inc(halves, 1)
                            nc.vector.scalar_tensor_tensor(rot_b[:, m], ps[:, mcs + m], bsw_sb[:, m:m + 1], sin_sb[:],
                                                           op0=ALU.add, op1=ALU.mult).then_inc(halves, 1)
                            dve.wait_ge(halves, i * 2 + 2)
                            dve.wait_ge(hi_done, b * mcs)
                            nc.vector.tensor_tensor(full[:, m], rot_a[:, m], rot_b[:, m], op=ALU.add).then_inc(rotated, 1)
                    for m in range(mcs):
                        i = b * mcs + m
                        dve.wait_ge(hi_done, i + 1)
                        if rope:
                            dve.wait_ge(rotated, i + 1)
                            nc.vector.tensor_tensor(lo[:, par, m], full[:, m], hi[:, par, m].bitcast(FP32),
                                                    op=ALU.subtract).then_inc(lo_done, 1)
                        elif bias is not None:
                            nc.vector.scalar_tensor_tensor(lo[:, par, m], ps[:, m], bias_sb[:, m:m + 1],
                                                           hi[:, par, m].bitcast(FP32),
                                                           op0=ALU.add, op1=ALU.subtract).then_inc(lo_done, 1)
                        else:
                            nc.vector.tensor_tensor(lo[:, par, m], ps[:, m], hi[:, par, m].bitcast(FP32),
                                                    op=ALU.subtract).then_inc(lo_done, 1)
                    if v:
                        for sc in range(SC):
                            dve.wait_ge(v_projected, b * SC + sc + 1)
                            tile = v_sb[:, bass.ds(b * SC + sc, 1), :].rearrange("p a f -> p (a f)")
                            if v_bias is not None:
                                nc.vector.tensor_tensor(tile, ps[:, V_BANK + sc, 0:vf], vb_sb[:], op=ALU.add).then_inc(v_done, 1)
                            else:
                                nc.vector.tensor_copy(tile, ps[:, V_BANK + sc, 0:vf]).then_inc(v_done, 1)


def attention_stage(nc, name, q_parts, k_parts, v_sb, attended, rep, ident, masks=None):
    KG = GH // rep
    G = B * NG
    with ExitStack() as ctx:
        sb = lambda n, shape, dt=FP32: ctx.enter_context(nc.sbuf_tensor(f"{name}_{n}", shape, dt))
        sem = lambda n: ctx.enter_context(nc.semaphore(f"{name}_{n}"))
        q4 = sb("q4", [P, NH, S], F32R)
        k4 = sb("k4", [P, NH // rep, S], F32R)
        probs = sb("probs", [P, SC, GH, S])
        values = sb("values", [P, SC, NH, 32])
        out_t = sb("out_t", [P, NG, S])
        shift = sb("shift", [P, 2, GH * SC])
        aug = sb("aug", [GH * SC, 2, 2, P], F32R)
        sums = sb("sums", [P, SC, NH])
        ps = ctx.enter_context(nc.psum_tensor(f"{name}_ps", [P, 8, 512], FP32))
        MAX_BANK, OUT_BANK, TURN_BANK = 4, 6, 7
        heads_loaded = [sem(f"heads_loaded{g}") for g in range(NG)]
        slots_ready, aug_loaded = sem("slots_ready"), sem("aug_loaded")
        scores_ready, exp_done = sem("scores_ready"), sem("exp_done")
        max_scores_ready, max_done = sem("max_scores_ready"), sem("max_done")
        shift_turned, aug_done, values_ready = sem("shift_turned"), sem("aug_done"), sem("values_ready")
        probs_used, out_copied, out_turned = sem("probs_used"), sem("out_copied"), sem("out_turned")
        sums_done, normed = sem("sums_done"), sem("normed")
        block = ctx.enter_context(nc.Block())
        BANK_CREDIT, PROBS_CREDIT = 2, SC

        @block.sync
        def _(sp):
            sp.wait_ge(slots_ready, 3)

            def load_heads(b, g):
                for r, part in enumerate((0, 1, 0)):
                    sp.dma_start(q4[r * HD:(r + 1) * HD, g * GH:(g + 1) * GH].bitcast(FP32),
                                 q_parts[part, g * GH * HD:(g + 1) * GH * HD, bass.ds(b * S, S)]
                                 .rearrange("(h d) t -> d h t", d=HD)).then_inc(heads_loaded[g], 16)
                for r, part in enumerate((0, 0, 1)):
                    sp.dma_start(k4[r * HD:(r + 1) * HD, g * KG:(g + 1) * KG].bitcast(FP32),
                                 k_parts[part, g * KG * HD:(g + 1) * KG * HD, bass.ds(b * S, S)]
                                 .rearrange("(h d) t -> d h t", d=HD)).then_inc(heads_loaded[g], 16)

            def load_aug(index, slot, par):
                sp.wait_ge(aug_done, 2 * index + 2)
                for part in range(2):
                    sp.dma_start(q4[AUG + part:AUG + part + 1, slot * GH:(slot + 1) * GH].bitcast(FP32),
                                 aug[:, par, part].bitcast(FP32)).then_inc(aug_loaded, 16)

            for g in range(NG):
                load_heads(0, g)
            load_aug(0, 0, 0)
            with sp.Fori(0, B - 1) as b:
                for g in range(NG):
                    load_aug(b * NG + g + 1, (g + 1) % NG, (g + 1) % 2)
                    sp.wait_ge(scores_ready, b * (2 * UNITS) + 2 * SC * (g + 1))
                    load_heads(b + 1, g)
            for g in range(NG - 1):
                load_aug((B - 1) * NG + g + 1, g + 1, (g + 1) % 2)

        @block.gpsimd
        def _(pool):
            nc.gpsimd.memset(values[:], 0.0).then_inc(slots_ready, 1)
            pool.wait_ge(slots_ready, 3)
            nc.gpsimd.memset(values[:, :, :, HD:HD + 1], 1.0).then_inc(slots_ready, 1)
            pool.wait_ge(slots_ready, 5)

            def spread(b, g):
                for r in range(rep):
                    last = nc.gpsimd.tensor_copy(
                        values[:, :, g * GH + r:(g + 1) * GH:rep, 0:HD],
                        v_sb[:, bass.ds(b * SC, SC), g * KG * HD:(g + 1) * KG * HD]
                        .rearrange("p c (h d) -> p c h d", d=HD))
                last.then_inc(values_ready, 1)

            for g in range(NG):
                spread(0, g)
            with pool.Fori(1, B) as b:
                for g in range(NG):
                    pool.wait_ge(probs_used, (b - 1) * UNITS + (PROBS_CREDIT + SC * (g + 1)))
                    spread(b, g)

        @block.tensor
        def _(pe):
            pe.sem_inc(probs_used, PROBS_CREDIT)
            pe.wait_ge(slots_ready, 5)

            def max_scores(b, index, slot, h):
                if h == 0:
                    pe.wait_ge(heads_loaded[slot], b * 96 + 96)
                for sc in range(SC):
                    m = h * SC + sc
                    pe.wait_ge(max_done, index * (GH * SC) + m + 1)
                    bank = MAX_BANK + sc % 2
                    last = nc.tensor.matmul(ps[:, bank], q4[0:AUG, slot * GH + h, sc * P:(sc + 1) * P],
                                            k4[0:AUG, (slot * GH + h) // rep], start=True, stop=masks is None)
                    if masks:
                        last = nc.tensor.matmul(ps[:, bank], masks[2][:], masks[0][:, sc], start=False, stop=True)
                    last.then_inc(max_scores_ready, 1)

            def turn_shift(index, par, b=0):
                pe.wait_ge(normed, b * SC)
                pe.wait_ge(max_done, index * (GH * SC) + (GH * SC + BANK_CREDIT))
                pe.wait_ge(aug_done, index * 2)
                nc.tensor.transpose(ps[0:GH * SC, TURN_BANK, 0:P], shift[:, par], ident[:]).then_inc(shift_turned, 1)

            def scores(b, g, tc, pair):
                n = b * UNITS + g * SC + tc
                if tc == 0 and pair == 0:
                    pe.wait_ge(aug_loaded, b * (32 * NG) + 32 * (g + 1))
                pe.wait_ge(exp_done, n * 2 + pair + 1)
                for j in range(2):
                    h = g * GH + 2 * pair + j
                    last = nc.tensor.matmul(ps[:, 2 * pair + j], k4[0:AUG + 2, h // rep, tc * P:(tc + 1) * P],
                                            q4[0:AUG + 2, h], start=True, stop=masks is None)
                    if masks:
                        last = nc.tensor.matmul(ps[:, 2 * pair + j], masks[2][:], masks[1][:, tc],
                                                start=False, stop=True)
                last.then_inc(scores_ready, 1)

            def weigh(b, g, tc):
                n = b * UNITS + g * SC + tc
                if tc == 0:
                    pe.wait_ge(values_ready, b * NG + g + 1)
                    pe.wait_ge(out_copied, b * NG + g)
                    if g == 0:
                        pe.wait_ge(normed, b * SC)
                pe.wait_ge(exp_done, n * 2 + 2 + BANK_CREDIT)
                for h in range(GH):
                    last = nc.tensor.matmul(ps[32 * h:32 * h + 32, OUT_BANK], values[:, tc, g * GH + h],
                                            probs[:, tc, h], start=(tc == 0), stop=(tc == SC - 1))
                last.then_inc(probs_used, 1)

            def turn_out(b, last):
                pe.wait_ge(out_copied, b * NG + NG)
                pe.wait_ge(aug_done, 2 * G if last else b * (2 * NG) + 2 * (NG + 1))
                for sc in range(SC):
                    pe.wait_ge(normed, b * SC + max(sc - 1, 0))
                    for g in range(NG):
                        last = nc.tensor.transpose(ps[:, TURN_BANK - sc % 2, g * P:(g + 1) * P],
                                                   out_t[:, g, sc * P:(sc + 1) * P], ident[:])
                    last.then_inc(out_turned, 1)

            def batch(b, last):
                for g in range(NG):
                    for tc in range(SC):
                        scores(b, g, tc, 0)
                        if tc == 0 and not (last and g == NG - 1):
                            turn_shift(b * NG + g + 1, (g + 1) % 2, b)
                        if not (last and g >= NG - 2):
                            max_scores(b + (g + 2) // NG, b * NG + g + 2, (g + 2) % NG, tc)
                        scores(b, g, tc, 1)
                        if g or tc:
                            weigh(b, (g * SC + tc - 1) // SC, (tc - 1) % SC)
                weigh(b, NG - 1, SC - 1)
                turn_out(b, last)

            for index in range(2):
                for h in range(GH):
                    max_scores(0, index, index, h)
                if index == 0:
                    turn_shift(0, 0)
            with pe.Fori(0, B - 1) as b:
                batch(b, False)
            batch(B - 1, True)

        def copy_out(act, b, g):
            act.wait_ge(probs_used, b * UNITS + (SC * (g + 1) + PROBS_CREDIT))
            act.wait_ge(out_turned, b * SC)
            nc.scalar.activation(out_t[:, g], ps[:, OUT_BANK], ACT.Copy).then_inc(out_copied, 1)

        @block.scalar
        def _(act):
            act.sem_inc(exp_done, BANK_CREDIT)
            with act.Fori(0, B) as b:
                for g in range(NG):
                    for tc in range(SC):
                        n = b * UNITS + g * SC + tc
                        act.wait_ge(probs_used, n + 1)
                        for pair in range(2):
                            act.wait_ge(scores_ready, n * 2 + pair + 1)
                            nc.scalar.activation(probs[:, tc, 2 * pair:2 * pair + 2], ps[:, 2 * pair:2 * pair + 2],
                                                 ACT.Exp, scale=HD ** -0.5).then_inc(exp_done, 1)
                        if tc == 0 and g > 0:
                            copy_out(act, b, g - 1)
                copy_out(act, b, NG - 1)

        @block.vector
        def _(dve):
            nc.vector.memset(q4[:].bitcast(FP32), 0.0).then_inc(slots_ready, 1)
            nc.vector.memset(k4[:].bitcast(FP32), 0.0).then_inc(slots_ready, 1)
            dve.wait_ge(slots_ready, 3)
            nc.vector.memset(k4[AUG:AUG + 2].bitcast(FP32), 1.0).then_inc(slots_ready, 1)
            dve.sem_inc(max_done, BANK_CREDIT)

            def maxima(index, par, h):
                for sc in range(SC):
                    m = h * SC + sc
                    dve.wait_ge(max_scores_ready, index * (GH * SC) + m + 1)
                    nc.vector.tensor_reduce(shift[:, par, m:m + 1], ps[:, MAX_BANK + sc % 2], axis=AX.X,
                                            op=ALU.max, negate=True).then_inc(max_done, 1)

            def split_shift(index, par):
                rows = ps[0:GH * SC, TURN_BANK, 0:P]
                dve.wait_ge(shift_turned, index + 1)
                nc.vector.tensor_copy(aug[:, par, 0], rows).then_inc(aug_done, 1)
                dve.wait_ge(aug_done, index * 2 + 1)
                nc.vector.tensor_tensor(aug[:, par, 1], rows, aug[:, par, 0].bitcast(FP32),
                                        op=ALU.subtract).then_inc(aug_done, 1)

            def normalise(b):
                for sc in range(SC):
                    turned = ps[:, TURN_BANK - sc % 2].rearrange("p (h c) -> p h c", c=32)
                    dve.wait_ge(out_turned, b * SC + sc + 1)
                    nc.vector.reciprocal(sums[:, sc], turned[:, :, HD]).then_inc(sums_done, 1)
                    dve.wait_ge(sums_done, b * SC + sc + 1)
                    nc.vector.tensor_tensor(
                        attended[:, bass.ds(b * SC + sc, 1), :].rearrange("p a (h d) -> p (a h) d", d=HD),
                        turned[:, :, 0:HD], sums[:, sc].unsqueeze(2).to_broadcast([P, NH, HD]),
                        op=ALU.mult).then_inc(normed, 1)

            def batch(b, last):
                for g in range(NG):
                    for tc in range(SC):
                        if not (last and g >= NG - 2):
                            maxima(b * NG + g + 2, g % 2, tc)
                        if tc == 0 and not (last and g == NG - 1):
                            split_shift(b * NG + g + 1, (g + 1) % 2)
                normalise(b)

            for index in range(2):
                for h in range(GH):
                    maxima(index, index, h)
                if index == 0:
                    split_shift(0, 0)
            with dve.Fori(0, B - 1) as b:
                batch(b, False)
            batch(B - 1, True)


def memory_stage(nc, name, q_parts, x, memory, memory_norm, mem_w):
    with ExitStack() as ctx:
        sb = lambda n, shape, dt=FP32: ctx.enter_context(nc.sbuf_tensor(f"{name}_{n}", shape, dt))
        sem = lambda n: ctx.enter_context(nc.semaphore(f"{name}_{n}"))
        q_sb = sb("q", [P, 2, 2, KC, S])
        mem_sb = sb("mem", [P, P + 1])
        q, low, positive, sigma = (sb(n, [P, KC, S]) for n in ("sum", "low", "positive", "sigma"))
        weight = sb("weight", [P, SC, KC])
        ps = ctx.enter_context(nc.psum_tensor(f"{name}_ps", [P, SC, 2, 256], FP32))
        loaded, mem_loaded = [sem("loaded0"), sem("loaded1")], sem("mem_loaded")
        q_done, low_done, exp_done, positive_done, sigma_done = (
            sem(n) for n in ("q_done", "low_done", "exp_done", "positive_done", "sigma_done"))
        retrieved, steps, added = sem("retrieved"), sem("steps"), sem("added")
        block = ctx.enter_context(nc.Block())

        @block.sync
        def _(sp):
            sp.dma_start(mem_sb[:, 0:P], memory).then_inc(mem_loaded, 16)
            sp.dma_start(mem_sb[:, P:P + 1], memory_norm.rearrange("(p a) -> p a", a=1)).then_inc(mem_loaded, 16)
            for b in range(B):
                if b >= 2:
                    sp.wait_ge(q_done, b - 1)
                for part in range(2):
                    sp.dma_start(q_sb[:, b % 2, part], q_parts[part, :, b * S:(b + 1) * S]
                                 .rearrange("(k p) t -> p k t", p=P)).then_inc(loaded[b % 2], 16)

        @block.gpsimd
        def _(pool):
            with pool.Fori(0, B // 2) as pairs:
                pair = pairs * 2
                for par in range(2):
                    pool.wait_ge(loaded[par], pair * 16 + 32)
                    pool.wait_ge(positive_done, pair + par)
                    pool.wait_ge(low_done, pair + par)
                    nc.gpsimd.tensor_tensor(q[:], q_sb[:, par, 0], q_sb[:, par, 1], op=ALU.add).then_inc(q_done, 1)

        @block.scalar
        def _(act):
            with act.Fori(0, B) as b:
                act.wait_ge(q_done, b + 1)
                act.wait_ge(sigma_done, b)
                nc.scalar.activation(positive[:], q[:], ACT.Relu).then_inc(positive_done, 1)
                act.wait_ge(low_done, b + 1)
                nc.scalar.activation(low[:], low[:], ACT.Exp).then_inc(exp_done, 1)

        @block.vector
        def _(dve):
            dve.wait_ge(q_done, 1)
            with dve.Fori(0, B) as b:
                dve.wait_ge(q_done, b + 1)
                nc.vector.tensor_scalar_min(low[:], q[:], 0.0).then_inc(low_done, 1)
                dve.wait_ge(exp_done, b + 1)
                dve.wait_ge(positive_done, b + 1)
                dve.wait_ge(retrieved, b * SC)
                nc.vector.scalar_tensor_tensor(sigma[:], low[:], -1.0, positive[:], op0=ALU.add, op1=ALU.add)\
                  .then_inc(sigma_done, 1)
                for sc in range(SC):
                    dve.wait_ge(retrieved, b * SC + sc + 1)
                    nc.vector.reciprocal(weight[:, sc], ps[:, sc, :, P]).then_inc(steps, 1)
                    dve.wait_ge(steps, b * (2 * SC) + 2 * sc + 1)
                    nc.vector.tensor_scalar_mul(weight[:, sc], weight[:, sc], mem_w[:, 0:1]).then_inc(steps, 1)
                    dve.wait_ge(steps, b * (2 * SC) + 2 * sc + 2)
                    tile = x[:, bass.ds(b * SC + sc, 1), :].rearrange("p a f -> p (a f)")
                    for j in range(2):
                        last = nc.vector.scalar_tensor_tensor(tile[:, j * P:(j + 1) * P], ps[:, sc, j, 0:P],
                                                              weight[:, sc, j:j + 1], tile[:, j * P:(j + 1) * P],
                                                              op0=ALU.mult, op1=ALU.add)
                    last.then_inc(added, 1)

        @block.tensor
        def _(pe):
            pe.wait_ge(mem_loaded, 32)
            with pe.Fori(0, B) as b:
                pe.wait_ge(sigma_done, b + 1)
                pe.wait_ge(added, b * SC)
                for sc in range(SC):
                    for j in range(2):
                        last = nc.tensor.matmul(ps[:, sc, j, 0:P + 1], sigma[:, j, sc * P:(sc + 1) * P], mem_sb[:],
                                                start=True, stop=True)
                    last.then_inc(retrieved, 1)


class Norm:

    def __init__(self, ctx, nc, name):
        sb = lambda n, shape: ctx.enter_context(nc.sbuf_tensor(f"{name}_{n}", shape, FP32))
        sem = lambda n: ctx.enter_context(nc.semaphore(f"{name}_{n}"))
        self.nc = nc
        self.y = sb("y", [P, SC, D])
        self.stats, self.moments = sb("stats", [P, SC, 6]), sb("moments", [P, SC, 2])
        self.rstd, self.eps = sb("rstd", [P, SC]), sb("eps", [P, 1])
        self.summed, self.stats_done, self.moments_done = sem("summed"), sem("stats_done"), sem("moments_done")
        self.eps_ready, self.root_done, self.rstd_done = sem("eps_ready"), sem("root_done"), sem("rstd_done")
        self.normed, self.stats_seen = sem("normed"), sem("stats_seen")

    def statistics(self, dve, b, sc):
        dve.wait_ge(self.summed, b * SC + sc + 1)
        self.nc.vector.bn_stats(self.stats[:, sc], self.y[:, sc]).then_inc(self.stats_done, 1)
        dve.wait_ge(self.stats_done, b * SC + sc + 1)
        dve.sem_inc(self.stats_seen, 1)
        self.nc.vector.bn_aggr(self.moments[:, sc], self.stats[:, sc]).then_inc(self.moments_done, 1)

    def root(self, act, b):
        act.wait_ge(self.eps_ready, 1)
        act.wait_ge(self.moments_done, b * SC + SC)
        act.wait_ge(self.normed, b * SC)
        self.nc.scalar.activation(self.rstd[:], self.moments[:, :, 1], ACT.Sqrt, bias=self.eps[:, 0:1])\
            .then_inc(self.root_done, 1)

    def invert(self, dve, b):
        dve.wait_ge(self.root_done, b + 1)
        self.nc.vector.reciprocal(self.rstd[:], self.rstd[:]).then_inc(self.rstd_done, 1)
        dve.wait_ge(self.rstd_done, b + 1)

    def apply(self, out, sc):
        self.nc.vector.tensor_scalar(out, self.y[:, sc], self.moments[:, sc, 0:1], self.rstd[:, sc:sc + 1],
                                     op0=ALU.subtract, op1=ALU.mult).then_inc(self.normed, 1)


def after_stage(nc, name, x, x_t, ident, attended=None, blend=None, wo=None, bo=None,
                block_t=None, out=None):
    turns = wo is not None and block_t is None
    with ExitStack() as ctx:
        sb = lambda n, shape, dt=FP32: ctx.enter_context(nc.sbuf_tensor(f"{name}_{n}", shape, dt))
        sem = lambda n: ctx.enter_context(nc.semaphore(f"{name}_{n}"))
        norm = Norm(ctx, nc, f"{name}_norm")
        fresh = sb("fresh", [P, 2, SC, D])
        turned = sb("turned", [P, 2, KC, S])
        ps = ctx.enter_context(nc.psum_tensor(f"{name}_ps", [P, 8, 512], FP32))
        TURN, ATT, PROJ = 0, 2, 4
        if wo is not None:
            wo_sb = sb("wo", [P, KC, D])
            att_t = sb("att_t", [P, 2, KC, S])
        if bo is not None:
            bo_sb = sb("bo", [P, D])
        if turns:
            att = sb("att", [P, 2, SC, D])
        weights_loaded, att_copied, att_turned, att_t_done, projected = (
            sem(n) for n in ("weights_loaded", "att_copied", "att_turned", "att_t_done", "projected"))
        biased, block_loaded = sem("biased"), [sem("block_loaded0"), sem("block_loaded1")]
        kept, x_turned, turned_done = (sem(n) for n in ("kept", "x_turned", "turned_done"))
        stored = [sem("stored0"), sem("stored1")]
        block = ctx.enter_context(nc.Block())

        @block.sync
        def _(sp):
            if wo is not None:
                sp.dma_start(wo_sb[:], wo.rearrange("(k p) f -> p k f", p=P)).then_inc(weights_loaded, 16)
                if bo is not None:
                    sp.dma_start(bo_sb[:], bo.partition_broadcast(P)).then_inc(weights_loaded, 16)

            def load_block(b):
                sp.dma_start(att_t[:, b % 2], block_t[:, b * S:(b + 1) * S].rearrange("(k p) t -> p k t", p=P))\
                  .then_inc(block_loaded[b % 2], 16)

            if block_t is not None:
                load_block(0)
                load_block(1)
            for b in range(B):
                if block_t is not None and b + 2 < B:
                    sp.wait_ge(projected, (b + 1) * SC)
                    load_block(b + 2)
                if out is None:
                    sp.wait_ge(turned_done, b + 1)
                    sp.dma_start(x_t[:, b * S:(b + 1) * S].rearrange("(k p) t -> p k t", p=P), turned[:, b % 2])\
                      .then_inc(stored[b % 2], 16)
                else:
                    sp.wait_ge(norm.normed, (b + 1) * SC)
                    sp.dma_start(out[b * S:(b + 1) * S].rearrange("(c p) d -> p c d", p=P), fresh[:, b % 2])\
                      .then_inc(stored[b % 2], 16)
            for slot in range(2):
                sp.wait_ge(stored[slot], 16 * (B // 2))

        @block.gpsimd
        def _(pool):
            nc.gpsimd.memset(norm.eps[:], LN_EPS).then_inc(norm.eps_ready, 1)
            if bo is not None:
                pool.wait_ge(weights_loaded, 32)
                for tt in range(TT):
                    nc.gpsimd.tensor_tensor(x[:, tt], x[:, tt], bo_sb[:], op=ALU.add).then_inc(biased, 1)
            if out is not None:
                return
            with pool.Fori(0, B // 2) as pairs:
                pair = pairs * 2
                for par in range(2):
                    b = pair + par
                    pool.wait_ge(norm.normed, b * SC + SC)
                    nc.gpsimd.tensor_copy(x[:, bass.ds(b * SC, SC)], fresh[:, par]).then_inc(kept, 1)

        @block.scalar
        def _(act):
            with act.Fori(0, B // 2) as pairs:
                pair = pairs * 2
                for par in range(2):
                    b = pair + par
                    if turns:
                        act.wait_ge(att_turned, b)
                        nc.scalar.activation(att[:, par], attended[:, bass.ds(b * SC, SC)], ACT.Copy)\
                          .then_inc(att_copied, 1)
                        act.wait_ge(att_turned, b + 1)
                        act.wait_ge(projected, b * SC)
                        nc.scalar.activation(att_t[:, par], ps[:, ATT:ATT + KC], ACT.Copy).then_inc(att_t_done, 1)
                    norm.root(act, b)
                    if out is None:
                        act.wait_ge(x_turned, b + 1)
                        act.wait_ge(stored[par], pair * 8)
                        nc.scalar.activation(turned[:, par], ps[:, TURN:TURN + KC], ACT.Copy).then_inc(turned_done, 1)

        @block.tensor
        def _(pe):
            if wo is not None:
                pe.wait_ge(weights_loaded, 16 + 16 * (bo is not None))
            with pe.Fori(0, B // 2) as pairs:
                pair = pairs * 2
                for par in range(2):
                    b = pair + par
                    if turns:
                        pe.wait_ge(att_copied, b + 1)
                        pe.wait_ge(att_t_done, b)
                        for sc in range(SC):
                            for k in range(KC):
                                last = nc.tensor.transpose(ps[:, ATT + k, sc * P:(sc + 1) * P],
                                                           att[:, par, sc, k * P:(k + 1) * P], ident[:])
                        last.then_inc(att_turned, 1)
                        pe.wait_ge(att_t_done, b + 1)
                    elif wo is not None:
                        pe.wait_ge(block_loaded[par], pair * 8 + 16)
                    if wo is not None:
                        pe.wait_ge(norm.summed, b * SC)
                        for sc in range(SC):
                            for k in range(KC):
                                last = nc.tensor.matmul(ps[:, PROJ + sc, 0:D], att_t[:, par, k, sc * P:(sc + 1) * P],
                                                        wo_sb[:, k], start=(k == 0), stop=(k == KC - 1))
                            last.then_inc(projected, 1)
                    if out is None:
                        pe.wait_ge(norm.normed, b * SC + SC)
                        pe.wait_ge(turned_done, b)
                        for sc in range(SC):
                            for k in range(KC):
                                last = nc.tensor.transpose(ps[:, TURN + k, sc * P:(sc + 1) * P],
                                                           fresh[:, par, sc, k * P:(k + 1) * P], ident[:])
                        last.then_inc(x_turned, 1)

        @block.vector
        def _(dve):
            if bo is not None:
                dve.wait_ge(biased, TT)
            with dve.Fori(0, B // 2) as pairs:
                pair = pairs * 2
                for par in range(2):
                    b = pair + par
                    dve.wait_ge(norm.normed, b * SC)
                    for sc in range(SC):
                        tile = x[:, bass.ds(b * SC + sc, 1)].rearrange("p a f -> p (a f)")
                        if wo is not None:
                            dve.wait_ge(projected, b * SC + sc + 1)
                            nc.vector.tensor_tensor(norm.y[:, sc], ps[:, PROJ + sc, 0:D], tile, op=ALU.add)\
                              .then_inc(norm.summed, 1)
                        else:
                            nc.vector.scalar_tensor_tensor(
                                norm.y[:, sc], attended[:, bass.ds(b * SC + sc, 1)].rearrange("p a f -> p (a f)"),
                                blend[:, 0:1], tile, op0=ALU.mult, op1=ALU.add).then_inc(norm.summed, 1)
                        norm.statistics(dve, b, sc)
                    norm.invert(dve, b)
                    if out is None:
                        dve.wait_ge(x_turned, b)
                        dve.wait_ge(kept, b)
                    else:
                        dve.wait_ge(stored[par], pair * 8)
                    for sc in range(SC):
                        norm.apply(fresh[:, par, sc], sc)


E0, FF0, CAP = 16, 512, 64
BE = B * E0
FC0 = FF0 // P


def router_stage(nc, name, x_t, w1, w2, logits):
    with ExitStack() as ctx:
        sb = lambda n, shape, dt=FP32: ctx.enter_context(nc.sbuf_tensor(f"{name}_{n}", shape, dt))
        sem = lambda n: ctx.enter_context(nc.semaphore(f"{name}_{n}"))
        x_sb, w1_sb, w2_sb = sb("x", [P, B, KC, S]), sb("w1", [P, KC, P]), sb("w2", [P, E0])
        hidden, rows = sb("hidden", [P, S]), sb("rows", [E0, B, S])
        ps = ctx.enter_context(nc.psum_tensor(f"{name}_ps", [P, 2, 512], FP32))
        weights_loaded, x_loaded = sem("weights_loaded"), [sem(f"x_loaded{b}") for b in range(B)]
        hidden_ready, hidden_done, logits_ready, logits_done, stored = (
            sem(n) for n in ("hidden_ready", "hidden_done", "logits_ready", "logits_done", "stored"))
        block = ctx.enter_context(nc.Block())

        @block.sync
        def _(sp):
            sp.dma_start(w1_sb[:], w1.rearrange("(k p) f -> p k f", p=P)).then_inc(weights_loaded, 16)
            sp.dma_start(w2_sb[:], w2).then_inc(weights_loaded, 16)
            for b in range(B):
                sp.dma_start(x_sb[:, b], x_t[:, b * S:(b + 1) * S].rearrange("(k p) t -> p k t", p=P))\
                  .then_inc(x_loaded[b], 16)
            sp.wait_ge(logits_done, B)
            sp.dma_start(logits.rearrange("(b e) t -> e b t", b=B), rows[:]).then_inc(stored, 16)
            sp.wait_ge(stored, 16)

        @block.tensor
        def _(pe):
            pe.wait_ge(weights_loaded, 32)
            for b in range(B):
                pe.wait_ge(x_loaded[b], 16)
                pe.wait_ge(hidden_done, b)
                for k in range(KC):
                    last = nc.tensor.matmul(ps[:, 0], w1_sb[:, k], x_sb[:, b, k], start=(k == 0), stop=(k == KC - 1))
                last.then_inc(hidden_ready, 1)
                pe.wait_ge(hidden_done, b + 1)
                pe.wait_ge(logits_done, b)
                nc.tensor.matmul(ps[0:E0, 1], w2_sb[:], hidden[:], start=True, stop=True).then_inc(logits_ready, 1)

        @block.scalar
        def _(act):
            for b in range(B):
                act.wait_ge(hidden_ready, b + 1)
                act.wait_ge(logits_ready, b)
                nc.scalar.activation(hidden[:], ps[:, 0], ACT.Silu).then_inc(hidden_done, 1)

        @block.vector
        def _(dve):
            for b in range(B):
                dve.wait_ge(logits_ready, b + 1)
                nc.vector.tensor_copy(rows[:, b], ps[0:E0, 1]).then_inc(logits_done, 1)


def choice_stage(nc, name, logits, slots, weights, ident):
    with ExitStack() as ctx:
        sb = lambda n, shape, dt=FP32: ctx.enter_context(nc.sbuf_tensor(f"{name}_{n}", shape, dt))
        sem = lambda n: ctx.enter_context(nc.semaphore(f"{name}_{n}"))
        row = lambda n: sb(n, [BE, S])
        rows, probs, left, chosen, counts, zeros, slot_rows, weight_rows = (
            row(n) for n in ("logits", "probs", "left", "chosen", "counts", "zeros", "slot_rows", "weight_rows"))
        shift, total, best, share = sb("shift", [BE, 1]), sb("total", [BE, 1]), sb("best", [BE, 8]), sb("share", [BE, 1])
        ps = ctx.enter_context(nc.psum_tensor(f"{name}_ps", [P, 2, SC, BE], FP32))
        loaded, shift_done, exp_done, step, ready, turned, done = (
            sem(n) for n in ("loaded", "shift_done", "exp_done", "step", "ready", "turned", "done"))
        block = ctx.enter_context(nc.Block())

        @block.sync
        def _(sp):
            sp.dma_start(rows[:], logits).then_inc(loaded, 16)

        @block.scalar
        def _(act):
            act.wait_ge(shift_done, 1)
            nc.scalar.activation(probs[:], rows[:], ACT.Exp, bias=shift[:, 0:1], accum_out=total[:, 0:1])\
              .then_inc(exp_done, 1)

        @block.vector
        def _(dve):
            steps = 0

            def then_wait(instruction):
                nonlocal steps
                steps += 1
                instruction.then_inc(step, 1)
                dve.wait_ge(step, steps)

            nc.vector.memset(zeros[:], 0.0)
            dve.wait_ge(loaded, 16)
            nc.vector.tensor_reduce(shift[:], rows[:], axis=AX.X, op=ALU.max, negate=True).then_inc(shift_done, 1)
            dve.wait_ge(exp_done, 1)
            then_wait(nc.vector.reciprocal(share[:], total[:]))
            then_wait(nc.vector.tensor_scalar_mul(probs[:], probs[:], share[:, 0:1]))
            then_wait(nc.vector.tensor_copy(left[:], probs[:]))
            for _ in range(CAP // 8):
                then_wait(nc.vector.max(best[:], left[:]))
                then_wait(nc.vector.match_replace(left[:], best[:], left[:], -1.0))
            then_wait(nc.vector.tensor_single_scalar(chosen[:], left[:], 0.0, op=ALU.is_lt))
            then_wait(nc.vector.scalar_tensor_tensor(weight_rows[:], left[:], 0.0, probs[:], op0=ALU.is_lt,
                                                     op1=ALU.mult, accum_out=total[:, 0:1]))
            then_wait(nc.vector.tensor_scalar_add(total[:], total[:], 1e-9))
            then_wait(nc.vector.reciprocal(share[:], total[:]))
            then_wait(nc.vector.tensor_scalar_mul(weight_rows[:], weight_rows[:], share[:, 0:1]))
            then_wait(nc.vector.tensor_tensor_scan(counts[:], chosen[:], zeros[:], 0.0, op0=ALU.add, op1=ALU.add))
            then_wait(nc.vector.tensor_tensor(counts[:], counts[:], chosen[:], op=ALU.mult))
            nc.vector.tensor_scalar_add(slot_rows[:], counts[:], -1.0).then_inc(ready, 1)
            dve.wait_ge(turned, 1)
            nc.vector.tensor_copy(slots[:], ps[:, 0]).then_inc(done, 1)
            nc.vector.tensor_copy(weights[:], ps[:, 1]).then_inc(done, 1)
            dve.wait_ge(done, 2)

        @block.tensor
        def _(pe):
            pe.wait_ge(ready, 1)
            for i, source in enumerate((slot_rows, weight_rows)):
                for sc in range(SC):
                    last = nc.tensor.transpose(ps[:, i, sc], source[:, sc * P:(sc + 1) * P], ident[0:BE, 0:BE])
            last.then_inc(turned, 1)


def gather_stage(nc, name, x, slots, numbers, chosen_t):
    with ExitStack() as ctx:
        sb = lambda n, shape, dt=FP32: ctx.enter_context(nc.sbuf_tensor(f"{name}_{n}", shape, dt))
        sem = lambda n: ctx.enter_context(nc.semaphore(f"{name}_{n}"))
        hi, lo = sb("hi", [P, 2, SC, D], F32R), sb("lo", [P, 2, SC, D], F32R)
        places = sb("places", [P, SC, E0, CAP], F32R)
        ps = ctx.enter_context(nc.psum_tensor(f"{name}_ps", [P, 2, KC, 2, 512], FP32))
        HE = E0 // 2
        hi_done, lo_done, places_done, gathered, kept = (
            sem(n) for n in ("hi_done", "lo_done", "places_done", "gathered", "kept"))
        block = ctx.enter_context(nc.Block())

        @block.scalar
        def _(act):
            with act.Fori(0, B // 2) as pairs:
                pair = pairs * 2
                for par in range(2):
                    b = pair + par
                    act.wait_ge(gathered, b)
                    nc.scalar.activation(hi[:, par], x[:, bass.ds(b * SC, SC)], ACT.Copy).then_inc(hi_done, 1)
                    act.wait_ge(gathered, b + 1)
                    for k in range(KC):
                        for half in range(2):
                            nc.scalar.activation(
                                chosen_t[:, k, half * HE:(half + 1) * HE, bass.ds(b * CAP, CAP)],
                                ps[:, par, k, half].rearrange("p (e c) -> p e c", c=CAP), ACT.Copy).then_inc(kept, 1)

        @block.vector
        def _(dve):
            with dve.Fori(0, B // 2) as pairs:
                pair = pairs * 2
                for par in range(2):
                    b = pair + par
                    dve.wait_ge(gathered, b)
                    for sc in range(SC):
                        nc.vector.tensor_tensor(
                            places[:, sc], numbers[:].unsqueeze(1).to_broadcast([P, E0, CAP]),
                            slots[:, sc, bass.ds(b * E0, E0)].unsqueeze(2).to_broadcast([P, E0, CAP]),
                            op=ALU.is_equal).then_inc(places_done, 1)
                    dve.wait_ge(hi_done, b + 1)
                    nc.vector.tensor_tensor(lo[:, par], x[:, bass.ds(b * SC, SC)], hi[:, par].bitcast(FP32),
                                            op=ALU.subtract).then_inc(lo_done, 1)

        @block.tensor
        def _(pe):
            with pe.Fori(0, B // 2) as pairs:
                pair = pairs * 2
                for par in range(2):
                    b = pair + par
                    pe.wait_ge(places_done, b * SC + SC)
                    pe.wait_ge(lo_done, b + 1)
                    pe.wait_ge(kept, b * (KC * 2))
                    for k in range(KC):
                        for half in range(2):
                            for sc in range(SC):
                                for part in (hi, lo):
                                    last = nc.tensor.matmul(
                                        ps[:, par, k, half], part[:, par, sc, k * P:(k + 1) * P],
                                        places[:, sc, half * HE:(half + 1) * HE],
                                        start=(sc == 0 and part is hi), stop=(sc == SC - 1 and part is lo))
                    last.then_inc(gathered, 1)


def expert_stage(nc, name, chosen_t, w1, w2, w3, made):
    N = B * CAP
    with ExitStack() as ctx:
        sb = lambda n, shape, dt=FP32: ctx.enter_context(nc.sbuf_tensor(f"{name}_{n}", shape, dt))
        sem = lambda n: ctx.enter_context(nc.semaphore(f"{name}_{n}"))
        w1_sb, w2_sb = sb("w1", [P, 2, KC, FF0]), sb("w2", [P, 2, KC, FF0])
        w3_sb = sb("w3", [P, 2, FC0, D])
        gate, act_t = sb("gate", [P, 2, 2, N]), sb("act_t", [P, 2, FC0, N])
        ps = ctx.enter_context(nc.psum_tensor(f"{name}_ps", [P, 8, 512], FP32))
        OUT = 4
        up_loaded, down_loaded = [sem("up_loaded0"), sem("up_loaded1")], [sem("down_loaded0"), sem("down_loaded1")]
        up_ready, gate_done, act_done, made_ready, kept = (
            sem(n) for n in ("up_ready", "gate_done", "act_done", "made_ready", "kept"))
        block = ctx.enter_context(nc.Block())

        @block.sync
        def _(sp):
            def load(e2, j):
                e = e2 * 2 + j
                row = lambda w: w[bass.ds(e, 1)].rearrange("a (k p) f -> p (a k) f", p=P)
                sp.dma_start(w1_sb[:, j], row(w1)).then_inc(up_loaded[j], 16)
                sp.dma_start(w2_sb[:, j], row(w2)).then_inc(up_loaded[j], 16)
                sp.dma_start(w3_sb[:, j], row(w3)).then_inc(down_loaded[j], 16)

            load(0, 0)
            load(0, 1)
            with sp.Fori(1, E0 // 2) as e2:
                for j in range(2):
                    sp.wait_ge(made_ready, e2)
                    load(e2, j)

        @block.tensor
        def _(pe):
            with pe.Fori(0, E0 // 2) as e2:
                for j in range(2):
                    pe.wait_ge(up_loaded[j], e2 * 32 + 32)
                    for f2 in range(FC0 // 2):
                        pe.wait_ge(act_done, e2 * 4 + (2 * j + f2 + 1))
                        for which, w in enumerate((w1_sb, w2_sb)):
                            for f in range(2):
                                for k in range(KC):
                                    fc = 2 * f2 + f
                                    last = nc.tensor.matmul(
                                        ps[:, 2 * f2 + which, f * N:(f + 1) * N], w[:, j, k, fc * P:(fc + 1) * P],
                                        chosen_t[:, k, bass.ds(e2 * 2 + j, 1)].rearrange("p a n -> p (a n)"),
                                        start=(k == 0), stop=(k == KC - 1))
                            last.then_inc(up_ready, 1)
                pe.wait_ge(act_done, e2 * 4 + 6)
                for j in range(2):
                    pe.wait_ge(down_loaded[j], e2 * 16 + 16)
                pe.wait_ge(kept, e2)
                for b in range(B):
                    for fc in range(FC0):
                        for j in range(2):
                            last = nc.tensor.matmul(ps[CAP * j:CAP * (j + 1), OUT + b, 0:D],
                                                    act_t[:, j, fc, b * CAP:(b + 1) * CAP], w3_sb[:, j, fc],
                                                    start=(fc == 0), stop=(fc == FC0 - 1))
                last.then_inc(made_ready, 1)

        @block.scalar
        def _(act):
            with act.Fori(0, E0 // 2) as e2:
                for u in range(4):
                    act.wait_ge(up_ready, e2 * 8 + (2 * u + 1))
                    act.wait_ge(act_done, e2 * 4 + (u + 1))
                    nc.scalar.activation(gate[:, u % 2], ps[:, 2 * (u % 2)].rearrange("p (f n) -> p f n", f=2),
                                         ACT.Silu).then_inc(gate_done, 1)
                act.wait_ge(made_ready, e2 + 1)
                nc.scalar.activation(made[:, bass.ds(e2, 1)].rearrange("p a b d -> p (a b) d"),
                                     ps[:, OUT:OUT + B, 0:D], ACT.Copy).then_inc(kept, 1)

        @block.vector
        def _(dve):
            dve.sem_inc(act_done, 2)
            with dve.Fori(0, E0 // 2) as e2:
                dve.wait_ge(made_ready, e2)
                for u in range(4):
                    dve.wait_ge(gate_done, e2 * 4 + (u + 1))
                    dve.wait_ge(up_ready, e2 * 8 + (2 * u + 2))
                    nc.vector.tensor_tensor(act_t[:, u // 2, 2 * (u % 2):2 * (u % 2) + 2],
                                            ps[:, 2 * (u % 2) + 1].rearrange("p (f n) -> p f n", f=2),
                                            gate[:, u % 2], op=ALU.mult).then_inc(act_done, 1)


def combine_stage(nc, name, x, x_t, ident, slots, weights, numbers, made):
    with ExitStack() as ctx:
        sb = lambda n, shape, dt=FP32: ctx.enter_context(nc.sbuf_tensor(f"{name}_{n}", shape, dt))
        sem = lambda n: ctx.enter_context(nc.semaphore(f"{name}_{n}"))
        norm = Norm(ctx, nc, f"{name}_norm")
        fresh, turned = sb("fresh", [P, SC, D]), sb("turned", [P, KC, S])
        places = sb("places", [P, 2, E0, CAP])
        places_t = sb("places_t", [P, 2, E0 // 2, P])
        ps = ctx.enter_context(nc.psum_tensor(f"{name}_ps", [P, 8, 512], FP32))
        TURN, PLACES, OUT = 0, 2, 6
        equal_done, weighted, places_turned, places_kept, summed_up = (
            sem(n) for n in ("equal_done", "weighted", "places_turned", "places_kept", "summed_up"))
        kept, x_turned, turned_done, stored = (sem(n) for n in ("kept", "x_turned", "turned_done", "stored"))
        block = ctx.enter_context(nc.Block())
        tile_of = lambda ap, i: ap[:, bass.ds(i, 1)].rearrange("p a f -> p (a f)")

        @block.sync
        def _(sp):
            for b in range(B):
                sp.wait_ge(turned_done, b + 1)
                sp.dma_start(x_t[:, b * S:(b + 1) * S].rearrange("(k p) t -> p k t", p=P), turned[:])\
                  .then_inc(stored, 16)
            sp.wait_ge(stored, 16 * B)

        @block.gpsimd
        def _(pool):
            nc.gpsimd.memset(norm.eps[:], LN_EPS).then_inc(norm.eps_ready, 1)
            with pool.Fori(0, B) as b:
                for sc in range(SC):
                    n = b * SC + sc
                    pool.wait_ge(equal_done, n + 1)
                    nc.gpsimd.tensor_tensor(places[:, sc % 2], places[:, sc % 2],
                                            weights[:, sc, bass.ds(b * E0, E0)].unsqueeze(2).to_broadcast([P, E0, CAP]),
                                            op=ALU.mult).then_inc(weighted, 1)
                pool.wait_ge(norm.normed, b * SC + SC)
                nc.gpsimd.tensor_copy(x[:, bass.ds(b * SC, SC)], fresh[:]).then_inc(kept, 1)

        @block.tensor
        def _(pe):
            with pe.Fori(0, B) as b:
                for sc in range(SC):
                    n = b * SC + sc
                    pe.wait_ge(weighted, n + 1)
                    pe.wait_ge(places_kept, n)
                    for e2 in range(E0 // 2):
                        last = nc.tensor.transpose(
                            ps[:, PLACES + 2 * (sc % 2) + e2 // 4, e2 % 4 * P:(e2 % 4 + 1) * P],
                            places[:, sc % 2, 2 * e2:2 * e2 + 2].rearrange("p e c -> p (e c)"), ident[:])
                    last.then_inc(places_turned, 1)
                    pe.wait_ge(places_kept, n + 1)
                    pe.wait_ge(norm.summed, n)
                    for e2 in range(E0 // 2):
                        last = nc.tensor.matmul(ps[:, OUT + sc % 2, 0:D], places_t[:, sc % 2, e2],
                                                made[:, e2, bass.ds(b, 1)].rearrange("p a d -> p (a d)"),
                                                start=(e2 == 0), stop=(e2 == E0 // 2 - 1))
                    last.then_inc(summed_up, 1)
                pe.wait_ge(norm.normed, b * SC + SC)
                pe.wait_ge(turned_done, b)
                for sc in range(SC):
                    for k in range(KC):
                        last = nc.tensor.transpose(ps[:, TURN + k, sc * P:(sc + 1) * P],
                                                   fresh[:, sc, k * P:(k + 1) * P], ident[:])
                last.then_inc(x_turned, 1)

        @block.scalar
        def _(act):
            with act.Fori(0, B) as b:
                for sc in range(SC):
                    n = b * SC + sc
                    act.wait_ge(places_turned, n + 1)
                    act.wait_ge(summed_up, n)
                    nc.scalar.activation(places_t[:, sc % 2].rearrange("p (a e) t -> p a (e t)", a=2),
                                         ps[:, PLACES + 2 * (sc % 2):PLACES + 2 * (sc % 2) + 2], ACT.Copy)\
                      .then_inc(places_kept, 1)
                norm.root(act, b)
                act.wait_ge(x_turned, b + 1)
                act.wait_ge(stored, b * 16)
                nc.scalar.activation(turned[:], ps[:, TURN:TURN + KC], ACT.Copy).then_inc(turned_done, 1)

        @block.vector
        def _(dve):
            def equal(n, b, sc):
                nc.vector.tensor_tensor(
                    places[:, sc % 2], numbers[:].unsqueeze(1).to_broadcast([P, E0, CAP]),
                    slots[:, sc, bass.ds(b * E0, E0)].unsqueeze(2).to_broadcast([P, E0, CAP]),
                    op=ALU.is_equal).then_inc(equal_done, 1)

            with dve.Fori(0, B) as b:
                dve.wait_ge(norm.normed, b * SC)
                for sc in range(SC):
                    n = b * SC + sc
                    if sc < 2:
                        if sc == 0:
                            dve.wait_ge(places_turned, b * SC)
                        equal(n, b, sc)
                for sc in range(SC):
                    n = b * SC + sc
                    if sc + 2 < SC:
                        dve.wait_ge(places_turned, n + 1)
                        equal(n + 2, b, sc + 2)
                    dve.wait_ge(summed_up, n + 1)
                    nc.vector.tensor_tensor(norm.y[:, sc], ps[:, OUT + sc % 2, 0:D], tile_of(x, n), op=ALU.add)\
                      .then_inc(norm.summed, 1)
                    norm.statistics(dve, b, sc)
                norm.invert(dve, b)
                dve.wait_ge(x_turned, b)
                dve.wait_ge(kept, b)
                for sc in range(SC):
                    norm.apply(fresh[:, sc], sc)


def time_mix_stage(nc, name, x_t, y_t, w, mix, decay, first):
    with ExitStack() as ctx:
        sb = lambda n, shape, dt=FP32: ctx.enter_context(nc.sbuf_tensor(f"{name}_{n}", shape, dt))
        sem = lambda n: ctx.enter_context(nc.semaphore(f"{name}_{n}"))
        x_sb = sb("x", [P, 2, KC, S + 1])
        mixed, before = sb("mixed", [P, 2, KC, S]), sb("before", [P, KC, S])
        w_sb = sb("w", [P, 3, KC, D])
        mix_sb, unmix = sb("mix", [P, KC]), sb("unmix", [P, KC])
        rate, now = sb("rate", [P, KC]), sb("now", [P, KC])
        rates = sb("rates", [P, KC, S])
        k_sb, kv_sb = sb("k", [P, KC, S]), sb("kv", [P, KC, S])
        past_k, past_kv = sb("past_k", [P, KC, S + 1]), sb("past_kv", [P, KC, S + 1])
        below, above, receptance = sb("below", [P, KC, S]), sb("above", [P, KC, S]), sb("receptance", [P, KC, S])
        y = sb("y", [P, 2, KC, S])
        ps = ctx.enter_context(nc.psum_tensor(f"{name}_ps", [P, 8, 512], FP32))
        loaded, x_loaded, consts = sem("loaded"), [sem("x_loaded0"), sem("x_loaded1")], sem("consts")
        mixed_seen = sem("mixed_seen")
        acts, scaled, mixed_done, projected = sem("acts"), sem("scaled"), sem("mixed_done"), sem("projected")
        low_done, k_done, receptance_done, link, y_done = (sem(n) for n in ("low_done", "k_done", "receptance_done", "link", "y_done"))
        kv_done, inverted, stored = sem("kv_done"), sem("inverted"), [sem("stored0"), sem("stored1")]
        block = ctx.enter_context(nc.Block())

        @block.sync
        def _(sp):
            def load_x(b):
                sp.dma_start(x_sb[:, b % 2, :, 1:S + 1], x_t[:, b * S:(b + 1) * S].rearrange("(k p) t -> p k t", p=P))\
                  .then_inc(x_loaded[b % 2], 16)

            load_x(0)
            for tile, source in ((mix_sb, mix), (rate, decay), (now, first)):
                sp.dma_start(tile[:], source).then_inc(loaded, 16)
            for i in range(3):
                sp.dma_start(w_sb[:, i], w[i].rearrange("(k p) f -> p k f", p=P)).then_inc(loaded, 16)
            load_x(1)
            for b in range(B):
                if b + 2 < B:
                    sp.wait_ge(mixed_done, (b + 1) * KC)
                    load_x(b + 2)
                sp.wait_ge(y_done, (b + 1) * KC)
                sp.dma_start(y_t[:, b * S:(b + 1) * S].rearrange("(k p) t -> p k t", p=P), y[:, b % 2])\
                  .then_inc(stored[b % 2], 16)
            for slot in range(2):
                sp.wait_ge(stored[slot], 16 * (B // 2))

        @block.gpsimd
        def _(pool):
            nc.gpsimd.memset(x_sb[:, :, :, 0:1], 0.0).then_inc(consts, 1)
            nc.gpsimd.memset(past_k[:, :, 0:1], 0.0).then_inc(consts, 1)
            nc.gpsimd.memset(past_kv[:, :, 0:1], 0.0).then_inc(consts, 1)
            pool.wait_ge(consts, 5)
            with pool.Fori(0, B // 2) as pairs:
                pair = pairs * 2
                for par in range(2):
                    b = pair + par
                    pool.wait_ge(x_loaded[par], pair * 8 + 16)
                    pool.wait_ge(projected, b * (3 * KC))
                    pool.sem_inc(mixed_seen, 1)
                    for k in range(KC):
                        nc.gpsimd.tensor_scalar_mul(mixed[:, par, k], x_sb[:, par, k, 1:S + 1], mix_sb[:, k:k + 1])\
                          .then_inc(scaled, 1)
                        nc.gpsimd.tensor_scalar_mul(before[:, k], x_sb[:, par, k, 0:S], unmix[:, k:k + 1])\
                          .then_inc(scaled, 1)
                    for k in range(KC):
                        pool.wait_ge(scaled, b * (2 * KC) + 2 * k + 2)
                        nc.gpsimd.tensor_tensor(mixed[:, par, k], mixed[:, par, k], before[:, k], op=ALU.add)\
                          .then_inc(mixed_done, 1)

        @block.scalar
        def _(act):
            act.wait_ge(loaded, 96)
            nc.scalar.activation(rate[:], rate[:], ACT.Exp).then_inc(acts, 1)
            nc.scalar.activation(now[:], now[:], ACT.Exp).then_inc(acts, 1)
            act.wait_ge(acts, 2)
            nc.scalar.activation(rate[:], rate[:], ACT.Exp, scale=-1.0).then_inc(acts, 1)
            with act.Fori(0, B) as b:
                for m in range(KC):
                    act.wait_ge(low_done, b * KC + m + 1)
                    nc.scalar.activation(k_sb[:, m], k_sb[:, m], ACT.Exp).then_inc(k_done, 1)
                for m in range(KC):
                    act.wait_ge(projected, b * (3 * KC) + 3 * m + 3)
                    act.wait_ge(y_done, b * KC)
                    nc.scalar.activation(receptance[:, m], ps[:, 3 * m + 2], ACT.Sigmoid).then_inc(receptance_done, 1)

        @block.tensor
        def _(pe):
            pe.wait_ge(loaded, 96)
            with pe.Fori(0, B // 2) as pairs:
                pair = pairs * 2
                for par in range(2):
                    b = pair + par
                    pe.wait_ge(mixed_done, b * KC + KC)
                    pe.wait_ge(low_done, b * KC)
                    pe.wait_ge(kv_done, b * KC)
                    pe.wait_ge(receptance_done, b * KC)
                    for m in range(KC):
                        for i in range(3):
                            for k in range(KC):
                                last = nc.tensor.matmul(ps[:, 3 * m + i], w_sb[:, i, k, m * P:(m + 1) * P],
                                                        mixed[:, par, k], start=(k == 0), stop=(k == KC - 1))
                            last.then_inc(projected, 1)

        @block.vector
        def _(dve):
            dve.wait_ge(acts, 3)
            nc.vector.tensor_scalar(unmix[:], mix_sb[:], -1.0, 1.0, op0=ALU.mult, op1=ALU.add).then_inc(consts, 1)
            nc.vector.memset(rates[:], 1.0).then_inc(consts, 1)
            dve.wait_ge(consts, 5)
            for m in range(KC):
                nc.vector.tensor_scalar_mul(rates[:, m], rates[:, m], rate[:, m:m + 1]).then_inc(consts, 1)
            dve.wait_ge(consts, 5 + KC)
            LINKS = 6
            with dve.Fori(0, B // 2) as pairs:
                pair = pairs * 2
                for par in range(2):
                    b = pair + par
                    dve.wait_ge(y_done, b * KC)
                    for m in range(KC):
                        dve.wait_ge(projected, b * (3 * KC) + 3 * m + 1)
                        nc.vector.tensor_scalar_min(k_sb[:, m], ps[:, 3 * m], 60.0).then_inc(low_done, 1)
                    for m in range(KC):
                        n = b * KC + m
                        dve.wait_ge(projected, b * (3 * KC) + 3 * m + 2)
                        dve.wait_ge(k_done, n + 1)
                        nc.vector.tensor_tensor(kv_sb[:, m], ps[:, 3 * m + 1], k_sb[:, m], op=ALU.mult).then_inc(kv_done, 1)
                        nc.vector.tensor_tensor_scan(past_k[:, m, 1:S + 1], rates[:, m], k_sb[:, m], 0.0,
                                                     op0=ALU.mult, op1=ALU.add).then_inc(link, 1)
                        dve.wait_ge(kv_done, n + 1)
                        nc.vector.tensor_tensor_scan(past_kv[:, m, 1:S + 1], rates[:, m], kv_sb[:, m], 0.0,
                                                     op0=ALU.mult, op1=ALU.add).then_inc(link, 1)
                        dve.wait_ge(link, n * LINKS + 1)
                        nc.vector.scalar_tensor_tensor(below[:, m], k_sb[:, m], now[:, m:m + 1], past_k[:, m, 0:S],
                                                       op0=ALU.mult, op1=ALU.add).then_inc(link, 1)
                        dve.wait_ge(link, n * LINKS + 2)
                        nc.vector.scalar_tensor_tensor(above[:, m], kv_sb[:, m], now[:, m:m + 1], past_kv[:, m, 0:S],
                                                       op0=ALU.mult, op1=ALU.add).then_inc(link, 1)
                        dve.wait_ge(link, n * LINKS + 3)
                        nc.vector.tensor_scalar_add(below[:, m], below[:, m], 1e-9).then_inc(link, 1)
                        dve.wait_ge(receptance_done, n + 1)
                        dve.wait_ge(link, n * LINKS + 4)
                        nc.vector.tensor_tensor(above[:, m], above[:, m], receptance[:, m], op=ALU.mult).then_inc(link, 1)
                        dve.wait_ge(link, n * LINKS + 5)
                        nc.vector.reciprocal(below[:, m], below[:, m]).then_inc(inverted, 1)
                        dve.wait_ge(link, n * LINKS + 6)
                        dve.wait_ge(inverted, n + 1)
                        if m == 0:
                            dve.wait_ge(stored[par], pair * 8)
                        nc.vector.tensor_tensor(y[:, par, m], above[:, m], below[:, m], op=ALU.mult).then_inc(y_done, 1)


E1, FF1 = 8, 1024
FC1 = FF1 // P


def gate_stage(nc, name, x_t, gate_w, order, share):
    with ExitStack() as ctx:
        sb = lambda n, shape, dt=FP32: ctx.enter_context(nc.sbuf_tensor(f"{name}_{n}", shape, dt))
        sem = lambda n: ctx.enter_context(nc.semaphore(f"{name}_{n}"))
        x_sb, w_sb, order_sb = sb("x", [P, B, KC, S]), sb("w", [P, KC, E1]), sb("order", [P, E1])
        probs, key, first, second = (sb(n, [P, TT, E1]) for n in ("probs", "key", "first", "second"))
        best, best2, rank, total = (sb(n, [P, TT]) for n in ("best", "best2", "rank", "total"))
        ps = ctx.enter_context(nc.psum_tensor(f"{name}_ps", [P, TT, E1], FP32))
        loaded, x_loaded = sem("loaded"), [sem(f"x_loaded{b}") for b in range(B)]
        logits_ready, centred, exp_done, step = (sem(n) for n in ("logits_ready", "centred", "exp_done", "step"))
        block = ctx.enter_context(nc.Block())
        spread = lambda ap: ap[:].unsqueeze(2).to_broadcast([P, TT, E1])

        @block.sync
        def _(sp):
            sp.dma_start(w_sb[:], gate_w.rearrange("(k p) f -> p k f", p=P)).then_inc(loaded, 16)
            sp.dma_start(order_sb[:], order).then_inc(loaded, 16)
            for b in range(B):
                sp.dma_start(x_sb[:, b], x_t[:, b * S:(b + 1) * S].rearrange("(k p) t -> p k t", p=P))\
                  .then_inc(x_loaded[b], 16)

        @block.tensor
        def _(pe):
            pe.wait_ge(loaded, 32)
            for b in range(B):
                pe.wait_ge(x_loaded[b], 16)
                for sc in range(SC):
                    for k in range(KC):
                        last = nc.tensor.matmul(ps[:, b * SC + sc], x_sb[:, b, k, sc * P:(sc + 1) * P], w_sb[:, k],
                                                start=(k == 0), stop=(k == KC - 1))
            last.then_inc(logits_ready, 1)

        @block.scalar
        def _(act):
            act.wait_ge(centred, 1)
            nc.scalar.activation(probs[:], probs[:], ACT.Exp).then_inc(exp_done, 1)

        @block.vector
        def _(dve):
            steps = 0

            def then_wait(instruction):
                nonlocal steps
                steps += 1
                instruction.then_inc(step, 1)
                dve.wait_ge(step, steps)

            def pick(chosen, top):
                then_wait(nc.vector.tensor_reduce(top[:], probs[:], axis=AX.X, op=ALU.max))
                then_wait(nc.vector.tensor_tensor(key[:], probs[:], spread(top), op=ALU.is_equal))
                then_wait(nc.vector.tensor_tensor(key[:], key[:], order_sb[:].unsqueeze(1).to_broadcast([P, TT, E1]),
                                                  op=ALU.mult))
                then_wait(nc.vector.tensor_reduce(rank[:], key[:], axis=AX.X, op=ALU.max))
                then_wait(nc.vector.tensor_tensor(chosen[:], key[:], spread(rank), op=ALU.is_equal))

            dve.wait_ge(logits_ready, 1)
            then_wait(nc.vector.tensor_reduce(best[:], ps[:], axis=AX.X, op=ALU.max))
            nc.vector.tensor_tensor(probs[:], ps[:], spread(best), op=ALU.subtract).then_inc(centred, 1)
            dve.wait_ge(exp_done, 1)
            then_wait(nc.vector.tensor_reduce(total[:], probs[:], axis=AX.X, op=ALU.add))
            then_wait(nc.vector.reciprocal(total[:], total[:]))
            then_wait(nc.vector.tensor_tensor(probs[:], probs[:], spread(total), op=ALU.mult))
            pick(first, best)
            then_wait(nc.vector.scalar_tensor_tensor(probs[:], first[:], -2.0, probs[:], op0=ALU.mult, op1=ALU.add))
            pick(second, best2)
            then_wait(nc.vector.tensor_tensor(total[:], best[:], best2[:], op=ALU.add))
            then_wait(nc.vector.reciprocal(total[:], total[:]))
            then_wait(nc.vector.tensor_tensor(first[:], first[:], spread(best), op=ALU.mult))
            then_wait(nc.vector.tensor_tensor(second[:], second[:], spread(best2), op=ALU.mult))
            then_wait(nc.vector.tensor_tensor(first[:], first[:], second[:], op=ALU.add))
            then_wait(nc.vector.tensor_tensor(share[:], first[:], spread(total), op=ALU.mult))


def mixture_stage(nc, name, x_t, up_w, down_w, share, total):
    with ExitStack() as ctx:
        sb = lambda n, shape, dt=FP32: ctx.enter_context(nc.sbuf_tensor(f"{name}_{n}", shape, dt))
        sem = lambda n: ctx.enter_context(nc.semaphore(f"{name}_{n}"))
        x_sb = sb("x", [P, KC, T])
        up_sb, down_sb = sb("up", [P, 2, KC, 2 * FF1]), sb("down", [P, 2, FC1, D])
        gate, act_t = sb("gate", [P, 2, S]), sb("act_t", [P, FC1, S])
        ps = ctx.enter_context(nc.psum_tensor(f"{name}_ps", [P, 8, 512], FP32))
        OUT = 4
        x_loaded, zeroed, weights_seen = sem("x_loaded"), sem("zeroed"), sem("weights_seen")
        up_loaded, down_loaded = [sem("up_loaded0"), sem("up_loaded1")], [sem("down_loaded0"), sem("down_loaded1")]
        up_ready, gate_done, act_done, down_ready, added = (
            sem(n) for n in ("up_ready", "gate_done", "act_done", "down_ready", "added"))
        block = ctx.enter_context(nc.Block())

        @block.sync
        def _(sp):
            def load(e2, j):
                e = e2 * 2 + j
                row = lambda w: w[bass.ds(e, 1)].rearrange("a (k p) f -> p (a k) f", p=P)
                sp.dma_start(up_sb[:, j], row(up_w)).then_inc(up_loaded[j], 16)
                sp.dma_start(down_sb[:, j], row(down_w)).then_inc(down_loaded[j], 16)

            sp.dma_start(x_sb[:], x_t.rearrange("(k p) t -> p k t", p=P)).then_inc(x_loaded, 16)
            load(0, 0)
            load(0, 1)
            with sp.Fori(1, E1 // 2) as e2:
                for j in range(2):
                    sp.wait_ge(down_ready, (e2 - 1) * (2 * B) + B * (j + 1))
                    load(e2, j)

        @block.tensor
        def _(pe):
            pe.wait_ge(x_loaded, 16)
            with pe.Fori(0, E1 // 2) as e2:
                for j in range(2):
                    pe.wait_ge(up_loaded[j], e2 * 16 + 16)
                    pe.wait_ge(down_loaded[j], e2 * 16 + 16)
                    pe.sem_inc(weights_seen, 1)
                    with pe.Fori(0, B) as b:
                        n = e2 * (2 * B) + j * B + b
                        for f in range(FC1):
                            pe.wait_ge(act_done, n * FC1 + (f + 1))
                            for which in range(2):
                                for k in range(KC):
                                    col = which * FF1 + f * P
                                    last = nc.tensor.matmul(ps[:, 2 * (f % 2) + which], up_sb[:, j, k, col:col + P],
                                                            x_sb[:, k, bass.ds(b * S, S)],
                                                            start=(k == 0), stop=(k == KC - 1))
                                last.then_inc(up_ready, 1)
                        pe.wait_ge(act_done, n * FC1 + (FC1 + 2))
                        pe.wait_ge(added, n)
                        for sc in range(SC):
                            for f in range(FC1):
                                last = nc.tensor.matmul(ps[:, OUT + sc, 0:D], act_t[:, f, sc * P:(sc + 1) * P],
                                                        down_sb[:, j, f], start=(f == 0), stop=(f == FC1 - 1))
                        last.then_inc(down_ready, 1)

        @block.scalar
        def _(act):
            with act.Fori(0, E1 * B) as n:
                for f in range(FC1):
                    act.wait_ge(up_ready, n * (2 * FC1) + (2 * f + 1))
                    act.wait_ge(act_done, n * FC1 + (f + 1))
                    nc.scalar.activation(gate[:, f % 2], ps[:, 2 * (f % 2)], ACT.Gelu).then_inc(gate_done, 1)

        @block.vector
        def _(dve):
            dve.sem_inc(act_done, 2)
            nc.vector.memset(total[:], 0.0).then_inc(zeroed, 1)
            dve.wait_ge(zeroed, 1)
            with dve.Fori(0, E1) as e:
                with dve.Fori(0, B) as b:
                    n = e * B + b
                    dve.wait_ge(down_ready, n)
                    for f in range(FC1):
                        dve.wait_ge(gate_done, n * FC1 + (f + 1))
                        dve.wait_ge(up_ready, n * (2 * FC1) + (2 * f + 2))
                        nc.vector.tensor_tensor(act_t[:, f], ps[:, 2 * (f % 2) + 1], gate[:, f % 2], op=ALU.mult)\
                          .then_inc(act_done, 1)
                    dve.wait_ge(down_ready, n + 1)
                    for sc in range(SC):
                        tile = total[:, bass.ds(b * SC + sc, 1)].rearrange("p a f -> p (a f)")
                        own = share[:, bass.ds(b * SC + sc, 1), bass.ds(e, 1)].rearrange("p a f -> p (a f)")
                        last = nc.vector.scalar_tensor_tensor(tile, ps[:, OUT + sc, 0:D], own, tile,
                                                              op0=ALU.mult, op1=ALU.add)
                    last.then_inc(added, 1)


def decoder(nc, a, out, upto=99):
    scratch = lambda n, shape, dt=FP32: nc.dram_tensor(n, shape, dt, kind="Internal").ap()
    x_t = [scratch(f"x_t{i}", [D, T]) for i in range(6)]
    q_parts = scratch("q_parts", [2, D, T])
    k_parts = scratch("k_parts", [2, D, T])
    with ExitStack() as ctx:
        sb = lambda n, shape, dt=FP32: ctx.enter_context(nc.sbuf_tensor(n, shape, dt))
        x = sb("x", [P, TT, D])
        ident = sb("ident", [P, P])
        ones_w = sb("gates", [P, 2])
        start_stage(nc, a, x, ident, ones_w)
        with ExitStack() as att_ctx:
            attended = att_ctx.enter_context(nc.sbuf_tensor("attended", [P, TT, D], FP32))
            v_sb = att_ctx.enter_context(nc.sbuf_tensor("v_sb", [P, TT, D], FP32))
            half = D // 2
            v_half = v_sb[:, 0:TT // 2].rearrange("p t (a f) -> p (t a) f", a=2)
            heads_stage(nc, "l0q", a["x_t"], q_parts, a["L0_attn_Wq"], D)
            heads_stage(nc, "l0k", a["x_t"], k_parts[:, 0:half], a["L0_attn_Wk"], half, v=(a["L0_attn_Wv"], None, v_half))
            memory_stage(nc, "l0m", q_parts, x, a["L0_attn_memory"], a["L0_attn_memory_norm"], ones_w)
            attention_stage(nc, "l0a", q_parts, k_parts[:, 0:half], v_half, attended, 2, ident)
            after_stage(nc, "l0n", x, x_t[0], ident, attended, blend=ones_w[:, 1:2])
            if upto <= 1: return
            heads_stage(nc, "x0q", x_t[0], q_parts, a["L0_xattn_Wq"], D, bias=a["L0_xattn_bq"],
                        rope=(a["L0_xattn_Wq_swapped"], a["L0_xattn_bq_swapped"], a["cos"], a["sin"]))
            heads_stage(nc, "x0k", a["ctx_t"], k_parts, a["L0_xattn_Wk"], D, bias=a["L0_xattn_bk"],
                        rope=(a["L0_xattn_Wk_swapped"], a["L0_xattn_bk_swapped"], a["cos"], a["sin"]),
                        v=(a["L0_xattn_Wv"], a["L0_xattn_bv"], v_sb))
            attention_stage(nc, "x0a", q_parts, k_parts, v_sb, attended, 1, ident)
            after_stage(nc, "x0n", x, x_t[1], ident, attended, wo=a["L0_xattn_Wo"], bo=a["L0_xattn_bo"])
            if upto <= 2: return
        clear_stage(nc)
        with ExitStack() as moe:
            tile = lambda n, shape: moe.enter_context(nc.sbuf_tensor(n, shape, FP32))
            slots, weights = tile("slots", [P, SC, BE]), tile("weights", [P, SC, BE])
            numbers = tile("numbers", [P, CAP])
            chosen_t, made = tile("chosen_t", [P, KC, E0, B * CAP]), tile("made", [P, E0 // 2, B, D])
            logits = scratch("logits", [BE, S])
            router_stage(nc, "er", x_t[1], a["L0_ffn_router_w1"], a["L0_ffn_router_w2"], logits)
            load_stage(nc, "en", numbers, a["numbers"])
            choice_stage(nc, "ec", logits, slots, weights, ident)
            gather_stage(nc, "eg", x, slots, numbers, chosen_t)
            expert_stage(nc, "ee", chosen_t, a["L0_ffn_w1"], a["L0_ffn_w2"], a["L0_ffn_w3"], made)
            combine_stage(nc, "es", x, x_t[2], ident, slots, weights, numbers, made)
        if upto <= 3: return
        y_t = scratch("y_t", [D, T])
        time_mix_stage(nc, "tm", x_t[2], y_t, [a[f"L1_attn_W{n}"] for n in "kvr"],
                       a["L1_attn_time_mix"], a["L1_attn_time_decay"], a["L1_attn_time_first"])
        after_stage(nc, "tn", x, x_t[3], ident, wo=a["L1_attn_Wo"], block_t=y_t)
        if upto <= 4: return
        clear_stage(nc)
        with ExitStack() as att_ctx:
            attended = att_ctx.enter_context(nc.sbuf_tensor("attended1", [P, TT, D], FP32))
            v_sb = att_ctx.enter_context(nc.sbuf_tensor("v_sb1", [P, TT, D], FP32))
            mask_q = att_ctx.enter_context(nc.sbuf_tensor("mask_q", [P, SC, S], BF16))
            mask_k = att_ctx.enter_context(nc.sbuf_tensor("mask_k", [P, SC, S], BF16))
            ident_bf = att_ctx.enter_context(nc.sbuf_tensor("ident_bf", [P, P], BF16))
            mask_stage(nc, "ms", a["mask"], a["mask_t"], mask_q, mask_k, ident, ident_bf)
            heads_stage(nc, "x1q", x_t[3], q_parts, a["L1_xattn_Wq"], D, bias=a["L1_xattn_bq"])
            heads_stage(nc, "x1k", a["ctx_t"], k_parts, a["L1_xattn_Wk"], D, bias=a["L1_xattn_bk"],
                        v=(a["L1_xattn_Wv"], a["L1_xattn_bv"], v_sb))
            attention_stage(nc, "x1a", q_parts, k_parts, v_sb, attended, 1, ident, (mask_q, mask_k, ident_bf))
            after_stage(nc, "x1n", x, x_t[4], ident, attended, wo=a["L1_xattn_Wo"], bo=a["L1_xattn_bo"])
        if upto <= 5: return
        total = sb("total", [P, TT, D])
        share = sb("share", [P, TT, E1])
        one = sb("one", [P, 1])
        gate_stage(nc, "mg", x_t[4], a["L1_ffn_gate_w"], a["order"], share)
        mixture_stage(nc, "mx", x_t[4], a["L1_ffn_gate_up_w"], a["L1_ffn_down_w"], share, total)
        load_stage(nc, "mo", one, a["ones"])
        after_stage(nc, "mn", x, None, ident, total, blend=one, out=out)


def clear_stage(nc):
    numbers = sorted(int(n) for n in nc.released_uncleared_semaphores)
    runs = []
    for n in numbers:
        if runs and runs[-1][1] == n:
            runs[-1][1] = n + 1
        else:
            runs.append([n, n + 1])
    with nc.Block() as block:
        @block.gpsimd
        def _(pool):
            for first, end in runs:
                pool.sem_clear(range(first, end))


def load_stage(nc, name, tile, source):
    with nc.semaphore(f"{name}_loaded") as loaded, nc.Block() as block:
        @block.sync
        def _(sp):
            sp.dma_start(tile[:], source).then_inc(loaded, 16)
            sp.wait_ge(loaded, 16)


def mask_stage(nc, name, mask, mask_t, mask_q, mask_k, ident, ident_bf):
    with ExitStack() as ctx:
        raw = ctx.enter_context(nc.sbuf_tensor(f"{name}_raw", [P, 2, SC, S], I32))
        loaded, done = ctx.enter_context(nc.semaphore(f"{name}_loaded")), ctx.enter_context(nc.semaphore(f"{name}_done"))
        block = ctx.enter_context(nc.Block())

        @block.sync
        def _(sp):
            for i, source in enumerate((mask, mask_t)):
                sp.dma_start(raw[:, i], source.rearrange("(c p) t -> p c t", p=P)).then_inc(loaded, 16)

        @block.vector
        def _(dve):
            nc.vector.tensor_copy(ident_bf[:], ident[:]).then_inc(done, 1)
            dve.wait_ge(loaded, 32)
            for i, tile in enumerate((mask_q, mask_k)):
                nc.vector.tensor_scalar(tile[:], raw[:, i], 0.0, MASKED, op0=ALU.is_equal, op1=ALU.mult).then_inc(done, 1)
            dve.wait_ge(done, 3)


def start_stage(nc, a, x, ident, gates):
    with ExitStack() as ctx:
        sem = lambda n: ctx.enter_context(nc.semaphore(f"start_{n}"))
        x_loaded, zeroed, ident_done, gate_loaded, gate_done = (
            sem(n) for n in ("x_loaded", "zeroed", "ident_done", "gate_loaded", "gate_done"))
        block = ctx.enter_context(nc.Block())

        @block.sync
        def _(sp):
            sp.dma_start(gates[:, 0:1], a["L0_attn_memory_weight"].partition_broadcast(P)).then_inc(gate_loaded, 16)
            sp.dma_start(x[:], a["x_tok"].rearrange("(t p) d -> p t d", p=P)).then_inc(x_loaded, 16)
            sp.wait_ge(x_loaded, 16)

        @block.gpsimd
        def _(pool):
            nc.gpsimd.memset(ident[:], 0.0).then_inc(zeroed, 1)
            pool.wait_ge(zeroed, 1)
            nc.gpsimd.affine_select(out=ident[:], in_=ident[:], compare_op=ALU.not_equal, fill=1.0,
                                    base=0, pattern=[[-1, P]], channel_multiplier=1).then_inc(ident_done, 1)

        @block.scalar
        def _(act):
            act.wait_ge(gate_loaded, 16)
            nc.scalar.activation(gates[:, 0:1], gates[:, 0:1], ACT.Sigmoid).then_inc(gate_done, 1)

        @block.vector
        def _(dve):
            dve.wait_ge(gate_done, 1)
            nc.vector.tensor_scalar(gates[:, 1:2], gates[:, 0:1], -1.0, 1.0, op0=ALU.mult, op1=ALU.add)\
              .then_inc(gate_done, 1)
            dve.wait_ge(gate_done, 2)
            dve.wait_ge(ident_done, 1)


def laid_out(inputs):
    g = {k: np.asarray(v) for k, v in inputs.items()}
    own = np.ascontiguousarray
    column = lambda v: own(v.reshape(-1, P).T)
    swap = (np.arange(D) // HD) * HD + (np.arange(D) % HD + HD // 2) % HD
    a = {"x_tok": own(g["x"].reshape(T, D)), "x_t": own(g["x"].reshape(T, D).T),
         "ctx_t": own(g["ctx_1024"].reshape(T, D).T)}
    for n in ("Wq", "Wk", "Wv", "memory", "memory_norm", "memory_weight"):
        a[f"L0_attn_{n}"] = own(g[f"L0_attn_{n}"])
    for layer in ("L0", "L1"):
        for n in "qkvo":
            a[f"{layer}_xattn_W{n}"] = own(g[f"{layer}_xattn_W{n}"].T)
        for n in "qk":
            a[f"{layer}_xattn_b{n}"] = column(g[f"{layer}_xattn_b{n}"])
        for n in "vo":
            a[f"{layer}_xattn_b{n}"] = own(g[f"{layer}_xattn_b{n}"])
    for n in "qk":
        a[f"L0_xattn_W{n}_swapped"] = own(g[f"L0_xattn_W{n}"][swap].T)
        a[f"L0_xattn_b{n}_swapped"] = column(g[f"L0_xattn_b{n}"][swap])
    inv = (np.float32(1.0) / np.float32(10000.0) ** (np.arange(0, HD, 2, dtype=np.float32) / np.float32(HD))).astype(np.float32)
    angle = (np.arange(S, dtype=np.float32)[:, None] * inv[None, :]).astype(np.float32)
    angle = np.concatenate([angle, angle], 1).T
    sign = np.where(np.arange(HD) < HD // 2, -1.0, 1.0).astype(np.float32)[:, None]
    a["cos"] = own(np.tile(np.cos(angle).astype(np.float32), (P // HD, 1)))
    a["sin"] = own(np.tile(np.sin(angle).astype(np.float32) * sign, (P // HD, 1)))
    more_laid_out(a, g, own, column)
    return a


def more_laid_out(a, g, own, column):
    for n in ("router_w1", "router_w2", "w1", "w2", "w3"):
        a[f"L0_ffn_{n}"] = own(g[f"L0_ffn_{n}"])
    for n in "kvro":
        a[f"L1_attn_W{n}"] = own(g[f"L1_attn_W{n}"].T)
    for n in ("time_mix", "time_decay", "time_first"):
        a[f"L1_attn_{n}"] = column(g[f"L1_attn_{n}"].reshape(-1))
    a["mask"] = own(g["mask_SxS2_ik0"])
    a["mask_t"] = own(g["mask_SxS2_ik0"].T)
    a["L1_ffn_gate_w"] = own(g["L1_ffn_gate_w"].T)
    a["L1_ffn_gate_up_w"] = own(g["L1_ffn_gate_up_w"].transpose(0, 2, 1))
    a["L1_ffn_down_w"] = own(g["L1_ffn_down_w"].transpose(0, 2, 1))
    rows = lambda v: own(np.tile(v.astype(np.float32)[None], (P, 1)))
    a["numbers"], a["order"], a["ones"] = rows(np.arange(CAP)), rows(np.arange(E1, 0, -1)), rows(np.ones(1))


def program(nc, arrays, **options):
    a = {n: nc.dram_tensor(f"in_{n}", v.shape, mybir.dt.from_np(v.dtype), kind="ExternalInput").ap()
         for n, v in arrays.items()}
    out = nc.dram_tensor("out", [T, D], FP32, kind="ExternalOutput").ap()
    decoder(nc, a, out, **options)


def kernel(**inputs):
    import concourse.bacc as _bacc
    from concourse.bass_utils import run_bass_kernel_spmd as _run

    arrays = laid_out(inputs)
    nc = _bacc.Bacc("TRN2", target_bir_lowering=False, num_devices=1)
    program(nc, arrays)
    r = _run(nc, [{f"in_{n}": v for n, v in arrays.items()}], core_ids=[0])
    return r.results[0]["out"].reshape(B, S, D)
```

```python
import math
from contextlib import ExitStack

import numpy as np
import concourse.bass as bass
from concourse import mybir
from concourse.alu_op_type import AluOpType as ALU

FP32 = mybir.dt.float32
F32R = mybir.dt.float32r
BF16 = mybir.dt.bfloat16
I32 = mybir.dt.int32
U32 = mybir.dt.uint32
ACT = mybir.ActivationFunctionType
AX = mybir.AxisListType

P = 128
B, S, D = 4, 512, 256
T = B * S
TT = T // P
SC = S // P
KC = D // P
NH, HD = 16, 16
GH = 4
NG = NH // GH
UNITS = NG * SC
AUG = 96
LN_EPS = 1e-5
MASKED = -1e38
START = 1


def r32(ap):
    return ap.bitcast(F32R)


def heads_stage(nc, name, src_t, dst, w, features, bias=None, rope=None, v=None):
    mcs = features // P
    with ExitStack() as ctx:
        sb = lambda n, shape, dt=FP32: ctx.enter_context(nc.sbuf_tensor(f"{name}_{n}", shape, dt))
        sem = lambda n: ctx.enter_context(nc.semaphore(f"{name}_{n}"))
        x_sb = sb("x", [P, 2, KC, S])
        w_sb = sb("w", [P, KC, features])
        hi = sb("hi", [P, 2, mcs, S], F32R)
        lo = sb("lo", [P, 2, mcs, S], F32R)
        full = sb("full", [P, mcs, S])
        bias_sb = sb("bias", [P, mcs]) if bias is not None else None
        if rope:
            w_swapped, bias_swapped, cos, sin = rope
            wsw_sb, bsw_sb = sb("wsw", [P, KC, features]), sb("bsw", [P, mcs])
            cos_sb, sin_sb = sb("cos", [P, S]), sb("sin", [P, S])
            rot_a, rot_b = sb("rot_a", [P, mcs, S]), sb("rot_b", [P, mcs, S])
        if v:
            wv, v_bias, v_sb = v
            vf = v_sb.shape[2]
            wv_sb, vb_sb = sb("wv", [P, KC, vf]), sb("vb", [P, vf])
        ps = ctx.enter_context(nc.psum_tensor(f"{name}_ps", [P, 8, 512], FP32))
        V_BANK = 4
        weights_loaded, x_loaded = sem("weights_loaded"), [sem("x_loaded0"), sem("x_loaded1")]
        projected = sem("projected")
        rotated, hi_done, lo_done = sem("rotated"), sem("hi_done"), sem("lo_done")
        stored = [sem("stored0"), sem("stored1")]
        v_projected, v_done, halves = sem("v_projected"), sem("v_done"), sem("halves")
        n_weights = 1 + (bias is not None) + 4 * bool(rope) + (1 + (v is not None and v[1] is not None)) * bool(v)
        block = ctx.enter_context(nc.Block())

        @block.sync
        def _(sp):
            for semaphore in stored:
                sp.sem_inc(semaphore, START)
            def load_x(b):
                if b >= 2:
                    sp.wait_ge(projected, mcs * (b - 1))
                    if v:
                        sp.wait_ge(v_projected, SC * (b - 1))
                sp.dma_start(x_sb[:, b % 2], src_t[:, b * S:(b + 1) * S].rearrange("(k p) t -> p k t", p=P))\
                  .then_inc(x_loaded[b % 2], 16)

            load_x(0)
            sp.dma_start(w_sb[:], w.rearrange("(k p) f -> p k f", p=P)).then_inc(weights_loaded, 16)
            if bias is not None:
                sp.dma_start(bias_sb[:], bias).then_inc(weights_loaded, 16)
            if rope:
                sp.dma_start(wsw_sb[:], w_swapped.rearrange("(k p) f -> p k f", p=P)).then_inc(weights_loaded, 16)
                sp.dma_start(bsw_sb[:], bias_swapped).then_inc(weights_loaded, 16)
                sp.dma_start(cos_sb[:], cos).then_inc(weights_loaded, 16)
                sp.dma_start(sin_sb[:], sin).then_inc(weights_loaded, 16)
            if v:
                sp.dma_start(wv_sb[:], wv.rearrange("(k p) f -> p k f", p=P)).then_inc(weights_loaded, 16)
                if v_bias is not None:
                    sp.dma_start(vb_sb[:], v_bias.partition_broadcast(P)).then_inc(weights_loaded, 16)
            load_x(1)
            for b in range(B):
                for m in range(mcs):
                    sp.wait_ge(lo_done, START + b * mcs + m + 1)
                    for part, tile in enumerate((hi, lo)):
                        sp.dma_start(dst[part, m * P:(m + 1) * P, b * S:(b + 1) * S],
                                     tile[:, b % 2, m].bitcast(FP32)).then_inc(stored[b % 2], 16)
                if b + 2 < B:
                    load_x(b + 2)
            for slot in range(2):
                sp.wait_ge(stored[slot], START + 32 * mcs * (B // 2))

        @block.tensor
        def _(pe):
            pe.wait_ge(weights_loaded, 16 * n_weights)
            with pe.Fori(0, B // 2) as pairs:
                pair = pairs * 2
                for par in range(2):
                    b = pair + par
                    pe.wait_ge(x_loaded[par], pair * 8 + 16)
                    pe.wait_ge(lo_done, START + b * mcs)
                    for m in range(mcs):
                        for k in range(KC):
                            last = nc.tensor.matmul(ps[:, m], w_sb[:, k, m * P:(m + 1) * P], x_sb[:, par, k],
                                                    start=(k == 0), stop=(k == KC - 1))
                        if rope:
                            for k in range(KC):
                                last = nc.tensor.matmul(ps[:, mcs + m], wsw_sb[:, k, m * P:(m + 1) * P],
                                                        x_sb[:, par, k], start=(k == 0), stop=(k == KC - 1))
                        last.then_inc(projected, 1)
                    if v:
                        pe.wait_ge(v_done, START + b * SC)
                        for sc in range(SC):
                            for k in range(KC):
                                last = nc.tensor.matmul(ps[:, V_BANK + sc, 0:vf], x_sb[:, par, k, sc * P:(sc + 1) * P],
                                                        wv_sb[:, k], start=(k == 0), stop=(k == KC - 1))
                            last.then_inc(v_projected, 1)

        @block.scalar
        def _(act):
            act.sem_inc(hi_done, START)
            act.wait_ge(weights_loaded, 16 * n_weights)
            with act.Fori(0, B // 2) as pairs:
                pair = pairs * 2
                for par in range(2):
                    b = pair + par
                    act.wait_ge(stored[par], START + pair * (16 * mcs))
                    for m in range(mcs):
                        if rope:
                            act.wait_ge(rotated, b * mcs + m + 1)
                            nc.scalar.activation(hi[:, par, m], full[:, m], ACT.Copy).then_inc(hi_done, 1)
                        else:
                            act.wait_ge(projected, b * mcs + m + 1)
                            nc.scalar.activation(hi[:, par, m], ps[:, m], ACT.Identity,
                                                 bias=bias_sb[:, m:m + 1] if bias is not None else 0.0).then_inc(hi_done, 1)

        @block.vector
        def _(dve):
            dve.sem_inc(lo_done, START)
            dve.sem_inc(v_done, START)
            dve.wait_ge(weights_loaded, 16 * n_weights)
            with dve.Fori(0, B // 2) as pairs:
                pair = pairs * 2
                for par in range(2):
                    b = pair + par
                    dve.wait_ge(stored[par], START + pair * (16 * mcs))
                    for m in range(mcs):
                        i = b * mcs + m
                        dve.wait_ge(projected, i + 1)
                        if rope:
                            nc.vector.scalar_tensor_tensor(rot_a[:, m], ps[:, m], bias_sb[:, m:m + 1], cos_sb[:],
                                                           op0=ALU.add, op1=ALU.mult).then_inc(halves, 1)
                            nc.vector.scalar_tensor_tensor(rot_b[:, m], ps[:, mcs + m], bsw_sb[:, m:m + 1], sin_sb[:],
                                                           op0=ALU.add, op1=ALU.mult).then_inc(halves, 1)
                            dve.wait_ge(halves, i * 2 + 2)
                            dve.wait_ge(hi_done, START + b * mcs)
                            nc.vector.tensor_tensor(full[:, m], rot_a[:, m], rot_b[:, m], op=ALU.add).then_inc(rotated, 1)
                    for m in range(mcs):
                        i = b * mcs + m
                        dve.wait_ge(hi_done, START + i + 1)
                        if rope:
                            dve.wait_ge(rotated, i + 1)
                            nc.vector.tensor_tensor(lo[:, par, m], full[:, m], hi[:, par, m].bitcast(FP32),
                                                    op=ALU.subtract).then_inc(lo_done, 1)
                        elif bias is not None:
                            nc.vector.scalar_tensor_tensor(lo[:, par, m], ps[:, m], bias_sb[:, m:m + 1],
                                                           hi[:, par, m].bitcast(FP32),
                                                           op0=ALU.add, op1=ALU.subtract).then_inc(lo_done, 1)
                        else:
                            nc.vector.tensor_tensor(lo[:, par, m], ps[:, m], hi[:, par, m].bitcast(FP32),
                                                    op=ALU.subtract).then_inc(lo_done, 1)
                    if v:
                        for sc in range(SC):
                            dve.wait_ge(v_projected, b * SC + sc + 1)
                            tile = v_sb[:, bass.ds(b * SC + sc, 1), :].rearrange("p a f -> p (a f)")
                            if v_bias is not None:
                                nc.vector.tensor_tensor(tile, ps[:, V_BANK + sc, 0:vf], vb_sb[:], op=ALU.add).then_inc(v_done, 1)
                            else:
                                nc.vector.tensor_copy(tile, ps[:, V_BANK + sc, 0:vf]).then_inc(v_done, 1)


def attention_stage(nc, name, q_parts, k_parts, v_sb, attended, rep, ident, masks=None):
    KG = GH // rep
    G = B * NG
    with ExitStack() as ctx:
        sb = lambda n, shape, dt=FP32: ctx.enter_context(nc.sbuf_tensor(f"{name}_{n}", shape, dt))
        sem = lambda n: ctx.enter_context(nc.semaphore(f"{name}_{n}"))
        q4 = sb("q4", [P, NH, S], F32R)
        k4 = sb("k4", [P, NH // rep, S], F32R)
        probs = sb("probs", [P, SC, GH, S])
        values = sb("values", [P, SC, NH, 32])
        out_t = sb("out_t", [P, NG, S])
        shift = sb("shift", [P, 2, GH * SC])
        aug = sb("aug", [GH * SC, 2, 2, P], F32R)
        sums = sb("sums", [P, SC, NH])
        ps = ctx.enter_context(nc.psum_tensor(f"{name}_ps", [P, 8, 512], FP32))
        MAX_BANK, OUT_BANK, TURN_BANK = 4, 6, 7
        heads_loaded = [sem(f"heads_loaded{g}") for g in range(NG)]
        slots_ready, aug_loaded = sem("slots_ready"), sem("aug_loaded")
        scores_ready, exp_done = sem("scores_ready"), sem("exp_done")
        max_scores_ready, max_done = sem("max_scores_ready"), sem("max_done")
        first_zeroed, rest_zeroed = sem("first_zeroed"), sem("rest_zeroed")
        shift_turned, aug_done, values_ready = sem("shift_turned"), sem("aug_done"), sem("values_ready")
        probs_used, out_copied, out_turned = sem("probs_used"), sem("out_copied"), sem("out_turned")
        sums_done, normed = sem("sums_done"), sem("normed")
        block = ctx.enter_context(nc.Block())
        BANK_CREDIT, PROBS_CREDIT = 2, SC

        @block.sync
        def _(sp):
            def load_heads(b, g):
                for r, part in enumerate((0, 1, 0)):
                    sp.dma_start(q4[r * HD:(r + 1) * HD, g * GH:(g + 1) * GH].bitcast(FP32),
                                 q_parts[part, g * GH * HD:(g + 1) * GH * HD, bass.ds(b * S, S)]
                                 .rearrange("(h d) t -> d h t", d=HD)).then_inc(heads_loaded[g], 16)
                for r, part in enumerate((0, 0, 1)):
                    sp.dma_start(k4[r * HD:(r + 1) * HD, g * KG:(g + 1) * KG].bitcast(FP32),
                                 k_parts[part, g * KG * HD:(g + 1) * KG * HD, bass.ds(b * S, S)]
                                 .rearrange("(h d) t -> d h t", d=HD)).then_inc(heads_loaded[g], 16)

            def load_aug(index, slot, par):
                sp.wait_ge(aug_done, 2 * index + 2)
                for part in range(2):
                    sp.dma_start(q4[AUG + part:AUG + part + 1, slot * GH:(slot + 1) * GH].bitcast(FP32),
                                 aug[:, par, part].bitcast(FP32)).then_inc(aug_loaded, 16)

            sp.wait_ge(first_zeroed, 2)
            load_heads(0, 0)
            sp.wait_ge(rest_zeroed, 2)
            for g in range(1, NG):
                load_heads(0, g)
            load_aug(0, 0, 0)
            with sp.Fori(0, B - 1) as b:
                for g in range(NG):
                    load_aug(b * NG + g + 1, (g + 1) % NG, (g + 1) % 2)
                    sp.wait_ge(scores_ready, b * (2 * UNITS) + 2 * SC * (g + 1))
                    load_heads(b + 1, g)
            for g in range(NG - 1):
                load_aug((B - 1) * NG + g + 1, g + 1, (g + 1) % 2)

        @block.gpsimd
        def _(pool):
            nc.gpsimd.memset(q4[:, GH:].bitcast(FP32), 0.0).then_inc(rest_zeroed, 1)
            nc.gpsimd.memset(k4[:, KG:].bitcast(FP32), 0.0).then_inc(rest_zeroed, 1)
            nc.gpsimd.memset(values[:], 0.0).then_inc(slots_ready, 1)
            pool.wait_ge(rest_zeroed, 2)
            pool.wait_ge(slots_ready, 3)
            nc.gpsimd.memset(k4[AUG:AUG + 2, KG:].bitcast(FP32), 1.0).then_inc(slots_ready, 1)
            pool.wait_ge(slots_ready, 4)
            nc.gpsimd.memset(values[:, :, :, HD:HD + 1], 1.0).then_inc(slots_ready, 1)
            pool.wait_ge(slots_ready, 5)

            def spread(b, g):
                for r in range(rep):
                    last = nc.gpsimd.tensor_copy(
                        values[:, :, g * GH + r:(g + 1) * GH:rep, 0:HD],
                        v_sb[:, bass.ds(b * SC, SC), g * KG * HD:(g + 1) * KG * HD]
                        .rearrange("p c (h d) -> p c h d", d=HD))
                last.then_inc(values_ready, 1)

            for g in range(NG):
                spread(0, g)
            with pool.Fori(1, B) as b:
                for g in range(NG):
                    pool.wait_ge(probs_used, (b - 1) * UNITS + (PROBS_CREDIT + SC * (g + 1)))
                    spread(b, g)

        @block.tensor
        def _(pe):
            pe.sem_inc(out_turned, START)
            pe.sem_inc(probs_used, PROBS_CREDIT)
            pe.wait_ge(slots_ready, 5)

            def max_scores(b, index, slot, h, sc):
                if h == 0 and sc == 0:
                    pe.wait_ge(heads_loaded[slot], b * 96 + 96)
                m = h * SC + sc
                pe.wait_ge(max_done, index * (GH * SC) + m + 1)
                bank = MAX_BANK + sc % 2
                last = nc.tensor.matmul(ps[:, bank], q4[0:AUG, slot * GH + h, sc * P:(sc + 1) * P],
                                        k4[0:AUG, (slot * GH + h) // rep], start=True, stop=masks is None)
                if masks:
                    last = nc.tensor.matmul(ps[:, bank], masks[2][:], masks[0][:, sc], start=False, stop=True)
                last.then_inc(max_scores_ready, 1)

            def turn_shift(index, par, b=0):
                pe.wait_ge(normed, START + b * SC)
                pe.wait_ge(max_done, index * (GH * SC) + (GH * SC + BANK_CREDIT))
                pe.wait_ge(aug_done, index * 2)
                nc.tensor.transpose(ps[0:GH * SC, TURN_BANK, 0:P], shift[:, par], ident[:]).then_inc(shift_turned, 1)

            def scores(b, g, tc, pair):
                n = b * UNITS + g * SC + tc
                if tc == 0 and pair == 0:
                    pe.wait_ge(aug_loaded, b * (32 * NG) + 32 * (g + 1))
                pe.wait_ge(exp_done, n * 2 + pair + 1)
                for j in range(2):
                    h = g * GH + 2 * pair + j
                    last = nc.tensor.matmul(ps[:, 2 * pair + j], k4[0:AUG + 2, h // rep, tc * P:(tc + 1) * P],
                                            q4[0:AUG + 2, h], start=True, stop=masks is None)
                    if masks:
                        last = nc.tensor.matmul(ps[:, 2 * pair + j], masks[2][:], masks[1][:, tc],
                                                start=False, stop=True)
                last.then_inc(scores_ready, 1)

            def weigh(b, g, tc):
                n = b * UNITS + g * SC + tc
                if tc == 0:
                    pe.wait_ge(values_ready, b * NG + g + 1)
                    pe.wait_ge(out_copied, START + b * NG + g)
                    if g == 0:
                        pe.wait_ge(normed, START + b * SC)
                pe.wait_ge(exp_done, n * 2 + 2 + BANK_CREDIT)
                for h in range(GH):
                    last = nc.tensor.matmul(ps[32 * h:32 * h + 32, OUT_BANK], values[:, tc, g * GH + h],
                                            probs[:, tc, h], start=(tc == 0), stop=(tc == SC - 1))
                last.then_inc(probs_used, 1)

            def turn_out(b, last):
                pe.wait_ge(out_copied, START + b * NG + NG)
                pe.wait_ge(aug_done, 2 * G if last else b * (2 * NG) + 2 * (NG + 1))
                for sc in range(SC):
                    pe.wait_ge(normed, START + b * SC + max(sc - 1, 0))
                    for g in range(NG):
                        last = nc.tensor.transpose(ps[:, TURN_BANK - sc % 2, g * P:(g + 1) * P],
                                                   out_t[:, g, sc * P:(sc + 1) * P], ident[:])
                    last.then_inc(out_turned, 1)

            def batch(b, last):
                for g in range(NG):
                    for tc in range(SC):
                        ahead = not (last and g >= NG - 2)
                        later = lambda sc: max_scores(b + (g + 2) // NG, b * NG + g + 2, (g + 2) % NG, tc, sc)
                        if ahead:
                            later(0)
                        scores(b, g, tc, 0)
                        if ahead:
                            later(1)
                        if tc == 0 and not (last and g == NG - 1):
                            turn_shift(b * NG + g + 1, (g + 1) % 2, b)
                        scores(b, g, tc, 1)
                        if ahead:
                            later(2)
                        if g or tc:
                            weigh(b, (g * SC + tc - 1) // SC, (tc - 1) % SC)
                        if ahead:
                            later(3)
                weigh(b, NG - 1, SC - 1)
                turn_out(b, last)

            for index in range(2):
                for h in range(GH):
                    for sc in range(SC):
                        max_scores(0, index, index, h, sc)
                if index == 0:
                    turn_shift(0, 0)
            with pe.Fori(0, B - 1) as b:
                batch(b, False)
            batch(B - 1, True)

        def copy_out(act, b, g):
            act.wait_ge(probs_used, b * UNITS + (SC * (g + 1) + PROBS_CREDIT))
            act.wait_ge(out_turned, START + b * SC)
            nc.scalar.activation(out_t[:, g], ps[:, OUT_BANK], ACT.Copy).then_inc(out_copied, 1)

        @block.scalar
        def _(act):
            act.sem_inc(exp_done, BANK_CREDIT)
            act.sem_inc(out_copied, START)
            with act.Fori(0, B) as b:
                for g in range(NG):
                    for tc in range(SC):
                        n = b * UNITS + g * SC + tc
                        act.wait_ge(probs_used, n + 1)
                        for pair in range(2):
                            act.wait_ge(scores_ready, n * 2 + pair + 1)
                            nc.scalar.activation(probs[:, tc, 2 * pair:2 * pair + 2], ps[:, 2 * pair:2 * pair + 2],
                                                 ACT.Exp, scale=HD ** -0.5).then_inc(exp_done, 1)
                        if tc == 0 and g > 0:
                            copy_out(act, b, g - 1)
                copy_out(act, b, NG - 1)

        @block.vector
        def _(dve):
            dve.sem_inc(normed, START)
            nc.vector.memset(q4[:, 0:GH].bitcast(FP32), 0.0).then_inc(first_zeroed, 1)
            nc.vector.memset(k4[:, 0:KG].bitcast(FP32), 0.0).then_inc(first_zeroed, 1)
            dve.wait_ge(first_zeroed, 2)
            nc.vector.memset(k4[AUG:AUG + 2, 0:KG].bitcast(FP32), 1.0).then_inc(slots_ready, 2)
            dve.sem_inc(max_done, BANK_CREDIT)

            def maxima(index, par, h):
                for sc in range(SC):
                    m = h * SC + sc
                    dve.wait_ge(max_scores_ready, index * (GH * SC) + m + 1)
                    nc.vector.tensor_reduce(shift[:, par, m:m + 1], ps[:, MAX_BANK + sc % 2], axis=AX.X,
                                            op=ALU.max, negate=True).then_inc(max_done, 1)

            def split_shift(index, par):
                rows = ps[0:GH * SC, TURN_BANK, 0:P]
                dve.wait_ge(shift_turned, index + 1)
                nc.vector.tensor_copy(aug[:, par, 0], rows).then_inc(aug_done, 1)
                dve.wait_ge(aug_done, index * 2 + 1)
                nc.vector.tensor_tensor(aug[:, par, 1], rows, aug[:, par, 0].bitcast(FP32),
                                        op=ALU.subtract).then_inc(aug_done, 1)

            def normalise(b):
                for sc in range(SC):
                    turned = ps[:, TURN_BANK - sc % 2].rearrange("p (h c) -> p h c", c=32)
                    dve.wait_ge(out_turned, START + b * SC + sc + 1)
                    nc.vector.reciprocal(sums[:, sc], turned[:, :, HD]).then_inc(sums_done, 1)
                    dve.wait_ge(sums_done, b * SC + sc + 1)
                    nc.vector.tensor_tensor(
                        attended[:, bass.ds(b * SC + sc, 1), :].rearrange("p a (h d) -> p (a h) d", d=HD),
                        turned[:, :, 0:HD], sums[:, sc].unsqueeze(2).to_broadcast([P, NH, HD]),
                        op=ALU.mult).then_inc(normed, 1)

            def batch(b, last):
                for g in range(NG):
                    for tc in range(SC):
                        if not (last and g >= NG - 2):
                            maxima(b * NG + g + 2, g % 2, tc)
                        if tc == 0 and not (last and g == NG - 1):
                            split_shift(b * NG + g + 1, (g + 1) % 2)
                normalise(b)

            for index in range(2):
                for h in range(GH):
                    maxima(index, index, h)
                if index == 0:
                    split_shift(0, 0)
            with dve.Fori(0, B - 1) as b:
                batch(b, False)
            batch(B - 1, True)


def memory_stage(nc, name, q_parts, x, memory, memory_norm, mem_w):
    with ExitStack() as ctx:
        sb = lambda n, shape, dt=FP32: ctx.enter_context(nc.sbuf_tensor(f"{name}_{n}", shape, dt))
        sem = lambda n: ctx.enter_context(nc.semaphore(f"{name}_{n}"))
        q_sb = sb("q", [P, 2, 2, KC, S])
        mem_sb = sb("mem", [P, P + 1])
        q, low, positive, sigma = (sb(n, [P, KC, S]) for n in ("sum", "low", "positive", "sigma"))
        weight = sb("weight", [P, SC, KC])
        ps = ctx.enter_context(nc.psum_tensor(f"{name}_ps", [P, SC, 2, 256], FP32))
        loaded, mem_loaded = [sem("loaded0"), sem("loaded1")], sem("mem_loaded")
        q_done, low_done, exp_done, positive_done, sigma_done = (
            sem(n) for n in ("q_done", "low_done", "exp_done", "positive_done", "sigma_done"))
        retrieved, steps, added = sem("retrieved"), sem("steps"), sem("added")
        block = ctx.enter_context(nc.Block())

        @block.sync
        def _(sp):
            sp.dma_start(mem_sb[:, 0:P], memory).then_inc(mem_loaded, 16)
            sp.dma_start(mem_sb[:, P:P + 1], memory_norm.rearrange("(p a) -> p a", a=1)).then_inc(mem_loaded, 16)
            for b in range(B):
                if b >= 2:
                    sp.wait_ge(q_done, b - 1)
                for part in range(2):
                    sp.dma_start(q_sb[:, b % 2, part], q_parts[part, :, b * S:(b + 1) * S]
                                 .rearrange("(k p) t -> p k t", p=P)).then_inc(loaded[b % 2], 16)

        @block.gpsimd
        def _(pool):
            with pool.Fori(0, B // 2) as pairs:
                pair = pairs * 2
                for par in range(2):
                    pool.wait_ge(loaded[par], pair * 16 + 32)
                    pool.wait_ge(positive_done, START + pair + par)
                    pool.wait_ge(low_done, START + pair + par)
                    nc.gpsimd.tensor_tensor(q[:], q_sb[:, par, 0], q_sb[:, par, 1], op=ALU.add).then_inc(q_done, 1)

        @block.scalar
        def _(act):
            act.sem_inc(positive_done, START)
            with act.Fori(0, B) as b:
                act.wait_ge(q_done, b + 1)
                act.wait_ge(sigma_done, START + b)
                nc.scalar.activation(positive[:], q[:], ACT.Relu).then_inc(positive_done, 1)
                act.wait_ge(low_done, START + b + 1)
                nc.scalar.activation(low[:], low[:], ACT.Exp).then_inc(exp_done, 1)

        @block.vector
        def _(dve):
            dve.sem_inc(added, START)
            dve.sem_inc(low_done, START)
            dve.sem_inc(sigma_done, START)
            dve.wait_ge(q_done, 1)
            with dve.Fori(0, B) as b:
                dve.wait_ge(q_done, b + 1)
                nc.vector.tensor_scalar_min(low[:], q[:], 0.0).then_inc(low_done, 1)
                dve.wait_ge(exp_done, b + 1)
                dve.wait_ge(positive_done, START + b + 1)
                dve.wait_ge(retrieved, START + b * SC)
                nc.vector.scalar_tensor_tensor(sigma[:], low[:], -1.0, positive[:], op0=ALU.add, op1=ALU.add)\
                  .then_inc(sigma_done, 1)
                for sc in range(SC):
                    dve.wait_ge(retrieved, START + b * SC + sc + 1)
                    nc.vector.reciprocal(weight[:, sc], ps[:, sc, :, P]).then_inc(steps, 1)
                    dve.wait_ge(steps, b * (2 * SC) + 2 * sc + 1)
                    nc.vector.tensor_scalar_mul(weight[:, sc], weight[:, sc], mem_w[:, 0:1]).then_inc(steps, 1)
                    dve.wait_ge(steps, b * (2 * SC) + 2 * sc + 2)
                    tile = x[:, bass.ds(b * SC + sc, 1), :].rearrange("p a f -> p (a f)")
                    for j in range(2):
                        last = nc.vector.scalar_tensor_tensor(tile[:, j * P:(j + 1) * P], ps[:, sc, j, 0:P],
                                                              weight[:, sc, j:j + 1], tile[:, j * P:(j + 1) * P],
                                                              op0=ALU.mult, op1=ALU.add)
                    last.then_inc(added, 1)

        @block.tensor
        def _(pe):
            pe.sem_inc(retrieved, START)
            pe.wait_ge(mem_loaded, 32)
            with pe.Fori(0, B) as b:
                pe.wait_ge(sigma_done, START + b + 1)
                pe.wait_ge(added, START + b * SC)
                for sc in range(SC):
                    for j in range(2):
                        last = nc.tensor.matmul(ps[:, sc, j, 0:P + 1], sigma[:, j, sc * P:(sc + 1) * P], mem_sb[:],
                                                start=True, stop=True)
                    last.then_inc(retrieved, 1)


class Norm:

    def __init__(self, ctx, nc, name):
        sb = lambda n, shape: ctx.enter_context(nc.sbuf_tensor(f"{name}_{n}", shape, FP32))
        sem = lambda n: ctx.enter_context(nc.semaphore(f"{name}_{n}"))
        self.nc = nc
        self.y = sb("y", [P, SC, D])
        self.stats, self.moments = sb("stats", [P, SC, 6]), sb("moments", [P, SC, 2])
        self.rstd, self.eps = sb("rstd", [P, SC]), sb("eps", [P, 1])
        self.summed, self.stats_done, self.moments_done = sem("summed"), sem("stats_done"), sem("moments_done")
        self.eps_ready, self.root_done, self.rstd_done = sem("eps_ready"), sem("root_done"), sem("rstd_done")
        self.normed, self.stats_seen = sem("normed"), sem("stats_seen")

    def statistics(self, dve, b, sc):
        dve.wait_ge(self.summed, START + b * SC + sc + 1)
        self.nc.vector.bn_stats(self.stats[:, sc], self.y[:, sc]).then_inc(self.stats_done, 1)
        dve.wait_ge(self.stats_done, b * SC + sc + 1)
        dve.sem_inc(self.stats_seen, 1)
        self.nc.vector.bn_aggr(self.moments[:, sc], self.stats[:, sc]).then_inc(self.moments_done, 1)

    def root(self, act, b):
        act.wait_ge(self.eps_ready, 1)
        act.wait_ge(self.moments_done, b * SC + SC)
        act.wait_ge(self.normed, START + b * SC)
        self.nc.scalar.activation(self.rstd[:], self.moments[:, :, 1], ACT.Sqrt, bias=self.eps[:, 0:1])\
            .then_inc(self.root_done, 1)

    def invert(self, dve, b):
        dve.wait_ge(self.root_done, b + 1)
        self.nc.vector.reciprocal(self.rstd[:], self.rstd[:]).then_inc(self.rstd_done, 1)
        dve.wait_ge(self.rstd_done, b + 1)

    def apply(self, out, sc):
        self.nc.vector.tensor_scalar(out, self.y[:, sc], self.moments[:, sc, 0:1], self.rstd[:, sc:sc + 1],
                                     op0=ALU.subtract, op1=ALU.mult).then_inc(self.normed, 1)


def after_stage(nc, name, x, x_t, ident, attended=None, blend=None, wo=None, bo=None,
                block_t=None, out=None):
    turns = wo is not None and block_t is None
    with ExitStack() as ctx:
        sb = lambda n, shape, dt=FP32: ctx.enter_context(nc.sbuf_tensor(f"{name}_{n}", shape, dt))
        sem = lambda n: ctx.enter_context(nc.semaphore(f"{name}_{n}"))
        norm = Norm(ctx, nc, f"{name}_norm")
        fresh = sb("fresh", [P, 2, SC, D])
        turned = sb("turned", [P, 2, KC, S])
        ps = ctx.enter_context(nc.psum_tensor(f"{name}_ps", [P, 8, 512], FP32))
        TURN, ATT, PROJ = 0, 2, 4
        if wo is not None:
            wo_sb = sb("wo", [P, KC, D])
            att_t = sb("att_t", [P, 2, KC, S])
        if bo is not None:
            bo_sb = sb("bo", [P, D])
        if turns:
            att = sb("att", [P, 2, SC, D])
        weights_loaded, att_copied, att_turned, att_t_done, projected = (
            sem(n) for n in ("weights_loaded", "att_copied", "att_turned", "att_t_done", "projected"))
        biased, block_loaded = sem("biased"), [sem("block_loaded0"), sem("block_loaded1")]
        kept, x_turned, turned_done = (sem(n) for n in ("kept", "x_turned", "turned_done"))
        stored = [sem("stored0"), sem("stored1")]
        block = ctx.enter_context(nc.Block())

        @block.sync
        def _(sp):
            for semaphore in stored:
                sp.sem_inc(semaphore, START)
            if wo is not None:
                sp.dma_start(wo_sb[:], wo.rearrange("(k p) f -> p k f", p=P)).then_inc(weights_loaded, 16)
                if bo is not None:
                    sp.dma_start(bo_sb[:], bo.partition_broadcast(P)).then_inc(weights_loaded, 16)

            def load_block(b):
                sp.dma_start(att_t[:, b % 2], block_t[:, b * S:(b + 1) * S].rearrange("(k p) t -> p k t", p=P))\
                  .then_inc(block_loaded[b % 2], 16)

            if block_t is not None:
                load_block(0)
                load_block(1)
            for b in range(B):
                if block_t is not None and b + 2 < B:
                    sp.wait_ge(projected, START + (b + 1) * SC)
                    load_block(b + 2)
                if out is None:
                    sp.wait_ge(turned_done, START + b + 1)
                    sp.dma_start(x_t[:, b * S:(b + 1) * S].rearrange("(k p) t -> p k t", p=P), turned[:, b % 2])\
                      .then_inc(stored[b % 2], 16)
                else:
                    sp.wait_ge(norm.normed, START + (b + 1) * SC)
                    sp.dma_start(out[b * S:(b + 1) * S].rearrange("(c p) d -> p c d", p=P), fresh[:, b % 2])\
                      .then_inc(stored[b % 2], 16)
            for slot in range(2):
                sp.wait_ge(stored[slot], START + 16 * (B // 2))

        @block.gpsimd
        def _(pool):
            pool.sem_inc(kept, START)
            nc.gpsimd.memset(norm.eps[:], LN_EPS).then_inc(norm.eps_ready, 1)
            if bo is not None:
                pool.wait_ge(weights_loaded, 32)
                for tt in range(TT):
                    nc.gpsimd.tensor_tensor(x[:, tt], x[:, tt], bo_sb[:], op=ALU.add).then_inc(biased, 1)
            if out is not None:
                return
            with pool.Fori(0, B // 2) as pairs:
                pair = pairs * 2
                for par in range(2):
                    b = pair + par
                    pool.wait_ge(norm.normed, START + b * SC + SC)
                    nc.gpsimd.tensor_copy(x[:, bass.ds(b * SC, SC)], fresh[:, par]).then_inc(kept, 1)

        @block.scalar
        def _(act):
            act.sem_inc(turned_done, START)
            act.sem_inc(att_t_done, START)
            with act.Fori(0, B // 2) as pairs:
                pair = pairs * 2
                for par in range(2):
                    b = pair + par
                    if turns:
                        act.wait_ge(att_turned, START + b)
                        nc.scalar.activation(att[:, par], attended[:, bass.ds(b * SC, SC)], ACT.Copy)\
                          .then_inc(att_copied, 1)
                        act.wait_ge(att_turned, START + b + 1)
                        act.wait_ge(projected, START + b * SC)
                        nc.scalar.activation(att_t[:, par], ps[:, ATT:ATT + KC], ACT.Copy).then_inc(att_t_done, 1)
                    norm.root(act, b)
                    if out is None:
                        act.wait_ge(x_turned, START + b + 1)
                        act.wait_ge(stored[par], START + pair * 8)
                        nc.scalar.activation(turned[:, par], ps[:, TURN:TURN + KC], ACT.Copy).then_inc(turned_done, 1)

        @block.tensor
        def _(pe):
            pe.sem_inc(x_turned, START)
            pe.sem_inc(att_turned, START)
            pe.sem_inc(projected, START)
            if wo is not None:
                pe.wait_ge(weights_loaded, 16 + 16 * (bo is not None))
            with pe.Fori(0, B // 2) as pairs:
                pair = pairs * 2
                for par in range(2):
                    b = pair + par
                    if turns:
                        pe.wait_ge(att_copied, b + 1)
                        pe.wait_ge(att_t_done, START + b)
                        for sc in range(SC):
                            for k in range(KC):
                                last = nc.tensor.transpose(ps[:, ATT + k, sc * P:(sc + 1) * P],
                                                           att[:, par, sc, k * P:(k + 1) * P], ident[:])
                        last.then_inc(att_turned, 1)
                        pe.wait_ge(att_t_done, START + b + 1)
                    elif wo is not None:
                        pe.wait_ge(block_loaded[par], pair * 8 + 16)
                    if wo is not None:
                        pe.wait_ge(norm.summed, START + b * SC)
                        for sc in range(SC):
                            for k in range(KC):
                                last = nc.tensor.matmul(ps[:, PROJ + sc, 0:D], att_t[:, par, k, sc * P:(sc + 1) * P],
                                                        wo_sb[:, k], start=(k == 0), stop=(k == KC - 1))
                            last.then_inc(projected, 1)
                    if out is None:
                        pe.wait_ge(norm.normed, START + b * SC + SC)
                        pe.wait_ge(turned_done, START + b)
                        for sc in range(SC):
                            for k in range(KC):
                                last = nc.tensor.transpose(ps[:, TURN + k, sc * P:(sc + 1) * P],
                                                           fresh[:, par, sc, k * P:(k + 1) * P], ident[:])
                        last.then_inc(x_turned, 1)

        @block.vector
        def _(dve):
            dve.sem_inc(norm.normed, START)
            dve.sem_inc(norm.summed, START)
            if bo is not None:
                dve.wait_ge(biased, TT)
            with dve.Fori(0, B // 2) as pairs:
                pair = pairs * 2
                for par in range(2):
                    b = pair + par
                    dve.wait_ge(norm.normed, START + b * SC)
                    for sc in range(SC):
                        tile = x[:, bass.ds(b * SC + sc, 1)].rearrange("p a f -> p (a f)")
                        if wo is not None:
                            dve.wait_ge(projected, START + b * SC + sc + 1)
                            nc.vector.tensor_tensor(norm.y[:, sc], ps[:, PROJ + sc, 0:D], tile, op=ALU.add)\
                              .then_inc(norm.summed, 1)
                        else:
                            nc.vector.scalar_tensor_tensor(
                                norm.y[:, sc], attended[:, bass.ds(b * SC + sc, 1)].rearrange("p a f -> p (a f)"),
                                blend[:, 0:1], tile, op0=ALU.mult, op1=ALU.add).then_inc(norm.summed, 1)
                        norm.statistics(dve, b, sc)
                    norm.invert(dve, b)
                    if out is None:
                        dve.wait_ge(x_turned, START + b)
                        dve.wait_ge(kept, START + b)
                    else:
                        dve.wait_ge(stored[par], START + pair * 8)
                    for sc in range(SC):
                        norm.apply(fresh[:, par, sc], sc)


E0, FF0, CAP = 16, 512, 64
BE = B * E0
FC0 = FF0 // P


def router_stage(nc, name, x_t, w1, w2, logits):
    with ExitStack() as ctx:
        sb = lambda n, shape, dt=FP32: ctx.enter_context(nc.sbuf_tensor(f"{name}_{n}", shape, dt))
        sem = lambda n: ctx.enter_context(nc.semaphore(f"{name}_{n}"))
        x_sb, w1_sb, w2_sb = sb("x", [P, B, KC, S]), sb("w1", [P, KC, P]), sb("w2", [P, E0])
        hidden, rows = sb("hidden", [P, S]), sb("rows", [E0, B, S])
        ps = ctx.enter_context(nc.psum_tensor(f"{name}_ps", [P, 2, 512], FP32))
        weights_loaded, x_loaded = sem("weights_loaded"), [sem(f"x_loaded{b}") for b in range(B)]
        hidden_ready, hidden_done, logits_ready, logits_done, stored = (
            sem(n) for n in ("hidden_ready", "hidden_done", "logits_ready", "logits_done", "stored"))
        block = ctx.enter_context(nc.Block())

        @block.sync
        def _(sp):
            sp.dma_start(w1_sb[:], w1.rearrange("(k p) f -> p k f", p=P)).then_inc(weights_loaded, 16)
            sp.dma_start(w2_sb[:], w2).then_inc(weights_loaded, 16)
            for b in range(B):
                sp.dma_start(x_sb[:, b], x_t[:, b * S:(b + 1) * S].rearrange("(k p) t -> p k t", p=P))\
                  .then_inc(x_loaded[b], 16)
            sp.wait_ge(logits_done, B)
            sp.dma_start(logits.rearrange("(b e) t -> e b t", b=B), rows[:]).then_inc(stored, 16)
            sp.wait_ge(stored, 16)

        @block.tensor
        def _(pe):
            pe.wait_ge(weights_loaded, 32)
            for b in range(B):
                pe.wait_ge(x_loaded[b], 16)
                pe.wait_ge(hidden_done, b)
                for k in range(KC):
                    last = nc.tensor.matmul(ps[:, 0], w1_sb[:, k], x_sb[:, b, k], start=(k == 0), stop=(k == KC - 1))
                last.then_inc(hidden_ready, 1)
                pe.wait_ge(hidden_done, b + 1)
                pe.wait_ge(logits_done, b)
                nc.tensor.matmul(ps[0:E0, 1], w2_sb[:], hidden[:], start=True, stop=True).then_inc(logits_ready, 1)

        @block.scalar
        def _(act):
            for b in range(B):
                act.wait_ge(hidden_ready, b + 1)
                act.wait_ge(logits_ready, b)
                nc.scalar.activation(hidden[:], ps[:, 0], ACT.Silu).then_inc(hidden_done, 1)

        @block.vector
        def _(dve):
            for b in range(B):
                dve.wait_ge(logits_ready, b + 1)
                nc.vector.tensor_copy(rows[:, b], ps[0:E0, 1]).then_inc(logits_done, 1)


def choice_stage(nc, name, logits, slots, weights, ident):
    with ExitStack() as ctx:
        sb = lambda n, shape, dt=FP32: ctx.enter_context(nc.sbuf_tensor(f"{name}_{n}", shape, dt))
        sem = lambda n: ctx.enter_context(nc.semaphore(f"{name}_{n}"))
        row = lambda n: sb(n, [BE, S])
        rows, probs, left, chosen, counts, zeros, slot_rows, weight_rows = (
            row(n) for n in ("logits", "probs", "left", "chosen", "counts", "zeros", "slot_rows", "weight_rows"))
        shift, total, best, share = sb("shift", [BE, 1]), sb("total", [BE, 1]), sb("best", [BE, 8]), sb("share", [BE, 1])
        ps = ctx.enter_context(nc.psum_tensor(f"{name}_ps", [P, 2, SC, BE], FP32))
        loaded, shift_done, exp_done, step, ready, turned, done = (
            sem(n) for n in ("loaded", "shift_done", "exp_done", "step", "ready", "turned", "done"))
        block = ctx.enter_context(nc.Block())

        @block.sync
        def _(sp):
            sp.dma_start(rows[:], logits).then_inc(loaded, 16)

        @block.scalar
        def _(act):
            act.wait_ge(shift_done, 1)
            nc.scalar.activation(probs[:], rows[:], ACT.Exp, bias=shift[:, 0:1], accum_out=total[:, 0:1])\
              .then_inc(exp_done, 1)

        @block.vector
        def _(dve):
            steps = 0

            def then_wait(instruction):
                nonlocal steps
                steps += 1
                instruction.then_inc(step, 1)
                dve.wait_ge(step, steps)

            nc.vector.memset(zeros[:], 0.0)
            dve.wait_ge(loaded, 16)
            nc.vector.tensor_reduce(shift[:], rows[:], axis=AX.X, op=ALU.max, negate=True).then_inc(shift_done, 1)
            dve.wait_ge(exp_done, 1)
            then_wait(nc.vector.reciprocal(share[:], total[:]))
            then_wait(nc.vector.tensor_scalar_mul(probs[:], probs[:], share[:, 0:1]))
            then_wait(nc.vector.tensor_copy(left[:], probs[:]))
            for _ in range(CAP // 8):
                then_wait(nc.vector.max(best[:], left[:]))
                then_wait(nc.vector.match_replace(left[:], best[:], left[:], -1.0))
            then_wait(nc.vector.tensor_single_scalar(chosen[:], left[:], 0.0, op=ALU.is_lt))
            then_wait(nc.vector.scalar_tensor_tensor(weight_rows[:], left[:], 0.0, probs[:], op0=ALU.is_lt,
                                                     op1=ALU.mult, accum_out=total[:, 0:1]))
            then_wait(nc.vector.tensor_scalar_add(total[:], total[:], 1e-9))
            then_wait(nc.vector.reciprocal(share[:], total[:]))
            then_wait(nc.vector.tensor_scalar_mul(weight_rows[:], weight_rows[:], share[:, 0:1]))
            then_wait(nc.vector.tensor_tensor_scan(counts[:], chosen[:], zeros[:], 0.0, op0=ALU.add, op1=ALU.add))
            then_wait(nc.vector.tensor_tensor(counts[:], counts[:], chosen[:], op=ALU.mult))
            nc.vector.tensor_scalar_add(slot_rows[:], counts[:], -1.0).then_inc(ready, 1)
            dve.wait_ge(turned, 1)
            nc.vector.tensor_copy(slots[:], ps[:, 0]).then_inc(done, 1)
            nc.vector.tensor_copy(weights[:], ps[:, 1]).then_inc(done, 1)
            dve.wait_ge(done, 2)

        @block.tensor
        def _(pe):
            pe.wait_ge(ready, 1)
            for i, source in enumerate((slot_rows, weight_rows)):
                for sc in range(SC):
                    last = nc.tensor.transpose(ps[:, i, sc], source[:, sc * P:(sc + 1) * P], ident[0:BE, 0:BE])
            last.then_inc(turned, 1)


def gather_stage(nc, name, x, slots, numbers, chosen_t):
    with ExitStack() as ctx:
        sb = lambda n, shape, dt=FP32: ctx.enter_context(nc.sbuf_tensor(f"{name}_{n}", shape, dt))
        sem = lambda n: ctx.enter_context(nc.semaphore(f"{name}_{n}"))
        hi, lo = sb("hi", [P, 2, SC, D], F32R), sb("lo", [P, 2, SC, D], F32R)
        places = sb("places", [P, SC, E0, CAP], F32R)
        ps = ctx.enter_context(nc.psum_tensor(f"{name}_ps", [P, 2, KC, 2, 512], FP32))
        HE = E0 // 2
        hi_done, lo_done, places_done, gathered, kept = (
            sem(n) for n in ("hi_done", "lo_done", "places_done", "gathered", "kept"))
        block = ctx.enter_context(nc.Block())

        @block.scalar
        def _(act):
            act.sem_inc(kept, START)
            with act.Fori(0, B // 2) as pairs:
                pair = pairs * 2
                for par in range(2):
                    b = pair + par
                    act.wait_ge(gathered, START + b)
                    nc.scalar.activation(hi[:, par], x[:, bass.ds(b * SC, SC)], ACT.Copy).then_inc(hi_done, 1)
                    act.wait_ge(gathered, START + b + 1)
                    for k in range(KC):
                        for half in range(2):
                            nc.scalar.activation(
                                chosen_t[:, k, half * HE:(half + 1) * HE, bass.ds(b * CAP, CAP)],
                                ps[:, par, k, half].rearrange("p (e c) -> p e c", c=CAP), ACT.Copy).then_inc(kept, 1)

        @block.vector
        def _(dve):
            with dve.Fori(0, B // 2) as pairs:
                pair = pairs * 2
                for par in range(2):
                    b = pair + par
                    dve.wait_ge(gathered, START + b)
                    for sc in range(SC):
                        nc.vector.tensor_tensor(
                            places[:, sc], numbers[:].unsqueeze(1).to_broadcast([P, E0, CAP]),
                            slots[:, sc, bass.ds(b * E0, E0)].unsqueeze(2).to_broadcast([P, E0, CAP]),
                            op=ALU.is_equal).then_inc(places_done, 1)
                    dve.wait_ge(hi_done, b + 1)
                    nc.vector.tensor_tensor(lo[:, par], x[:, bass.ds(b * SC, SC)], hi[:, par].bitcast(FP32),
                                            op=ALU.subtract).then_inc(lo_done, 1)

        @block.tensor
        def _(pe):
            pe.sem_inc(gathered, START)
            with pe.Fori(0, B // 2) as pairs:
                pair = pairs * 2
                for par in range(2):
                    b = pair + par
                    pe.wait_ge(places_done, b * SC + SC)
                    pe.wait_ge(lo_done, b + 1)
                    pe.wait_ge(kept, START + b * (KC * 2))
                    for k in range(KC):
                        for half in range(2):
                            for sc in range(SC):
                                for part in (hi, lo):
                                    last = nc.tensor.matmul(
                                        ps[:, par, k, half], part[:, par, sc, k * P:(k + 1) * P],
                                        places[:, sc, half * HE:(half + 1) * HE],
                                        start=(sc == 0 and part is hi), stop=(sc == SC - 1 and part is lo))
                    last.then_inc(gathered, 1)


def expert_stage(nc, name, chosen_t, w1, w2, w3, made):
    N = B * CAP
    with ExitStack() as ctx:
        sb = lambda n, shape, dt=FP32: ctx.enter_context(nc.sbuf_tensor(f"{name}_{n}", shape, dt))
        sem = lambda n: ctx.enter_context(nc.semaphore(f"{name}_{n}"))
        w1_sb, w2_sb = sb("w1", [P, 2, KC, FF0]), sb("w2", [P, 2, KC, FF0])
        w3_sb = sb("w3", [P, 2, FC0, D])
        gate, act_t = sb("gate", [P, 2, 2, N]), sb("act_t", [P, 2, FC0, N])
        ps = ctx.enter_context(nc.psum_tensor(f"{name}_ps", [P, 8, 512], FP32))
        OUT = 4
        up_loaded, down_loaded = [sem("up_loaded0"), sem("up_loaded1")], [sem("down_loaded0"), sem("down_loaded1")]
        up_ready, gate_done, act_done, made_ready, kept = (
            sem(n) for n in ("up_ready", "gate_done", "act_done", "made_ready", "kept"))
        block = ctx.enter_context(nc.Block())

        @block.sync
        def _(sp):
            def load(e2, j):
                e = e2 * 2 + j
                row = lambda w: w[bass.ds(e, 1)].rearrange("a (k p) f -> p (a k) f", p=P)
                sp.dma_start(w1_sb[:, j], row(w1)).then_inc(up_loaded[j], 16)
                sp.dma_start(w2_sb[:, j], row(w2)).then_inc(up_loaded[j], 16)
                sp.dma_start(w3_sb[:, j], row(w3)).then_inc(down_loaded[j], 16)

            load(0, 0)
            load(0, 1)
            with sp.Fori(1, E0 // 2) as e2:
                for j in range(2):
                    sp.wait_ge(made_ready, START + e2)
                    load(e2, j)

        @block.tensor
        def _(pe):
            pe.sem_inc(made_ready, START)
            with pe.Fori(0, E0 // 2) as e2:
                for j in range(2):
                    pe.wait_ge(up_loaded[j], e2 * 32 + 32)
                    for f2 in range(FC0 // 2):
                        pe.wait_ge(act_done, e2 * 4 + (2 * j + f2 + 1))
                        for which, w in enumerate((w1_sb, w2_sb)):
                            for f in range(2):
                                for k in range(KC):
                                    fc = 2 * f2 + f
                                    last = nc.tensor.matmul(
                                        ps[:, 2 * f2 + which, f * N:(f + 1) * N], w[:, j, k, fc * P:(fc + 1) * P],
                                        chosen_t[:, k, bass.ds(e2 * 2 + j, 1)].rearrange("p a n -> p (a n)"),
                                        start=(k == 0), stop=(k == KC - 1))
                            last.then_inc(up_ready, 1)
                pe.wait_ge(kept, START + e2)
                for j in range(2):
                    pe.wait_ge(down_loaded[j], e2 * 16 + 16)
                    for fc in range(FC0):
                        if fc % 2 == 0:
                            pe.wait_ge(act_done, e2 * 4 + (2 * j + fc // 2 + 3))
                        for b in range(B):
                            last = nc.tensor.matmul(ps[CAP * j:CAP * (j + 1), OUT + b, 0:D],
                                                    act_t[:, j, fc, b * CAP:(b + 1) * CAP], w3_sb[:, j, fc],
                                                    start=(fc == 0), stop=(fc == FC0 - 1))
                last.then_inc(made_ready, 1)

        @block.scalar
        def _(act):
            act.sem_inc(kept, START)
            with act.Fori(0, E0 // 2) as e2:
                for u in range(4):
                    act.wait_ge(up_ready, e2 * 8 + (2 * u + 1))
                    act.wait_ge(act_done, e2 * 4 + (u + 1))
                    nc.scalar.activation(gate[:, u % 2], ps[:, 2 * (u % 2)].rearrange("p (f n) -> p f n", f=2),
                                         ACT.Silu).then_inc(gate_done, 1)
                act.wait_ge(made_ready, START + e2 + 1)
                nc.scalar.activation(made[:, bass.ds(e2, 1)].rearrange("p a b d -> p (a b) d"),
                                     ps[:, OUT:OUT + B, 0:D], ACT.Copy).then_inc(kept, 1)

        @block.vector
        def _(dve):
            dve.sem_inc(act_done, 2)
            with dve.Fori(0, E0 // 2) as e2:
                dve.wait_ge(made_ready, START + e2)
                for u in range(4):
                    dve.wait_ge(gate_done, e2 * 4 + (u + 1))
                    dve.wait_ge(up_ready, e2 * 8 + (2 * u + 2))
                    nc.vector.tensor_tensor(act_t[:, u // 2, 2 * (u % 2):2 * (u % 2) + 2],
                                            ps[:, 2 * (u % 2) + 1].rearrange("p (f n) -> p f n", f=2),
                                            gate[:, u % 2], op=ALU.mult).then_inc(act_done, 1)


def combine_stage(nc, name, x, x_t, ident, slots, weights, numbers, made):
    with ExitStack() as ctx:
        sb = lambda n, shape, dt=FP32: ctx.enter_context(nc.sbuf_tensor(f"{name}_{n}", shape, dt))
        sem = lambda n: ctx.enter_context(nc.semaphore(f"{name}_{n}"))
        norm = Norm(ctx, nc, f"{name}_norm")
        fresh, turned = sb("fresh", [P, SC, D]), sb("turned", [P, KC, S])
        places = sb("places", [P, 2, E0, CAP])
        places_t = sb("places_t", [P, 2, E0 // 2, P])
        ps = ctx.enter_context(nc.psum_tensor(f"{name}_ps", [P, 8, 512], FP32))
        TURN, PLACES, OUT = 0, 2, 6
        equal_done, weighted, places_turned, places_kept, summed_up = (
            sem(n) for n in ("equal_done", "weighted", "places_turned", "places_kept", "summed_up"))
        kept, x_turned, turned_done, stored = (sem(n) for n in ("kept", "x_turned", "turned_done", "stored"))
        block = ctx.enter_context(nc.Block())
        tile_of = lambda ap, i: ap[:, bass.ds(i, 1)].rearrange("p a f -> p (a f)")

        @block.sync
        def _(sp):
            sp.sem_inc(stored, START)
            for b in range(B):
                sp.wait_ge(turned_done, START + b + 1)
                sp.dma_start(x_t[:, b * S:(b + 1) * S].rearrange("(k p) t -> p k t", p=P), turned[:])\
                  .then_inc(stored, 16)
            sp.wait_ge(stored, START + 16 * B)

        @block.gpsimd
        def _(pool):
            pool.sem_inc(kept, START)
            nc.gpsimd.memset(norm.eps[:], LN_EPS).then_inc(norm.eps_ready, 1)
            with pool.Fori(0, B) as b:
                for sc in range(SC):
                    n = b * SC + sc
                    pool.wait_ge(equal_done, n + 1)
                    nc.gpsimd.tensor_tensor(places[:, sc % 2], places[:, sc % 2],
                                            weights[:, sc, bass.ds(b * E0, E0)].unsqueeze(2).to_broadcast([P, E0, CAP]),
                                            op=ALU.mult).then_inc(weighted, 1)
                pool.wait_ge(norm.normed, START + b * SC + SC)
                nc.gpsimd.tensor_copy(x[:, bass.ds(b * SC, SC)], fresh[:]).then_inc(kept, 1)

        @block.tensor
        def _(pe):
            pe.sem_inc(places_turned, START)
            pe.sem_inc(summed_up, START)
            pe.sem_inc(x_turned, START)
            with pe.Fori(0, B) as b:
                for sc in range(SC):
                    n = b * SC + sc
                    pe.wait_ge(weighted, n + 1)
                    pe.wait_ge(places_kept, START + n)
                    for e2 in range(E0 // 2):
                        last = nc.tensor.transpose(
                            ps[:, PLACES + 2 * (sc % 2) + e2 // 4, e2 % 4 * P:(e2 % 4 + 1) * P],
                            places[:, sc % 2, 2 * e2:2 * e2 + 2].rearrange("p e c -> p (e c)"), ident[:])
                    last.then_inc(places_turned, 1)
                    pe.wait_ge(places_kept, START + n + 1)
                    pe.wait_ge(norm.summed, START + n)
                    for e2 in range(E0 // 2):
                        last = nc.tensor.matmul(ps[:, OUT + sc % 2, 0:D], places_t[:, sc % 2, e2],
                                                made[:, e2, bass.ds(b, 1)].rearrange("p a d -> p (a d)"),
                                                start=(e2 == 0), stop=(e2 == E0 // 2 - 1))
                    last.then_inc(summed_up, 1)
                pe.wait_ge(norm.normed, START + b * SC + SC)
                pe.wait_ge(turned_done, START + b)
                for sc in range(SC):
                    for k in range(KC):
                        last = nc.tensor.transpose(ps[:, TURN + k, sc * P:(sc + 1) * P],
                                                   fresh[:, sc, k * P:(k + 1) * P], ident[:])
                last.then_inc(x_turned, 1)

        @block.scalar
        def _(act):
            act.sem_inc(places_kept, START)
            act.sem_inc(turned_done, START)
            with act.Fori(0, B) as b:
                for sc in range(SC):
                    n = b * SC + sc
                    act.wait_ge(places_turned, START + n + 1)
                    act.wait_ge(summed_up, START + n)
                    nc.scalar.activation(places_t[:, sc % 2].rearrange("p (a e) t -> p a (e t)", a=2),
                                         ps[:, PLACES + 2 * (sc % 2):PLACES + 2 * (sc % 2) + 2], ACT.Copy)\
                      .then_inc(places_kept, 1)
                norm.root(act, b)
                act.wait_ge(x_turned, START + b + 1)
                act.wait_ge(stored, START + b * 16)
                nc.scalar.activation(turned[:], ps[:, TURN:TURN + KC], ACT.Copy).then_inc(turned_done, 1)

        @block.vector
        def _(dve):
            dve.sem_inc(norm.normed, START)
            dve.sem_inc(norm.summed, START)
            def equal(n, b, sc):
                nc.vector.tensor_tensor(
                    places[:, sc % 2], numbers[:].unsqueeze(1).to_broadcast([P, E0, CAP]),
                    slots[:, sc, bass.ds(b * E0, E0)].unsqueeze(2).to_broadcast([P, E0, CAP]),
                    op=ALU.is_equal).then_inc(equal_done, 1)

            with dve.Fori(0, B) as b:
                dve.wait_ge(norm.normed, START + b * SC)
                for sc in range(SC):
                    n = b * SC + sc
                    if sc < 2:
                        if sc == 0:
                            dve.wait_ge(places_turned, START + b * SC)
                        equal(n, b, sc)
                for sc in range(SC):
                    n = b * SC + sc
                    if sc + 2 < SC:
                        dve.wait_ge(places_turned, START + n + 1)
                        equal(n + 2, b, sc + 2)
                    dve.wait_ge(summed_up, START + n + 1)
                    nc.vector.tensor_tensor(norm.y[:, sc], ps[:, OUT + sc % 2, 0:D], tile_of(x, n), op=ALU.add)\
                      .then_inc(norm.summed, 1)
                    norm.statistics(dve, b, sc)
                norm.invert(dve, b)
                dve.wait_ge(x_turned, START + b)
                dve.wait_ge(kept, START + b)
                for sc in range(SC):
                    norm.apply(fresh[:, sc], sc)


def time_mix_stage(nc, name, x_t, y_t, w, mix, decay, first):
    with ExitStack() as ctx:
        sb = lambda n, shape, dt=FP32: ctx.enter_context(nc.sbuf_tensor(f"{name}_{n}", shape, dt))
        sem = lambda n: ctx.enter_context(nc.semaphore(f"{name}_{n}"))
        x_sb = sb("x", [P, 2, KC, S + 1])
        mixed, before = sb("mixed", [P, 2, KC, S]), sb("before", [P, KC, S])
        w_sb = sb("w", [P, 3, KC, D])
        mix_sb, unmix = sb("mix", [P, KC]), sb("unmix", [P, KC])
        rate, now = sb("rate", [P, KC]), sb("now", [P, KC])
        rates = sb("rates", [P, KC, S])
        k_sb, kv_sb = sb("k", [P, KC, S]), sb("kv", [P, KC, S])
        past_k, past_kv = sb("past_k", [P, KC, S + 1]), sb("past_kv", [P, KC, S + 1])
        below, above, receptance = sb("below", [P, KC, S]), sb("above", [P, KC, S]), sb("receptance", [P, KC, S])
        y = sb("y", [P, 2, KC, S])
        ps = ctx.enter_context(nc.psum_tensor(f"{name}_ps", [P, 8, 512], FP32))
        loaded, x_loaded, consts = sem("loaded"), [sem("x_loaded0"), sem("x_loaded1")], sem("consts")
        mixed_seen = sem("mixed_seen")
        acts, scaled, mixed_done, projected = sem("acts"), sem("scaled"), sem("mixed_done"), sem("projected")
        low_done, k_done, receptance_done, link, y_done = (sem(n) for n in ("low_done", "k_done", "receptance_done", "link", "y_done"))
        kv_done, inverted, stored = sem("kv_done"), sem("inverted"), [sem("stored0"), sem("stored1")]
        block = ctx.enter_context(nc.Block())

        @block.sync
        def _(sp):
            for semaphore in stored:
                sp.sem_inc(semaphore, START)
            def load_x(b):
                sp.dma_start(x_sb[:, b % 2, :, 1:S + 1], x_t[:, b * S:(b + 1) * S].rearrange("(k p) t -> p k t", p=P))\
                  .then_inc(x_loaded[b % 2], 16)

            load_x(0)
            for tile, source in ((mix_sb, mix), (rate, decay), (now, first)):
                sp.dma_start(tile[:], source).then_inc(loaded, 16)
            for i in range(3):
                sp.dma_start(w_sb[:, i], w[i].rearrange("(k p) f -> p k f", p=P)).then_inc(loaded, 16)
            load_x(1)
            for b in range(B):
                if b + 2 < B:
                    sp.wait_ge(mixed_done, (b + 1) * KC)
                    load_x(b + 2)
                sp.wait_ge(y_done, START + (b + 1) * KC)
                sp.dma_start(y_t[:, b * S:(b + 1) * S].rearrange("(k p) t -> p k t", p=P), y[:, b % 2])\
                  .then_inc(stored[b % 2], 16)
            for slot in range(2):
                sp.wait_ge(stored[slot], START + 16 * (B // 2))

        @block.gpsimd
        def _(pool):
            nc.gpsimd.memset(x_sb[:, :, :, 0:1], 0.0).then_inc(consts, 1)
            nc.gpsimd.memset(past_k[:, :, 0:1], 0.0).then_inc(consts, 1)
            nc.gpsimd.memset(past_kv[:, :, 0:1], 0.0).then_inc(consts, 1)
            pool.wait_ge(consts, 5)
            with pool.Fori(0, B // 2) as pairs:
                pair = pairs * 2
                for par in range(2):
                    b = pair + par
                    pool.wait_ge(x_loaded[par], pair * 8 + 16)
                    pool.wait_ge(projected, START + b * (3 * KC))
                    pool.sem_inc(mixed_seen, 1)
                    for k in range(KC):
                        nc.gpsimd.tensor_scalar_mul(mixed[:, par, k], x_sb[:, par, k, 1:S + 1], mix_sb[:, k:k + 1])\
                          .then_inc(scaled, 1)
                        nc.gpsimd.tensor_scalar_mul(before[:, k], x_sb[:, par, k, 0:S], unmix[:, k:k + 1])\
                          .then_inc(scaled, 1)
                    for k in range(KC):
                        pool.wait_ge(scaled, b * (2 * KC) + 2 * k + 2)
                        nc.gpsimd.tensor_tensor(mixed[:, par, k], mixed[:, par, k], before[:, k], op=ALU.add)\
                          .then_inc(mixed_done, 1)

        @block.scalar
        def _(act):
            act.sem_inc(receptance_done, START)
            act.wait_ge(loaded, 96)
            nc.scalar.activation(rate[:], rate[:], ACT.Exp).then_inc(acts, 1)
            nc.scalar.activation(now[:], now[:], ACT.Exp).then_inc(acts, 1)
            act.wait_ge(acts, 2)
            nc.scalar.activation(rate[:], rate[:], ACT.Exp, scale=-1.0).then_inc(acts, 1)
            with act.Fori(0, B) as b:
                for m in range(KC):
                    act.wait_ge(low_done, START + b * KC + m + 1)
                    nc.scalar.activation(k_sb[:, m], k_sb[:, m], ACT.Exp).then_inc(k_done, 1)
                for m in range(KC):
                    act.wait_ge(projected, START + b * (3 * KC) + 3 * m + 3)
                    act.wait_ge(y_done, START + b * KC)
                    nc.scalar.activation(receptance[:, m], ps[:, 3 * m + 2], ACT.Sigmoid).then_inc(receptance_done, 1)

        @block.tensor
        def _(pe):
            pe.sem_inc(projected, START)
            pe.wait_ge(loaded, 96)
            with pe.Fori(0, B // 2) as pairs:
                pair = pairs * 2
                for par in range(2):
                    b = pair + par
                    pe.wait_ge(mixed_done, b * KC + KC)
                    pe.wait_ge(low_done, START + b * KC)
                    pe.wait_ge(kv_done, START + b * KC)
                    pe.wait_ge(receptance_done, START + b * KC)
                    for m in range(KC):
                        for i in range(3):
                            for k in range(KC):
                                last = nc.tensor.matmul(ps[:, 3 * m + i], w_sb[:, i, k, m * P:(m + 1) * P],
                                                        mixed[:, par, k], start=(k == 0), stop=(k == KC - 1))
                            last.then_inc(projected, 1)

        @block.vector
        def _(dve):
            dve.sem_inc(kv_done, START)
            dve.sem_inc(low_done, START)
            dve.sem_inc(y_done, START)
            dve.wait_ge(acts, 3)
            nc.vector.tensor_scalar(unmix[:], mix_sb[:], -1.0, 1.0, op0=ALU.mult, op1=ALU.add).then_inc(consts, 1)
            nc.vector.memset(rates[:], 1.0).then_inc(consts, 1)
            dve.wait_ge(consts, 5)
            for m in range(KC):
                nc.vector.tensor_scalar_mul(rates[:, m], rates[:, m], rate[:, m:m + 1]).then_inc(consts, 1)
            dve.wait_ge(consts, 5 + KC)
            LINKS = 6
            with dve.Fori(0, B // 2) as pairs:
                pair = pairs * 2
                for par in range(2):
                    b = pair + par
                    dve.wait_ge(y_done, START + b * KC)
                    for m in range(KC):
                        dve.wait_ge(projected, START + b * (3 * KC) + 3 * m + 1)
                        nc.vector.tensor_scalar_min(k_sb[:, m], ps[:, 3 * m], 60.0).then_inc(low_done, 1)
                    for m in range(KC):
                        n = b * KC + m
                        dve.wait_ge(projected, START + b * (3 * KC) + 3 * m + 2)
                        dve.wait_ge(k_done, n + 1)
                        nc.vector.tensor_tensor(kv_sb[:, m], ps[:, 3 * m + 1], k_sb[:, m], op=ALU.mult).then_inc(kv_done, 1)
                        nc.vector.tensor_tensor_scan(past_k[:, m, 1:S + 1], rates[:, m], k_sb[:, m], 0.0,
                                                     op0=ALU.mult, op1=ALU.add).then_inc(link, 1)
                        dve.wait_ge(kv_done, START + n + 1)
                        nc.vector.tensor_tensor_scan(past_kv[:, m, 1:S + 1], rates[:, m], kv_sb[:, m], 0.0,
                                                     op0=ALU.mult, op1=ALU.add).then_inc(link, 1)
                        dve.wait_ge(link, n * LINKS + 1)
                        nc.vector.scalar_tensor_tensor(below[:, m], k_sb[:, m], now[:, m:m + 1], past_k[:, m, 0:S],
                                                       op0=ALU.mult, op1=ALU.add).then_inc(link, 1)
                        dve.wait_ge(link, n * LINKS + 2)
                        nc.vector.scalar_tensor_tensor(above[:, m], kv_sb[:, m], now[:, m:m + 1], past_kv[:, m, 0:S],
                                                       op0=ALU.mult, op1=ALU.add).then_inc(link, 1)
                        dve.wait_ge(link, n * LINKS + 3)
                        nc.vector.tensor_scalar_add(below[:, m], below[:, m], 1e-9).then_inc(link, 1)
                        dve.wait_ge(receptance_done, START + n + 1)
                        dve.wait_ge(link, n * LINKS + 4)
                        nc.vector.tensor_tensor(above[:, m], above[:, m], receptance[:, m], op=ALU.mult).then_inc(link, 1)
                        dve.wait_ge(link, n * LINKS + 5)
                        nc.vector.reciprocal(below[:, m], below[:, m]).then_inc(inverted, 1)
                        dve.wait_ge(link, n * LINKS + 6)
                        dve.wait_ge(inverted, n + 1)
                        if m == 0:
                            dve.wait_ge(stored[par], START + pair * 8)
                        nc.vector.tensor_tensor(y[:, par, m], above[:, m], below[:, m], op=ALU.mult).then_inc(y_done, 1)


E1, FF1 = 8, 1024
FC1 = FF1 // P


def gate_stage(nc, name, x_t, gate_w, order, share):
    with ExitStack() as ctx:
        sb = lambda n, shape, dt=FP32: ctx.enter_context(nc.sbuf_tensor(f"{name}_{n}", shape, dt))
        sem = lambda n: ctx.enter_context(nc.semaphore(f"{name}_{n}"))
        x_sb, w_sb, order_sb = sb("x", [P, B, KC, S]), sb("w", [P, KC, E1]), sb("order", [P, E1])
        probs, key, first, second = (sb(n, [P, TT, E1]) for n in ("probs", "key", "first", "second"))
        best, best2, rank, total = (sb(n, [P, TT]) for n in ("best", "best2", "rank", "total"))
        ps = ctx.enter_context(nc.psum_tensor(f"{name}_ps", [P, TT, E1], FP32))
        loaded, x_loaded = sem("loaded"), [sem(f"x_loaded{b}") for b in range(B)]
        logits_ready, centred, exp_done, step = (sem(n) for n in ("logits_ready", "centred", "exp_done", "step"))
        block = ctx.enter_context(nc.Block())
        spread = lambda ap: ap[:].unsqueeze(2).to_broadcast([P, TT, E1])

        @block.sync
        def _(sp):
            sp.dma_start(w_sb[:], gate_w.rearrange("(k p) f -> p k f", p=P)).then_inc(loaded, 16)
            sp.dma_start(order_sb[:], order).then_inc(loaded, 16)
            for b in range(B):
                sp.dma_start(x_sb[:, b], x_t[:, b * S:(b + 1) * S].rearrange("(k p) t -> p k t", p=P))\
                  .then_inc(x_loaded[b], 16)

        @block.tensor
        def _(pe):
            pe.wait_ge(loaded, 32)
            for b in range(B):
                pe.wait_ge(x_loaded[b], 16)
                for sc in range(SC):
                    for k in range(KC):
                        last = nc.tensor.matmul(ps[:, b * SC + sc], x_sb[:, b, k, sc * P:(sc + 1) * P], w_sb[:, k],
                                                start=(k == 0), stop=(k == KC - 1))
            last.then_inc(logits_ready, 1)

        @block.scalar
        def _(act):
            act.wait_ge(centred, 1)
            nc.scalar.activation(probs[:], probs[:], ACT.Exp).then_inc(exp_done, 1)

        @block.vector
        def _(dve):
            steps = 0

            def then_wait(instruction):
                nonlocal steps
                steps += 1
                instruction.then_inc(step, 1)
                dve.wait_ge(step, steps)

            def pick(chosen, top):
                then_wait(nc.vector.tensor_reduce(top[:], probs[:], axis=AX.X, op=ALU.max))
                then_wait(nc.vector.tensor_tensor(key[:], probs[:], spread(top), op=ALU.is_equal))
                then_wait(nc.vector.tensor_tensor(key[:], key[:], order_sb[:].unsqueeze(1).to_broadcast([P, TT, E1]),
                                                  op=ALU.mult))
                then_wait(nc.vector.tensor_reduce(rank[:], key[:], axis=AX.X, op=ALU.max))
                then_wait(nc.vector.tensor_tensor(chosen[:], key[:], spread(rank), op=ALU.is_equal))

            dve.wait_ge(logits_ready, 1)
            then_wait(nc.vector.tensor_reduce(best[:], ps[:], axis=AX.X, op=ALU.max))
            nc.vector.tensor_tensor(probs[:], ps[:], spread(best), op=ALU.subtract).then_inc(centred, 1)
            dve.wait_ge(exp_done, 1)
            then_wait(nc.vector.tensor_reduce(total[:], probs[:], axis=AX.X, op=ALU.add))
            then_wait(nc.vector.reciprocal(total[:], total[:]))
            then_wait(nc.vector.tensor_tensor(probs[:], probs[:], spread(total), op=ALU.mult))
            pick(first, best)
            then_wait(nc.vector.scalar_tensor_tensor(probs[:], first[:], -2.0, probs[:], op0=ALU.mult, op1=ALU.add))
            pick(second, best2)
            then_wait(nc.vector.tensor_tensor(total[:], best[:], best2[:], op=ALU.add))
            then_wait(nc.vector.reciprocal(total[:], total[:]))
            then_wait(nc.vector.tensor_tensor(first[:], first[:], spread(best), op=ALU.mult))
            then_wait(nc.vector.tensor_tensor(second[:], second[:], spread(best2), op=ALU.mult))
            then_wait(nc.vector.tensor_tensor(first[:], first[:], second[:], op=ALU.add))
            then_wait(nc.vector.tensor_tensor(share[:], first[:], spread(total), op=ALU.mult))


def mixture_stage(nc, name, x_t, up_w, down_w, share, total):
    with ExitStack() as ctx:
        sb = lambda n, shape, dt=FP32: ctx.enter_context(nc.sbuf_tensor(f"{name}_{n}", shape, dt))
        sem = lambda n: ctx.enter_context(nc.semaphore(f"{name}_{n}"))
        x_hi, x_lo = sb("x_hi", [P, KC, T], F32R), sb("x_lo", [P, KC, T], F32R)
        up_raw, down_sb = sb("up_raw", [P, KC, 2 * FF1]), sb("down", [P, 2, FC1, D])
        up_hi, up_lo = sb("up_hi", [P, 2, KC, 2 * FF1], F32R), sb("up_lo", [P, 2, KC, 2 * FF1], F32R)
        gate, act_t = sb("gate", [P, 2, S]), sb("act_t", [P, FC1, S])
        x_raw = act_t[:].rearrange("p (k c) s -> p k (c s)", k=KC)
        ps = ctx.enter_context(nc.psum_tensor(f"{name}_ps", [P, 8, 512], FP32))
        OUT = 4
        x_loaded, zeroed, weights_seen = sem("x_loaded"), sem("zeroed"), sem("weights_seen")
        up_loaded, down_loaded = sem("up_loaded"), [sem("down_loaded0"), sem("down_loaded1")]
        x_high, x_split, up_high, up_split, raw_seen = (
            sem(n) for n in ("x_high", "x_split", "up_high", "up_split", "raw_seen"))
        up_ready, gate_done, act_done, down_ready, added = (
            sem(n) for n in ("up_ready", "gate_done", "act_done", "down_ready", "added"))
        block = ctx.enter_context(nc.Block())

        @block.sync
        def _(sp):
            row = lambda w, e: w[bass.ds(e, 1)].rearrange("a (k p) f -> p (a k) f", p=P)
            sp.dma_start(x_raw, x_t.rearrange("(k p) t -> p k t", p=P)).then_inc(x_loaded, 16)
            sp.dma_start(up_raw[:], row(up_w, 0)).then_inc(up_loaded, 16)
            for e in range(2):
                sp.dma_start(down_sb[:, e], row(down_w, e)).then_inc(down_loaded[e], 16)
            sp.wait_ge(up_split, KC)
            sp.dma_start(up_raw[:], row(up_w, 1)).then_inc(up_loaded, 16)
            with sp.Fori(1, E1 // 2) as e2:
                for j in range(2):
                    e = e2 * 2 + j
                    sp.wait_ge(up_split, e2 * (2 * KC) + j * KC)
                    sp.dma_start(up_raw[:], row(up_w, e)).then_inc(up_loaded, 16)
                    sp.wait_ge(down_ready, START + (e2 - 1) * (2 * B) + B * (j + 1))
                    sp.dma_start(down_sb[:, j], row(down_w, e)).then_inc(down_loaded[j], 16)

        @block.gpsimd
        def _(pool):
            def split(j, high_before):
                for k in range(KC):
                    nc.gpsimd.tensor_copy(up_hi[:, j, k], up_raw[:, k]).then_inc(up_high, 1)
                pool.wait_ge(up_high, high_before + KC)
                pool.sem_inc(raw_seen, 1)
                for k in range(KC):
                    nc.gpsimd.tensor_tensor(up_lo[:, j, k], up_raw[:, k], up_hi[:, j, k].bitcast(FP32),
                                            op=ALU.subtract).then_inc(up_split, 1)

            pool.wait_ge(up_loaded, 32)
            split(1, KC)
            with pool.Fori(1, E1 // 2) as e2:
                for j in range(2):
                    pool.wait_ge(up_loaded, e2 * 32 + 16 * (j + 1))
                    pool.wait_ge(down_ready, START + (e2 - 1) * (2 * B) + B * (j + 1))
                    pool.sem_inc(raw_seen, 1)
                    split(j, e2 * (2 * KC) + j * KC)

        @block.tensor
        def _(pe):
            pe.sem_inc(down_ready, START)
            pe.wait_ge(x_split, KC)
            with pe.Fori(0, E1 // 2) as e2:
                for j in range(2):
                    pe.wait_ge(up_split, e2 * (2 * KC) + KC * (j + 1))
                    pe.wait_ge(down_loaded[j], e2 * 16 + 16)
                    pe.sem_inc(weights_seen, 1)
                    with pe.Fori(0, B) as b:
                        n = e2 * (2 * B) + j * B + b
                        for f in range(FC1):
                            pe.wait_ge(act_done, n * FC1 + (f + 1))
                            for which in range(2):
                                col = which * FF1 + f * P
                                products = [(up_hi, x_hi, k) for k in range(KC)] + [(up_hi, x_lo, k) for k in range(KC)]
                                products += [(up_lo, x_hi, k) for k in range(KC)]
                                for i, (w_part, x_part, k) in enumerate(products):
                                    last = nc.tensor.matmul(ps[:, 2 * (f % 2) + which], w_part[:, j, k, col:col + P],
                                                            x_part[:, k, bass.ds(b * S, S)],
                                                            start=(i == 0), stop=(i == len(products) - 1))
                                last.then_inc(up_ready, 1)
                        pe.wait_ge(added, START + n)
                        for f in range(FC1):
                            pe.wait_ge(act_done, n * FC1 + (f + 3))
                            for sc in range(SC):
                                last = nc.tensor.matmul(ps[:, OUT + sc, 0:D], act_t[:, f, sc * P:(sc + 1) * P],
                                                        down_sb[:, j, f], start=(f == 0), stop=(f == FC1 - 1))
                        last.then_inc(down_ready, 1)

        @block.scalar
        def _(act):
            with act.Fori(0, E1 * B) as n:
                for f in range(FC1):
                    act.wait_ge(up_ready, n * (2 * FC1) + (2 * f + 1))
                    act.wait_ge(act_done, n * FC1 + (f + 1))
                    nc.scalar.activation(gate[:, f % 2], ps[:, 2 * (f % 2)], ACT.Gelu).then_inc(gate_done, 1)

        @block.vector
        def _(dve):
            dve.sem_inc(added, START)
            dve.sem_inc(act_done, 2)
            nc.vector.memset(total[:], 0.0).then_inc(zeroed, 1)
            for raw, hi, lo, loaded, high, split in ((x_raw, x_hi[:], x_lo[:], x_loaded, x_high, x_split),
                                                     (up_raw[:], up_hi[:, 0], up_lo[:, 0], up_loaded, up_high, up_split)):
                dve.wait_ge(loaded, 16)
                for k in range(KC):
                    nc.vector.tensor_copy(hi[:, k], raw[:, k]).then_inc(high, 1)
                dve.wait_ge(high, KC)
                for k in range(KC):
                    nc.vector.tensor_tensor(lo[:, k], raw[:, k], hi[:, k].bitcast(FP32), op=ALU.subtract).then_inc(split, 1)
            dve.wait_ge(zeroed, 1)
            dve.wait_ge(x_split, KC)
            with dve.Fori(0, E1) as e:
                with dve.Fori(0, B) as b:
                    n = e * B + b
                    dve.wait_ge(down_ready, START + n)
                    for f in range(FC1):
                        dve.wait_ge(gate_done, n * FC1 + (f + 1))
                        dve.wait_ge(up_ready, n * (2 * FC1) + (2 * f + 2))
                        nc.vector.tensor_tensor(act_t[:, f], ps[:, 2 * (f % 2) + 1], gate[:, f % 2], op=ALU.mult)\
                          .then_inc(act_done, 1)
                    dve.wait_ge(down_ready, START + n + 1)
                    for sc in range(SC):
                        tile = total[:, bass.ds(b * SC + sc, 1)].rearrange("p a f -> p (a f)")
                        own = share[:, bass.ds(b * SC + sc, 1), bass.ds(e, 1)].rearrange("p a f -> p (a f)")
                        last = nc.vector.scalar_tensor_tensor(tile, ps[:, OUT + sc, 0:D], own, tile,
                                                              op0=ALU.mult, op1=ALU.add)
                    last.then_inc(added, 1)


def decoder(nc, a, out, upto=99):
    scratch = lambda n, shape, dt=FP32: nc.dram_tensor(n, shape, dt, kind="Internal").ap()
    x_t = [scratch(f"x_t{i}", [D, T]) for i in range(6)]
    q_parts = scratch("q_parts", [2, D, T])
    k_parts = scratch("k_parts", [2, D, T])
    with ExitStack() as ctx:
        sb = lambda n, shape, dt=FP32: ctx.enter_context(nc.sbuf_tensor(n, shape, dt))
        x = sb("x", [P, TT, D])
        ident = sb("ident", [P, P])
        ones_w = sb("gates", [P, 2])
        start_stage(nc, a, x, ident, ones_w)
        with ExitStack() as att_ctx:
            attended = att_ctx.enter_context(nc.sbuf_tensor("attended", [P, TT, D], FP32))
            v_sb = att_ctx.enter_context(nc.sbuf_tensor("v_sb", [P, TT, D], FP32))
            half = D // 2
            v_half = v_sb[:, 0:TT // 2].rearrange("p t (a f) -> p (t a) f", a=2)
            heads_stage(nc, "l0q", a["x_t"], q_parts, a["L0_attn_Wq"], D)
            heads_stage(nc, "l0k", a["x_t"], k_parts[:, 0:half], a["L0_attn_Wk"], half, v=(a["L0_attn_Wv"], None, v_half))
            memory_stage(nc, "l0m", q_parts, x, a["L0_attn_memory"], a["L0_attn_memory_norm"], ones_w)
            attention_stage(nc, "l0a", q_parts, k_parts[:, 0:half], v_half, attended, 2, ident)
            after_stage(nc, "l0n", x, x_t[0], ident, attended, blend=ones_w[:, 1:2])
            if upto <= 1: return
            heads_stage(nc, "x0q", x_t[0], q_parts, a["L0_xattn_Wq"], D, bias=a["L0_xattn_bq"],
                        rope=(a["L0_xattn_Wq_swapped"], a["L0_xattn_bq_swapped"], a["cos"], a["sin"]))
            heads_stage(nc, "x0k", a["ctx_t"], k_parts, a["L0_xattn_Wk"], D, bias=a["L0_xattn_bk"],
                        rope=(a["L0_xattn_Wk_swapped"], a["L0_xattn_bk_swapped"], a["cos"], a["sin"]),
                        v=(a["L0_xattn_Wv"], a["L0_xattn_bv"], v_sb))
            attention_stage(nc, "x0a", q_parts, k_parts, v_sb, attended, 1, ident)
            after_stage(nc, "x0n", x, x_t[1], ident, attended, wo=a["L0_xattn_Wo"], bo=a["L0_xattn_bo"])
            if upto <= 2: return
        clear_stage(nc)
        with ExitStack() as moe:
            tile = lambda n, shape: moe.enter_context(nc.sbuf_tensor(n, shape, FP32))
            slots, weights = tile("slots", [P, SC, BE]), tile("weights", [P, SC, BE])
            numbers = tile("numbers", [P, CAP])
            chosen_t, made = tile("chosen_t", [P, KC, E0, B * CAP]), tile("made", [P, E0 // 2, B, D])
            logits = scratch("logits", [BE, S])
            router_stage(nc, "er", x_t[1], a["L0_ffn_router_w1"], a["L0_ffn_router_w2"], logits)
            load_stage(nc, "en", numbers, a["numbers"])
            choice_stage(nc, "ec", logits, slots, weights, ident)
            gather_stage(nc, "eg", x, slots, numbers, chosen_t)
            expert_stage(nc, "ee", chosen_t, a["L0_ffn_w1"], a["L0_ffn_w2"], a["L0_ffn_w3"], made)
            combine_stage(nc, "es", x, x_t[2], ident, slots, weights, numbers, made)
        if upto <= 3: return
        y_t = scratch("y_t", [D, T])
        time_mix_stage(nc, "tm", x_t[2], y_t, [a[f"L1_attn_W{n}"] for n in "kvr"],
                       a["L1_attn_time_mix"], a["L1_attn_time_decay"], a["L1_attn_time_first"])
        after_stage(nc, "tn", x, x_t[3], ident, wo=a["L1_attn_Wo"], block_t=y_t)
        if upto <= 4: return
        clear_stage(nc)
        with ExitStack() as att_ctx:
            attended = att_ctx.enter_context(nc.sbuf_tensor("attended1", [P, TT, D], FP32))
            v_sb = att_ctx.enter_context(nc.sbuf_tensor("v_sb1", [P, TT, D], FP32))
            mask_q = att_ctx.enter_context(nc.sbuf_tensor("mask_q", [P, SC, S], BF16))
            mask_k = att_ctx.enter_context(nc.sbuf_tensor("mask_k", [P, SC, S], BF16))
            ident_bf = att_ctx.enter_context(nc.sbuf_tensor("ident_bf", [P, P], BF16))
            mask_stage(nc, "ms", a["mask"], a["mask_t"], mask_q, mask_k, ident, ident_bf)
            heads_stage(nc, "x1q", x_t[3], q_parts, a["L1_xattn_Wq"], D, bias=a["L1_xattn_bq"])
            heads_stage(nc, "x1k", a["ctx_t"], k_parts, a["L1_xattn_Wk"], D, bias=a["L1_xattn_bk"],
                        v=(a["L1_xattn_Wv"], a["L1_xattn_bv"], v_sb))
            attention_stage(nc, "x1a", q_parts, k_parts, v_sb, attended, 1, ident, (mask_q, mask_k, ident_bf))
            after_stage(nc, "x1n", x, x_t[4], ident, attended, wo=a["L1_xattn_Wo"], bo=a["L1_xattn_bo"])
        if upto <= 5: return
        total = sb("total", [P, TT, D])
        share = sb("share", [P, TT, E1])
        one = sb("one", [P, 1])
        gate_stage(nc, "mg", x_t[4], a["L1_ffn_gate_w"], a["order"], share)
        mixture_stage(nc, "mx", x_t[4], a["L1_ffn_gate_up_w"], a["L1_ffn_down_w"], share, total)
        load_stage(nc, "mo", one, a["ones"])
        after_stage(nc, "mn", x, None, ident, total, blend=one, out=out)


def clear_stage(nc):
    numbers = sorted(int(n) for n in nc.released_uncleared_semaphores)
    runs = []
    for n in numbers:
        if runs and runs[-1][1] == n:
            runs[-1][1] = n + 1
        else:
            runs.append([n, n + 1])
    with nc.Block() as block:
        @block.gpsimd
        def _(pool):
            for first, end in runs:
                pool.sem_clear(range(first, end))


def load_stage(nc, name, tile, source):
    with nc.semaphore(f"{name}_loaded") as loaded, nc.Block() as block:
        @block.sync
        def _(sp):
            sp.dma_start(tile[:], source).then_inc(loaded, 16)
            sp.wait_ge(loaded, 16)


def mask_stage(nc, name, mask, mask_t, mask_q, mask_k, ident, ident_bf):
    with ExitStack() as ctx:
        raw = ctx.enter_context(nc.sbuf_tensor(f"{name}_raw", [P, 2, SC, S], I32))
        loaded, done = ctx.enter_context(nc.semaphore(f"{name}_loaded")), ctx.enter_context(nc.semaphore(f"{name}_done"))
        block = ctx.enter_context(nc.Block())

        @block.sync
        def _(sp):
            for i, source in enumerate((mask, mask_t)):
                sp.dma_start(raw[:, i], source.rearrange("(c p) t -> p c t", p=P)).then_inc(loaded, 16)

        @block.vector
        def _(dve):
            nc.vector.tensor_copy(ident_bf[:], ident[:]).then_inc(done, 1)
            dve.wait_ge(loaded, 32)
            for i, tile in enumerate((mask_q, mask_k)):
                nc.vector.tensor_scalar(tile[:], raw[:, i], 0.0, MASKED, op0=ALU.is_equal, op1=ALU.mult).then_inc(done, 1)
            dve.wait_ge(done, 3)


def start_stage(nc, a, x, ident, gates):
    with ExitStack() as ctx:
        sem = lambda n: ctx.enter_context(nc.semaphore(f"start_{n}"))
        x_loaded, zeroed, ident_done, gate_loaded, gate_done = (
            sem(n) for n in ("x_loaded", "zeroed", "ident_done", "gate_loaded", "gate_done"))
        block = ctx.enter_context(nc.Block())

        @block.sync
        def _(sp):
            sp.dma_start(gates[:, 0:1], a["L0_attn_memory_weight"].partition_broadcast(P)).then_inc(gate_loaded, 16)
            sp.dma_start(x[:], a["x_tok"].rearrange("(t p) d -> p t d", p=P)).then_inc(x_loaded, 16)
            sp.wait_ge(x_loaded, 16)

        @block.gpsimd
        def _(pool):
            nc.gpsimd.memset(ident[:], 0.0).then_inc(zeroed, 1)
            pool.wait_ge(zeroed, 1)
            nc.gpsimd.affine_select(out=ident[:], in_=ident[:], compare_op=ALU.not_equal, fill=1.0,
                                    base=0, pattern=[[-1, P]], channel_multiplier=1).then_inc(ident_done, 1)

        @block.scalar
        def _(act):
            act.wait_ge(gate_loaded, 16)
            nc.scalar.activation(gates[:, 0:1], gates[:, 0:1], ACT.Sigmoid).then_inc(gate_done, 1)

        @block.vector
        def _(dve):
            dve.wait_ge(gate_done, 1)
            nc.vector.tensor_scalar(gates[:, 1:2], gates[:, 0:1], -1.0, 1.0, op0=ALU.mult, op1=ALU.add)\
              .then_inc(gate_done, 1)
            dve.wait_ge(gate_done, 2)
            dve.wait_ge(ident_done, 1)


def laid_out(inputs):
    g = {k: np.asarray(v) for k, v in inputs.items()}
    own = np.ascontiguousarray
    column = lambda v: own(v.reshape(-1, P).T)
    swap = (np.arange(D) // HD) * HD + (np.arange(D) % HD + HD // 2) % HD
    a = {"x_tok": own(g["x"].reshape(T, D)), "x_t": own(g["x"].reshape(T, D).T),
         "ctx_t": own(g["ctx_1024"].reshape(T, D).T)}
    for n in ("Wq", "Wk", "Wv", "memory", "memory_norm", "memory_weight"):
        a[f"L0_attn_{n}"] = own(g[f"L0_attn_{n}"])
    for layer in ("L0", "L1"):
        for n in "qkvo":
            a[f"{layer}_xattn_W{n}"] = own(g[f"{layer}_xattn_W{n}"].T)
        for n in "qk":
            a[f"{layer}_xattn_b{n}"] = column(g[f"{layer}_xattn_b{n}"])
        for n in "vo":
            a[f"{layer}_xattn_b{n}"] = own(g[f"{layer}_xattn_b{n}"])
    for n in "qk":
        a[f"L0_xattn_W{n}_swapped"] = own(g[f"L0_xattn_W{n}"][swap].T)
        a[f"L0_xattn_b{n}_swapped"] = column(g[f"L0_xattn_b{n}"][swap])
    inv = (np.float32(1.0) / np.float32(10000.0) ** (np.arange(0, HD, 2, dtype=np.float32) / np.float32(HD))).astype(np.float32)
    angle = (np.arange(S, dtype=np.float32)[:, None] * inv[None, :]).astype(np.float32)
    angle = np.concatenate([angle, angle], 1).T
    sign = np.where(np.arange(HD) < HD // 2, -1.0, 1.0).astype(np.float32)[:, None]
    a["cos"] = own(np.tile(np.cos(angle).astype(np.float32), (P // HD, 1)))
    a["sin"] = own(np.tile(np.sin(angle).astype(np.float32) * sign, (P // HD, 1)))
    more_laid_out(a, g, own, column)
    return a


def more_laid_out(a, g, own, column):
    for n in ("router_w1", "router_w2", "w1", "w2", "w3"):
        a[f"L0_ffn_{n}"] = own(g[f"L0_ffn_{n}"])
    for n in "kvro":
        a[f"L1_attn_W{n}"] = own(g[f"L1_attn_W{n}"].T)
    for n in ("time_mix", "time_decay", "time_first"):
        a[f"L1_attn_{n}"] = column(g[f"L1_attn_{n}"].reshape(-1))
    a["mask"] = own(g["mask_SxS2_ik0"])
    a["mask_t"] = own(g["mask_SxS2_ik0"].T)
    a["L1_ffn_gate_w"] = own(g["L1_ffn_gate_w"].T)
    a["L1_ffn_gate_up_w"] = own(g["L1_ffn_gate_up_w"].transpose(0, 2, 1))
    a["L1_ffn_down_w"] = own(g["L1_ffn_down_w"].transpose(0, 2, 1))
    rows = lambda v: own(np.tile(v.astype(np.float32)[None], (P, 1)))
    a["numbers"], a["order"], a["ones"] = rows(np.arange(CAP)), rows(np.arange(E1, 0, -1)), rows(np.ones(1))


def program(nc, arrays, **options):
    a = {n: nc.dram_tensor(f"in_{n}", v.shape, mybir.dt.from_np(v.dtype), kind="ExternalInput").ap()
         for n, v in arrays.items()}
    out = nc.dram_tensor("out", [T, D], FP32, kind="ExternalOutput").ap()
    decoder(nc, a, out, **options)


def kernel(**inputs):
    import concourse.bacc as _bacc
    from concourse.bass_utils import run_bass_kernel_spmd as _run

    arrays = laid_out(inputs)
    nc = _bacc.Bacc("TRN2", target_bir_lowering=False, num_devices=1)
    program(nc, arrays)
    r = _run(nc, [{f"in_{n}": v for n, v in arrays.items()}], core_ids=[0])
    return r.results[0]["out"].reshape(B, S, D)
```
